# Optimizing a Trainium2 kernel written in Bass

```python
import numpy as np
import jax
import jax.numpy as jnp

def _softmax(x, axis=-1):
    return jax.nn.softmax(x, axis=axis)

def _gelu(x):
    return jax.nn.gelu(x, approximate=True)

def _silu(x):
    return jax.nn.silu(x)

def _sigmoid(x):
    return jax.nn.sigmoid(x)

def _layernorm(x, axis=-1, eps=1e-05):
    m = jnp.mean(x, axis=axis, keepdims=True)
    v = jnp.var(x, axis=axis, keepdims=True)
    return (x - m) / jnp.sqrt(v + eps)

def _scatter_add(tgt, idx, src, axis=0):
    return tgt.at[idx].add(src)

def _segment_sum(src, seg, n):
    return jax.ops.segment_sum(src, seg, n)
kernel_name = 'mk_hybrid_d1_jaxref_r8_0aa94e'

def setup_inputs(seed: int=0):
    np.random.seed(seed)
    _w = jnp.asarray

    def _L0_attn_a_setup():
        import jax, jax.numpy as jnp
        import numpy as np
        import math
        DIM = 256
        NH = 16
        Q_RANK = 192
        KV_RANK = 64
        D_NOPE = 128
        D_ROPE = 64
        D_V = 128
        EPS = 1e-06
        B, S = (2, 256)
        THETA = 10000.0

        def _rms_norm(x, w):
            return x * jax.lax.rsqrt(jnp.mean(x * x, axis=-1, keepdims=True) + EPS) * w

        def _rope_cos_sin(seq_len, d):
            inv_freq = 1.0 / THETA ** (jnp.arange(0, d, 2, dtype=jnp.float32) / d)
            t = jnp.arange(seq_len, dtype=jnp.float32)
            freqs = jnp.outer(t, inv_freq)
            return (jnp.cos(freqs), jnp.sin(freqs))

        def _apply_rope(x, cos, sin):
            x1 = x[..., 0::2]
            x2 = x[..., 1::2]
            c = cos[None, :, None, :]
            s = sin[None, :, None, :]
            o1 = x1 * c - x2 * s
            o2 = x1 * s + x2 * c
            return jnp.stack([o1, o2], axis=-1).reshape(x.shape)
        if __name__ == '__main__':
            inp = setup_inputs()
            y = jax.jit(reference)(**inp)
            print(y.shape, y.dtype)
        key = jax.random.key(seed)
        ks = jax.random.split(key, 10)
        sd = 0.02
        return {'x': jax.random.normal(ks[0], (B, S, DIM), dtype=jnp.float32), 'wq_down': jax.random.normal(ks[1], (Q_RANK, DIM), dtype=jnp.float32) * sd, 'wq_up': jax.random.normal(ks[2], (NH * D_NOPE, Q_RANK), dtype=jnp.float32) * sd, 'wq_rope': jax.random.normal(ks[3], (NH * D_ROPE, Q_RANK), dtype=jnp.float32) * sd, 'q_norm_w': jnp.ones((Q_RANK,), dtype=jnp.float32), 'wkv_down': jax.random.normal(ks[4], (KV_RANK, DIM), dtype=jnp.float32) * sd, 'kv_norm_w': jnp.ones((KV_RANK,), dtype=jnp.float32), 'wkv_up': jax.random.normal(ks[5], (NH * (D_NOPE + D_V), KV_RANK), dtype=jnp.float32) * sd, 'wk_rope': jax.random.normal(ks[6], (D_ROPE, DIM), dtype=jnp.float32) * sd, 'wo': jax.random.normal(ks[7], (DIM, NH * D_V), dtype=jnp.float32) * sd}
    _L0_attn_a_in = _L0_attn_a_setup()

    def _L0_attn_b_setup():
        import jax, jax.numpy as jnp
        import numpy as np
        D_MODEL = 256
        N_HEADS = 32
        HEAD_DIM = D_MODEL // N_HEADS
        B, T = (4, 512)

        def _reference_tuple_inner(x, W_in, W_out, log_A, W_dt, b_dt):
            Bsz, Tlen, D = x.shape
            H, hd = log_A.shape
            xp = jnp.einsum('btd,ed->bte', x, W_in)
            dt = jax.nn.softplus(jnp.einsum('btd,hd->bth', xp, W_dt) + b_dt)
            A_cont = -jnp.exp(log_A)
            a = jnp.exp(dt[..., None] * A_cont)
            xh = xp.reshape(Bsz, Tlen, H, hd)

            def combine(c1, c2):
                a1, u1 = c1
                a2, u2 = c2
                return (a1 * a2, a2 * u1 + u2)
            _, ys = jax.lax.associative_scan(combine, (a, xh), axis=1)
            s = ys[:, -1]
            y = jnp.einsum('btd,ed->bte', ys.reshape(Bsz, Tlen, D), W_out)
            return (y, s)
        key = jax.random.key(seed)
        ks = jax.random.split(key, 6)
        return {'x': jax.random.normal(ks[0], (B, T, D_MODEL), dtype=jnp.float32), 'W_in': jax.random.normal(ks[1], (D_MODEL, D_MODEL), dtype=jnp.float32) * (1.0 / np.sqrt(D_MODEL)), 'W_out': jax.random.normal(ks[2], (D_MODEL, D_MODEL), dtype=jnp.float32) * (1.0 / np.sqrt(D_MODEL)), 'log_A': jax.random.normal(ks[3], (N_HEADS, HEAD_DIM), dtype=jnp.float32) * 0.02, 'W_dt': jax.random.normal(ks[4], (N_HEADS, D_MODEL), dtype=jnp.float32) * (1.0 / np.sqrt(D_MODEL)), 'b_dt': jax.random.normal(ks[5], (N_HEADS,), dtype=jnp.float32) * 0.02}
    _L0_attn_b_in = _L0_attn_b_setup()

    def _L0_ffn_setup():
        import jax, jax.numpy as jnp
        import numpy as np
        HIDDEN = 256
        INTER = 688
        LUT_SIZE = 16

        def _ghost_linear(x, idx, lut):
            w = lut[idx]
            return jnp.einsum('bsh,oh->bso', x, w)
        key = jax.random.key(seed)
        k_x, k_lut, k_g, k_u, k_d = jax.random.split(key, 5)
        x = jax.random.normal(k_x, (2, 512, HIDDEN), dtype=jnp.float32)
        lut = jax.random.normal(k_lut, (LUT_SIZE,), dtype=jnp.float32) * 0.02
        gate_idx = jax.random.randint(k_g, (INTER, HIDDEN), 0, LUT_SIZE, dtype=jnp.int32)
        up_idx = jax.random.randint(k_u, (INTER, HIDDEN), 0, LUT_SIZE, dtype=jnp.int32)
        down_idx = jax.random.randint(k_d, (HIDDEN, INTER), 0, LUT_SIZE, dtype=jnp.int32)
        return {'x': x, 'lut': lut, 'gate_idx': gate_idx, 'up_idx': up_idx, 'down_idx': down_idx}
    _L0_ffn_in = _L0_ffn_setup()
    _d = {'L0_attn_a_x': _L0_attn_a_in['x'], 'L0_attn_a_wq_down': _L0_attn_a_in['wq_down'], 'L0_attn_a_wq_up': _L0_attn_a_in['wq_up'], 'L0_attn_a_wq_rope': _L0_attn_a_in['wq_rope'], 'L0_attn_a_q_norm_w': _L0_attn_a_in['q_norm_w'], 'L0_attn_a_wkv_down': _L0_attn_a_in['wkv_down'], 'L0_attn_a_kv_norm_w': _L0_attn_a_in['kv_norm_w'], 'L0_attn_a_wkv_up': _L0_attn_a_in['wkv_up'], 'L0_attn_a_wk_rope': _L0_attn_a_in['wk_rope'], 'L0_attn_a_wo': _L0_attn_a_in['wo'], 'L0_attn_b_W_in': _L0_attn_b_in['W_in'], 'L0_attn_b_W_out': _L0_attn_b_in['W_out'], 'L0_attn_b_log_A': _L0_attn_b_in['log_A'], 'L0_attn_b_W_dt': _L0_attn_b_in['W_dt'], 'L0_attn_b_b_dt': _L0_attn_b_in['b_dt'], 'L0_ffn_lut': _L0_ffn_in['lut'], 'L0_ffn_gate_idx': _L0_ffn_in['gate_idx'], 'L0_ffn_up_idx': _L0_ffn_in['up_idx'], 'L0_ffn_down_idx': _L0_ffn_in['down_idx']}
    _x0 = _d['L0_attn_a_x']
    _d['L0_attn_a_x'] = jax.random.normal(jax.random.fold_in(jax.random.key(seed), 1), (4, 512, 256), dtype=_x0.dtype)
    del _x0
    return _d

def reference(L0_attn_a_x, L0_attn_a_wq_down, L0_attn_a_wq_up, L0_attn_a_wq_rope, L0_attn_a_q_norm_w, L0_attn_a_wkv_down, L0_attn_a_kv_norm_w, L0_attn_a_wkv_up, L0_attn_a_wk_rope, L0_attn_a_wo, L0_attn_b_W_in, L0_attn_b_W_out, L0_attn_b_log_A, L0_attn_b_W_dt, L0_attn_b_b_dt, L0_ffn_lut, L0_ffn_gate_idx, L0_ffn_up_idx, L0_ffn_down_idx):

    def _L0_attn_a_ref(x, wq_down, wq_up, wq_rope, q_norm_w, wkv_down, kv_norm_w, wkv_up, wk_rope, wo):
        import jax, jax.numpy as jnp
        import numpy as np
        import math
        DIM = 256
        NH = 16
        Q_RANK = 192
        KV_RANK = 64
        D_NOPE = 128
        D_ROPE = 64
        D_V = 128
        EPS = 1e-06
        B, S = (2, 256)
        THETA = 10000.0

        def _rms_norm(x, w):
            return x * jax.lax.rsqrt(jnp.mean(x * x, axis=-1, keepdims=True) + EPS) * w

        def _rope_cos_sin(seq_len, d):
            inv_freq = 1.0 / THETA ** (jnp.arange(0, d, 2, dtype=jnp.float32) / d)
            t = jnp.arange(seq_len, dtype=jnp.float32)
            freqs = jnp.outer(t, inv_freq)
            return (jnp.cos(freqs), jnp.sin(freqs))

        def _apply_rope(x, cos, sin):
            x1 = x[..., 0::2]
            x2 = x[..., 1::2]
            c = cos[None, :, None, :]
            s = sin[None, :, None, :]
            o1 = x1 * c - x2 * s
            o2 = x1 * s + x2 * c
            return jnp.stack([o1, o2], axis=-1).reshape(x.shape)
        if __name__ == '__main__':
            inp = setup_inputs()
            y = jax.jit(reference)(**inp)
            print(y.shape, y.dtype)
        bs, seq_len, _ = x.shape
        q_c = _rms_norm(x @ wq_down.T, q_norm_w)
        q_nope = (q_c @ wq_up.T).reshape(bs, seq_len, NH, D_NOPE)
        q_pe = (q_c @ wq_rope.T).reshape(bs, seq_len, NH, D_ROPE)
        kv_c = _rms_norm(x @ wkv_down.T, kv_norm_w)
        kv_up = (kv_c @ wkv_up.T).reshape(bs, seq_len, NH, D_NOPE + D_V)
        k_nope = kv_up[..., :D_NOPE]
        v = kv_up[..., D_NOPE:]
        k_rope_shared = (x @ wk_rope.T).reshape(bs, seq_len, 1, D_ROPE)
        cos, sin = _rope_cos_sin(seq_len, D_ROPE)
        q_pe = _apply_rope(q_pe, cos, sin)
        k_rope_shared = _apply_rope(k_rope_shared, cos, sin)
        k_rope = jnp.broadcast_to(k_rope_shared, (bs, seq_len, NH, D_ROPE))
        q = jnp.concatenate([q_nope, q_pe], axis=-1)
        k = jnp.concatenate([k_nope, k_rope], axis=-1)
        scale = 1.0 / math.sqrt(D_NOPE + D_ROPE)
        scores = jnp.einsum('bqhd,bkhd->bhqk', q, k) * scale
        causal = jnp.tril(jnp.ones((seq_len, seq_len), dtype=bool))
        scores = jnp.where(causal[None, None], scores, -jnp.inf)
        probs = jax.nn.softmax(scores.astype(jnp.float32), axis=-1).astype(q.dtype)
        out = jnp.einsum('bhqk,bkhd->bqhd', probs, v)
        out = out.reshape(bs, seq_len, NH * D_V)
        return out @ wo.T

    def _L0_attn_b_ref(x, W_in, W_out, log_A, W_dt, b_dt):
        import jax, jax.numpy as jnp
        import numpy as np
        D_MODEL = 256
        N_HEADS = 32
        HEAD_DIM = D_MODEL // N_HEADS
        B, T = (4, 512)

        def _reference_tuple_inner(x, W_in, W_out, log_A, W_dt, b_dt):
            Bsz, Tlen, D = x.shape
            H, hd = log_A.shape
            xp = jnp.einsum('btd,ed->bte', x, W_in)
            dt = jax.nn.softplus(jnp.einsum('btd,hd->bth', xp, W_dt) + b_dt)
            A_cont = -jnp.exp(log_A)
            a = jnp.exp(dt[..., None] * A_cont)
            xh = xp.reshape(Bsz, Tlen, H, hd)

            def combine(c1, c2):
                a1, u1 = c1
                a2, u2 = c2
                return (a1 * a2, a2 * u1 + u2)
            _, ys = jax.lax.associative_scan(combine, (a, xh), axis=1)
            s = ys[:, -1]
            y = jnp.einsum('btd,ed->bte', ys.reshape(Bsz, Tlen, D), W_out)
            return (y, s)
        return _reference_tuple_inner(x, W_in, W_out, log_A, W_dt, b_dt)[0]

    def _L0_ffn_ref(x, lut, gate_idx, up_idx, down_idx):
        import jax, jax.numpy as jnp
        import numpy as np
        HIDDEN = 256
        INTER = 688
        LUT_SIZE = 16

        def _ghost_linear(x, idx, lut):
            w = lut[idx]
            return jnp.einsum('bsh,oh->bso', x, w)
        gate = _ghost_linear(x, gate_idx, lut)
        up = _ghost_linear(x, up_idx, lut)
        h = jax.nn.silu(gate) * up
        return _ghost_linear(h, down_idx, lut)
    x = L0_attn_a_x
    x = x + _L0_attn_a_ref(_layernorm(x, axis=-1), L0_attn_a_wq_down, L0_attn_a_wq_up, L0_attn_a_wq_rope, L0_attn_a_q_norm_w, L0_attn_a_wkv_down, L0_attn_a_kv_norm_w, L0_attn_a_wkv_up, L0_attn_a_wk_rope, L0_attn_a_wo)
    x = x + _L0_ffn_ref(_layernorm(x, axis=-1), L0_ffn_lut, L0_ffn_gate_idx, L0_ffn_up_idx, L0_ffn_down_idx)
    x = x + _L0_attn_b_ref(_layernorm(x, axis=-1), L0_attn_b_W_in, L0_attn_b_W_out, L0_attn_b_log_A, L0_attn_b_W_dt, L0_attn_b_b_dt)
    x = x + _L0_ffn_ref(_layernorm(x, axis=-1), L0_ffn_lut, L0_ffn_gate_idx, L0_ffn_up_idx, L0_ffn_down_idx)
    return x

_drawn_inputs = setup_inputs


def setup_inputs(seed=0):
    import zlib

    import numpy as np

    out = dict(_drawn_inputs(seed))
    spreads = {'L0_attn_a_q_norm_w': (1.0, 0.6), 'L0_attn_a_kv_norm_w': (1.0, 0.6)}
    factors = {'L0_attn_a_wq_down': 8.0,
     'L0_attn_a_wq_up': 8.0,
     'L0_attn_a_wq_rope': 8.0,
     'L0_attn_a_wk_rope': 8.0,
     'L0_attn_b_log_A': 8.0,
     'L0_attn_b_b_dt': 8.0}
    for name, (base, spread) in spreads.items():
        noise = np.random.default_rng([zlib.crc32(name.encode()), seed]).standard_normal(out[name].shape)
        drawn = base * np.exp(spread * noise) if base else spread * noise
        out[name] = jnp.asarray(drawn.astype(out[name].dtype))
    for name, factor in factors.items():
        out[name] = (out[name] * factor).astype(out[name].dtype)
    return out
```

```python
import concourse.bass as bass
from concourse import mybir
from contextlib import ExitStack

F32 = mybir.dt.float32
F32R = mybir.dt.float32r
BF16 = mybir.dt.bfloat16
I32 = mybir.dt.int32
ALU = mybir.AluOpType
ACT = mybir.ActivationFunctionType

P = 128
BATCH, SEQ, DIM = 4, 512, 256
TB = SEQ // P
CK = DIM // P
HEADS, NOPE, ROPE, DV = 16, 128, 64, 128
QR, KR = 192, 64
QB = QR - P
DOWN = QR + KR + ROPE
G = 4
UNITS = TB * (HEADS // G)
BLOCKS = (HEADS // G) * TB * (TB + 1) // 2
INTER = 688
FT = INTER // P
TAIL = INTER - FT * P
UP0 = 64
GT = 2 * FT + 1
GW = 2 * FT * P + UP0 + TAIL
LUT = 16
SM_SCALE = float(NOPE + ROPE) ** -0.5
LN_EPS, RMS_EPS = 1e-5, 1e-6
BIG = 1e30


def tile_of(n):
    return n // (HEADS // G)


def blocks_before(n):
    return sum(tile_of(m) + 1 for m in range(n))


class Arena:

    def __init__(self, nc, start, size):
        self.nc, self.at, self.end = nc, start, start + size

    def __call__(self, name, shape, dt):
        n = 2 if dt == BF16 else 4
        for s in shape[1:]:
            n *= s
        t = self.nc.alloc_sbuf_tensor_at(name, shape, dt, offset=self.at)
        self.at += (n + 31) // 32 * 32
        assert self.at <= self.end, (name, self.at, self.end)
        return t


def build(nc, x_in, wq_down, wq_up, wq_rope, q_norm_w, wkv_down, kv_norm_w, wkv_up, wk_rope, wo,
          w_in, w_out, log_a, w_dt, b_dt, lut_in, gate_idx, up_idx, down_idx,
          c_ident, c_mask, c_cos, c_sin, out):
    ctx = ExitStack()
    with ctx:
        start = (nc.sbuf_base + 63) // 64 * 64
        space = nc.sbuf_usable_end - start
        keep = Arena(nc, start, space)
        x = keep("x", [P, BATCH * TB, DIM], F32)
        idx_gu = keep("idx_gu", [P, GT, DIM], BF16)
        idx_dn = keep("idx_dn", [P, CK, INTER], BF16)
        w_gu = keep("w_gu", [P, GT, DIM], F32)
        w_dn = keep("w_dn", [P, CK * INTER], F32)
        raw_gu = nc.alloc_sbuf_tensor_at("raw_gu", [P, GT, DIM], I32, offset=keep.at - 4 * (GT * DIM + CK * INTER))
        raw_dn = nc.alloc_sbuf_tensor_at("raw_dn", [P, CK, INTER], I32, offset=keep.at - 4 * CK * INTER)
        down_hi = keep("down_hi", [P, CK, DOWN], F32R)
        down_lo = keep("down_lo", [P, CK, DOWN], F32R)
        ssm_hi = keep("ssm_hi", [P, 3, CK, DIM], F32R)
        ssm_lo = keep("ssm_lo", [P, 3, CK, DIM], F32R)
        cos2 = keep("cos2", [P, TB, ROPE], F32)
        sin2 = keep("sin2", [P, TB, ROPE], F32)
        mask = keep("mask", [P, TB * P], F32)
        ident = keep("ident", [P, P], F32)
        lut = keep("lut", [P, LUT], F32)
        qn_a = keep("qn_a", [P, 1], F32)
        qn_b = keep("qn_b", [P, 1], F32)
        kvn = keep("kvn", [P, KR], F32)
        dt_bias = keep("dt_bias", [P, CK], F32)
        a_neg = keep("a_neg", [P, CK], F32)
        eps_ln = keep("eps_ln", [P, 1], F32)
        eps_rms = keep("eps_rms", [P, 1], F32)
        one = keep("one", [P, 1], F32)
        scratch = keep("scratch", [P, 2 * G + 1], F32)
        stats = keep("stats", [P, TB, 6], F32)
        mv = keep("mv", [P, TB, 2], F32)
        ln_v = keep("ln_v", [P, TB], F32)
        ln_y = keep("ln_y", [P, TB], F32)
        ln_t = keep("ln_t", [P, TB], F32)
        ln_r = keep("ln_r", [P, TB], F32)
        ms = keep("ms", [P, TB, 2], F32)
        rms_v = keep("rms_v", [P, TB, 2], F32)
        rms_y = keep("rms_y", [P, TB, 2], F32)
        rms_t = keep("rms_t", [P, TB, 2], F32)
        rms_r = keep("rms_r", [P, TB, 2], F32)
        bias_m = keep("bias_m", [P, 2, G], F32)
        den = keep("den", [P, 2, G], F32)
        rden = keep("rden", [P, 2, G], F32)
        xt_hi = keep("xt_hi", [P, CK, SEQ], F32R)
        xt_lo = keep("xt_lo", [P, CK, SEQ], F32R)
        xn = keep("xn", [P, TB, DIM], F32)

        r1_at, r1_size = keep.at, 65536
        r1 = Arena(nc, r1_at, r1_size)
        wa_hi = r1("wa_hi", [P, HEADS, 2, KR], F32R)
        wa_lo = r1("wa_lo", [P, HEADS, 2, KR], F32R)
        wb_hi = r1("wb_hi", [P, HEADS, 2, KR], F32R)
        wb_lo = r1("wb_lo", [QB, HEADS, 2, KR], F32R)
        ssm_at = r1.at
        wo_a = r1("wo_a", [P, HEADS, DIM], F32R)
        wo_at = r1.at
        wo_b = r1("wo_b", [P, HEADS, DIM], F32R)
        ssm_nat = nc.alloc_sbuf_tensor_at("ssm_nat", [P, 3, CK, DIM], F32, offset=ssm_at)
        wo_nat = nc.alloc_sbuf_tensor_at("wo_nat", [P, CK, HEADS * DV], F32, offset=wo_at)
        r1f = Arena(nc, r1_at, r1_size)
        gu_hi = r1f("gu_hi", [P, CK, GW], F32R)
        gu_lo = r1f("gu_lo", [P, CK, GW], F32R)
        dn_hi = r1f("dn_hi", [P, FT + 1, DIM], F32R)
        dn_lo = r1f("dn_lo", [P, FT + 1, DIM], F32R)
        h_hi = r1f("h_hi", [P, FT + 1, SEQ], F32R)
        h_lo = r1f("h_lo", [P, FT, SEQ], F32R)

        r2_at = r1_at + r1_size
        r2_size = start + space - r2_at
        r2s = Arena(nc, r2_at, r2_size)
        wqu = r2s("wqu", [P, HEADS, QR + QB], F32)
        wkn = r2s("wkn", [P, HEADS, KR], F32)
        wv2 = r2s("wv2", [P, HEADS, 2, KR], F32)
        wo_t = r2s("wo_t", [P, HEADS, DIM], F32)
        wqr = r2s("wqr", [P, HEADS // 2, QR + QB], F32)
        dn_nat = r2s("dn_nat", [P, 3, DIM], F32)
        r2 = Arena(nc, r2_at, r2_size)
        cd = r2("cd", [P, TB, DOWN], F32)
        k_rot = r2("k_rot", [P, TB, ROPE], F32)
        qa_hi = r2("qa_hi", [P, SEQ], F32R)
        qa_lo = r2("qa_lo", [P, SEQ], F32R)
        qb_hl = r2("qb_hl", [P, SEQ], F32R)
        kt_hi = r2("kt_hi", [P, SEQ], F32R)
        kt_lo = r2("kt_lo", [P, SEQ], F32R)
        v_hl = r2("v_hl", [P, TB, 2, KR], F32R)
        q_tok = r2("q_tok", [P, 2, G, P], F32)
        q_rot = r2("q_rot", [P, G, ROPE], F32)
        qt_hi = r2("qt_hi", [P, 2, G, P], F32R)
        qt_lo = r2("qt_lo", [P, 2, G, P], F32R)
        prob = r2("prob", [P, 2, G, SEQ], F32)
        pt_hi = r2("pt_hi", [P, 2, G, P], F32R)
        pt_lo = r2("pt_lo", [P, 2, G, P], F32R)
        o_a = r2("o_a", [P, 2, G, P], F32R)
        o_b = r2("o_b", [P, 2, G, P], F32R)
        r2f = Arena(nc, r2_at, r2_size)
        silu = r2f("silu", [P, 2, SEQ], F32)
        h_f = r2f("h_f", [P, 2, SEQ], F32)
        xp_hi = r2f("xp_hi", [P, CK, SEQ], F32R)
        xp_lo = r2f("xp_lo", [P, CK, SEQ], F32R)
        sp = r2f("sp", [P, CK, SEQ], F32)
        dts = r2f("dts", [P, CK, SEQ], F32)
        decay = r2f("decay", [P, CK, SEQ], F32)
        ys = r2f("ys", [P, CK, SEQ], F32)
        y_hi = r2f("y_hi", [P, CK, SEQ], F32R)
        y_lo = r2f("y_lo", [P, CK, SEQ], F32R)
        r2.at = max(r2.at, r2s.at)
        DC = CK * INTER // BATCH
        hot_dn = r2("hot_dn", [P, DC], F32)
        GC = GT * DIM // 11
        hot_gu = r2("hot_gu", [P, GC], F32)

        bank = [nc.alloc_psum_tensor(f"bank{i}", [P, 512], F32) for i in range(8)]

        def sem(name):
            return ctx.enter_context(nc.semaphore(name))

        x_in_s = [sem(f"x_in{b}") for b in range(BATCH)]
        const_in, bias_in = sem("const_in"), sem("bias_in")
        dnat_in, ssm_in, wqu_in, wkn_in, wv_in, wqr_in, wo_in = (
            sem(n) for n in ("dnat_in", "ssm_in", "wqu_in", "wkn_in", "wv_in", "wqr_in", "wo_in"))
        gu_in, dn_in = sem("gu_in"), sem("dn_in")
        consts = sem("consts")
        pads = sem("pads")
        a_exp, a_ready = sem("a_exp"), sem("a_ready")
        idx_ready = sem("idx_ready")
        lut_hot, lut_sum = sem("lut_hot"), sem("lut_sum")
        dlut_hot, dlut_sum = sem("dlut_hot"), sem("dlut_sum")
        prep_mm, prep_act, prep_dve = sem("prep_mm"), sem("prep_act"), sem("prep_dve")
        ln_stats, ln_aggr, ln_seed, ln_ref, ln_norm = (
            sem(n) for n in ("ln_stats", "ln_aggr", "ln_seed", "ln_ref", "ln_norm"))
        xt_mm, xt_hi_s, xt_lo_s = sem("xt_mm"), sem("xt_hi_s"), sem("xt_lo_s")

        dp_mm, dp_cp, sq, rms_seed, rms_ref, tok = (
            sem(n) for n in ("dp_mm", "dp_cp", "sq", "rms_seed", "rms_ref", "tok"))
        at_mm, at_hi, at_lo = sem("at_mm"), sem("at_hi"), sem("at_lo")
        qa_mm, qa_cp, q_rope = sem("qa_mm"), sem("qa_cp"), sem("q_rope")
        qt_mm, qt_hi_s, qt_lo_s = sem("qt_mm"), sem("qt_hi_s"), sem("qt_lo_s")
        s_mm, s_max, s_exp = sem("s_mm"), sem("s_max"), sem("s_exp")
        recip_s, norm_a, norm_d = sem("recip_s"), sem("norm_a"), sem("norm_d")
        pt_mm, pt_hi_s, pt_lo_s, pv_mm = sem("pt_mm"), sem("pt_hi_s"), sem("pt_lo_s"), sem("pv_mm")
        o_hi_s, o_lo_s, y_mm = sem("o_hi_s"), sem("o_lo_s"), sem("y_mm")
        x_add = [sem(f"x_add{layer}") for layer in range(4)]

        class Ffn:
            def __init__(self, name):
                self.gu_mm, self.silu, self.hf, self.hhi, self.hlo, self.dn_mm = (
                    sem(name + n) for n in ("gu_mm", "silu", "hf", "hhi", "hlo", "dn_mm"))

        ffn = {1: Ffn("f1_"), 3: Ffn("f3_")}
        xp_mm, xp_hi_s, xp_lo_s, dt_mm = sem("xp_mm"), sem("xp_hi_s"), sem("xp_lo_s"), sem("dt_mm")
        sp_act, sp_relu, dt_sum, dec_s, scan_s = (
            sem(n) for n in ("sp_act", "sp_relu", "dt_sum", "dec_s", "scan_s"))
        y_hi_s, y_lo_s, so_mm = sem("y_hi_s"), sem("y_lo_s"), sem("so_mm")
        stored = sem("stored")

        block = ctx.enter_context(nc.Block())

        def t_down(c):
            def pe(e, o):
                for r, rows in ((0, P), (1, P), (2, ROPE)):
                    last = nc.tensor.transpose(o[:, r * P:r * P + rows], dn_nat[0:rows, r, c * P:(c + 1) * P],
                                               ident[0:rows, 0:rows])
                return last

            def act(e, o):
                return nc.scalar.copy(down_hi[:, c, :], o[:, 0:DOWN])

            def dve(e, o):
                return nc.vector.tensor_tensor(down_lo[:, c, :], o[:, 0:DOWN], down_hi[:, c, :], ALU.subtract)
            return pe, act, dve

        def split_scaled(o, hi, lo, s, rows):
            def act(e, b):
                return nc.scalar.activation(hi, o(b), ACT.Copy, scale=s[:, 0:1])

            def dve(e, b):
                return nc.vector.scalar_tensor_tensor(out=lo, in0=o(b)[0:rows], scalar=s[0:rows, 0:1],
                                                      in1=hi[0:rows], op0=ALU.mult, op1=ALU.subtract)
            return act, dve

        def t_nope(part, k):
            hs = slice(8 * k, 8 * k + 8)
            hi, lo, s, rows = ((wa_hi, wa_lo, qn_a, P), (wb_hi, wb_lo, qn_b, QB))[part]

            def pe(e, o):
                for j in range(8):
                    last = nc.tensor.matmul(o[:, j * KR:(j + 1) * KR], wqu[:, 8 * k + j, part * P:(part + 1) * P],
                                            wkn[:, 8 * k + j, :], start=True, stop=True)
                return last
            return (pe, *split_scaled(lambda b: b[:, :].rearrange("p (h r) -> p h r", h=8),
                                      hi[:, hs, 0, :], lo[:, hs, 0, :], s, rows))

        def t_rope(part, k):
            hs = slice(8 * k, 8 * k + 8)
            hi, lo, s, rows = ((wa_hi, wa_lo, qn_a, P), (wb_hi, wb_lo, qn_b, QB))[part]

            def pe(e, o):
                for j in range(4):
                    last = nc.tensor.transpose(o[:, j * P:(j + 1) * P], wqr[:, 4 * k + j, part * P:(part + 1) * P],
                                               ident[:, :])
                return last
            return (pe, *split_scaled(lambda b: b[:, :].rearrange("p (h r) -> p h r", h=8),
                                      hi[:, hs, 1, :], lo[:, hs, 1, :], s, rows))

        def t_wo_t(k):
            def pe(e, o):
                for j in range(2):
                    for r in range(CK):
                        last = nc.tensor.transpose(o[:, j * DIM + r * P:j * DIM + (r + 1) * P],
                                                   wo_nat[:, r, (2 * k + j) * DV:(2 * k + j + 1) * DV], ident[:, :])
                return last

            def act(e, o):
                return nc.scalar.copy(wo_t[:, 2 * k, :], o[:, 0:DIM])

            def dve(e, o):
                return nc.vector.tensor_copy(wo_t[:, 2 * k + 1, :], o[:, DIM:2 * DIM])
            return pe, act, dve

        def t_ssm(j):
            def pe(e, o):
                for c in range(CK):
                    for r in range(CK):
                        last = nc.tensor.transpose(o[:, c * DIM + r * P:c * DIM + (r + 1) * P],
                                                   ssm_nat[:, j, r, c * P:(c + 1) * P], ident[:, :])
                return last

            def act(e, o):
                return nc.scalar.copy(ssm_hi[:, j, :, :], o[:, :].rearrange("p (c n) -> p c n", c=CK))

            def dve(e, o):
                return nc.vector.tensor_tensor(ssm_lo[:, j, :, :], o[:, :].rearrange("p (c n) -> p c n", c=CK),
                                               ssm_hi[:, j, :, :], ALU.subtract)
            return pe, act, dve

        def t_vo(k):
            def pe(e, o):
                for j in range(2):
                    last = nc.tensor.matmul(o[:, j * DIM:(j + 1) * DIM],
                                            wv2[:, 2 * k + j, :, :].rearrange("p a r -> p (a r)"),
                                            wo_t[:, 2 * k + j, :], start=True, stop=True)
                return last

            def act(e, o):
                nc.scalar.copy(wo_a[:, 2 * k:2 * k + 2, :], o[:, :].rearrange("p (h n) -> p h n", h=2))
                return nc.scalar.copy(wo_b[KR:P, 2 * k:2 * k + 2, :], o[KR:P, :].rearrange("p (h n) -> p h n", h=2))

            def dve(e, o):
                return nc.vector.tensor_tensor(wo_b[0:KR, 2 * k:2 * k + 2, :],
                                               o[0:KR, :].rearrange("p (h n) -> p h n", h=2),
                                               wo_a[0:KR, 2 * k:2 * k + 2, :], ALU.subtract)
            return pe, act, dve

        def t_gu(c, k):
            lo_t, hi_t = 4 * k, min(4 * k + 4, GT)
            c0, c1 = lo_t * P, min(hi_t * P, GW)

            def pe(e, o):
                for t in range(lo_t, hi_t):
                    n = min(P, GW - t * P)
                    last = nc.tensor.transpose(o[:, (t - lo_t) * P:(t - lo_t) * P + n], w_gu[0:n, t, c * P:(c + 1) * P],
                                               ident[0:n, 0:n])
                return last

            def act(e, o):
                return nc.scalar.copy(gu_hi[:, c, c0:c1], o[:, 0:c1 - c0])

            def dve(e, o):
                return nc.vector.tensor_tensor(gu_lo[:, c, c0:c1], o[:, 0:c1 - c0], gu_hi[:, c, c0:c1], ALU.subtract)
            return pe, act, dve

        def t_dn(k):
            tail = k == FT // 2

            def pe(e, o):
                for j in range(2):
                    f = 2 * k + j
                    n = min(P, INTER - f * P)
                    for r in range(CK):
                        last = nc.tensor.transpose(o[0:n, j * DIM + r * P:j * DIM + (r + 1) * P],
                                                   w_dn[:, r * INTER + f * P:r * INTER + f * P + n], ident[:, :])
                return last

            def act(e, o):
                if not tail:
                    return nc.scalar.copy(dn_hi[:, 2 * k:2 * k + 2, :], o[:, :].rearrange("p (f n) -> p f n", f=2))
                nc.scalar.copy(dn_hi[:, 2 * k, :], o[:, 0:DIM])
                nc.scalar.copy(dn_hi[0:TAIL, FT, :], o[0:TAIL, DIM:2 * DIM])
                return nc.scalar.copy(dn_hi[UP0:UP0 + TAIL, FT, :], o[0:TAIL, DIM:2 * DIM])

            def dve(e, o):
                if not tail:
                    return nc.vector.tensor_tensor(dn_lo[:, 2 * k:2 * k + 2, :],
                                                   o[:, :].rearrange("p (f n) -> p f n", f=2),
                                                   dn_hi[:, 2 * k:2 * k + 2, :], ALU.subtract)
                nc.vector.tensor_tensor(dn_lo[:, 2 * k, :], o[:, 0:DIM], dn_hi[:, 2 * k, :], ALU.subtract)
                return nc.vector.tensor_tensor(dn_lo[0:TAIL, FT, :], o[0:TAIL, DIM:2 * DIM],
                                               dn_hi[0:TAIL, FT, :], ALU.subtract)
            return pe, act, dve

        A_TASKS = [((dnat_in, 80), t_down(c)) for c in range(CK)]
        A_TASKS += [((wqu_in, 32), t_nope(p, k)) for p in range(2) for k in range(2)]
        A_TASKS += [((wqr_in, 128), t_rope(p, k)) for p in range(2) for k in range(2)]
        WO_T0 = len(A_TASKS)
        A_TASKS += [((wo_in, 16), t_wo_t(k)) for k in range(HEADS // 2)]
        A_TASKS += [((ssm_in, 64), t_ssm(j)) for j in range(3)]
        VO0 = len(A_TASKS)
        A_TASKS += [((wv_in, 32), t_vo(k)) for k in range(HEADS // 2)]
        F_TASKS = [(None, t_gu(c, k)) for c in range(CK) for k in range(3)] + [(None, t_dn(k)) for k in range(3)]
        NA, NF = len(A_TASKS), len(F_TASKS)

        def pe_tasks(e, tasks, k0):
            for k, (load, (pe, _, _)) in enumerate(tasks, k0):
                if load:
                    e.wait_ge(*load)
                if load and load[0] is wqu_in:
                    e.wait_ge(wkn_in, 16)
                if k == VO0:
                    e.wait_ge(prep_act, VO0)
                    e.wait_ge(prep_dve, VO0)
                if k - 8 >= 0:
                    e.wait_ge(prep_dve, k - 7)
                pe(e, bank[k % 8]).then_inc(prep_mm, 1)

        def act_tasks(e, tasks, k0):
            for k, (_, (_, act, _)) in enumerate(tasks, k0):
                e.wait_ge(prep_mm, k + 1)
                act(e, bank[k % 8]).then_inc(prep_act, 1)

        def dve_tasks(e, tasks, k0):
            for k, (_, (_, _, dve)) in enumerate(tasks, k0):
                e.wait_ge(prep_act, k + 1)
                dve(e, bank[k % 8]).then_inc(prep_dve, 1)

        def settle(k):
            nc.vector.memset(scratch[:, k:k + 1], 0.0)

        def dve_ln(p, xb):
            e = nc.vector
            for t in range(TB):
                e.bn_stats(stats[:, t, :], x[:, bass.ds(xb * TB + t, 1), :].rearrange("p a d -> p (a d)"))\
                    .then_inc(ln_stats, 1)
            e.wait_ge(ln_stats, p * TB + TB)
            e.wait_ge(ln_norm, p * TB)
            settle(2 * G)
            for t in range(TB):
                e.bn_aggr(mv[:, t, :], stats[:, t, :]).then_inc(ln_aggr, 1)
            e.wait_ge(ln_aggr, p * TB + TB)
            e.tensor_scalar(ln_v[:, :], mv[:, :, 1], LN_EPS, None, ALU.add).then_inc(ln_ref, 1)
            e.wait_ge(ln_seed, 2 * p + 2)
            e.tensor_tensor(ln_t[:, :], ln_y[:, :], ln_y[:, :], ALU.mult).then_inc(ln_ref, 1)
            e.wait_ge(ln_ref, 5 * p + 2)
            e.tensor_tensor(ln_t[:, :], ln_t[:, :], ln_v[:, :], ALU.mult).then_inc(ln_ref, 1)
            e.wait_ge(ln_ref, 5 * p + 3)
            e.tensor_scalar(ln_t[:, :], ln_t[:, :], -0.5, 1.5, ALU.mult, ALU.add).then_inc(ln_ref, 1)
            e.wait_ge(ln_ref, 5 * p + 4)
            e.tensor_tensor(ln_r[:, :], ln_t[:, :], ln_y[:, :], ALU.mult).then_inc(ln_ref, 1)
            e.wait_ge(ln_ref, 5 * p + 5)
            e.wait_ge(xt_mm, 2 * p)
            for t in range(TB):
                e.tensor_scalar(xn[:, t, :], x[:, bass.ds(xb * TB + t, 1), :].rearrange("p a d -> p (a d)"),
                                mv[:, t, 0:1], ln_r[:, t:t + 1],
                                ALU.subtract, ALU.mult).then_inc(ln_norm, 1)

        def act_ln(p):
            e = nc.scalar
            e.wait_ge(ln_aggr, p * TB + TB)
            e.activation(ln_y[:, :], mv[:, :, 1], ACT.Ln, bias=eps_ln[:, 0:1]).then_inc(ln_seed, 1)
            e.wait_ge(ln_seed, 2 * p + 1)
            e.activation(ln_y[:, :], ln_y[:, :], ACT.Exp, scale=-0.5).then_inc(ln_seed, 1)

        def pe_xt(p):
            e = nc.tensor
            e.wait_ge(ln_norm, p * TB + TB)
            e.wait_ge(xt_lo_s, 2 * p)
            for c in range(CK):
                for t in range(TB):
                    last = nc.tensor.transpose(bank[4 + c][:, t * P:(t + 1) * P], xn[:, t, c * P:(c + 1) * P],
                                               ident[:, :])
                last.then_inc(xt_mm, 1)

        def act_xt(p):
            for c in range(CK):
                nc.scalar.wait_ge(xt_mm, 2 * p + c + 1)
                nc.scalar.copy(xt_hi[:, c, :], bank[4 + c][:, :]).then_inc(xt_hi_s, 1)

        def dve_xt(p):
            for c in range(CK):
                nc.vector.wait_ge(xt_hi_s, 2 * p + c + 1)
                nc.vector.tensor_tensor(xt_lo[:, c, :], bank[4 + c][:, :], xt_hi[:, c, :], ALU.subtract)\
                    .then_inc(xt_lo_s, 1)

        def wait_xt(e, p):
            e.wait_ge(xt_hi_s, 2 * p + 2)
            e.wait_ge(xt_lo_s, 2 * p + 2)

        def split_mm(o, pairs, start, stop):
            n = len(pairs)
            for k, (l_hi, l_lo, r_hi, r_lo) in enumerate(pairs):
                nc.tensor.matmul(o, l_hi, r_hi, start=start and k == 0, stop=False)
                nc.tensor.matmul(o, l_hi, r_lo, start=False, stop=False)
                last = nc.tensor.matmul(o, l_lo, r_hi, start=False, stop=stop and k == n - 1)
            return last

        def dve_x_add(layer, b, t, o):
            xr = x[:, bass.ds(b * TB + t, 1), :].rearrange("p a d -> p (a d)")
            nc.vector.tensor_tensor(xr, o[:, 0:DIM], xr, ALU.add).then_inc(x_add[layer], 1)

        primed = {
            "act": [qa_cp, s_exp, dec_s, y_hi_s, ffn[1].silu, ffn[3].silu],
            "dve": [tok, qt_lo_s, o_lo_s, dt_sum, scan_s, y_lo_s, sp_relu, ffn[1].hf, ffn[3].hf, *x_add],
            "pe": [at_mm, so_mm],
        }

        def prime(e, name):
            for s in primed[name]:
                e.sem_inc(s, 1)

        @block.sync
        def _(sp_):
            xr = x_in.rearrange("b (t p) d -> b p t d", p=P)
            outr = out.rearrange("b (t p) d -> b p t d", p=P)
            sp_.dma_start(x[:, 0:TB, :], xr[0]).then_inc(x_in_s[0], 16)
            sp_.dma_start(ident[:, :], c_ident).then_inc(const_in, 16)
            sp_.dma_start(dn_nat[:, 0, :], wq_down[0:P, :]).then_inc(dnat_in, 16)
            sp_.dma_start(dn_nat[0:QB, 1, :], wq_down[P:QR, :]).then_inc(dnat_in, 16)
            sp_.dma_start(dn_nat[QB:QB + KR, 1, :], wkv_down[:, :]).then_inc(dnat_in, 16)
            wkr = wk_rope.rearrange("(r two) d -> two r d", two=2)
            for two in range(2):
                sp_.dma_start(dn_nat[32 * two:32 * two + 32, 2, :], wkr[two]).then_inc(dnat_in, 16)
            qu = wq_up.rearrange("(h d) q -> d h q", h=HEADS)
            sp_.dma_start(wqu[:, :, 0:QR], qu).then_inc(wqu_in, 16)
            sp_.dma_start(wqu[:, :, QR:QR + QB], qu[:, :, P:QR]).then_inc(wqu_in, 16)
            sp_.dma_start(wo_nat[:, :, :], wo.rearrange("(c p) d -> p c d", p=P)).then_inc(wo_in, 16)
            for b in range(1, BATCH):
                sp_.dma_start(x[:, b * TB:(b + 1) * TB, :], xr[b]).then_inc(x_in_s[b], 16)
            with sp_.Fori(0, BATCH) as b:
                for t in range(TB):
                    sp_.wait_ge(x_add[3], 1 + b * TB + t + 1)
                    sp_.dma_start(outr[bass.ds(b, 1), :, t, :].rearrange("a p d -> (a p) d"),
                                  x[:, bass.ds(b * TB + t, 1), :].rearrange("p a d -> p (a d)")).then_inc(stored, 16)
            sp_.wait_ge(stored, 16 * BATCH * TB)

        @block.gpsimd
        def _(pool):
            nc.gpsimd.memset(raw_gu[:, GT - 1, :].bitcast(F32), 0.0).then_inc(pads, 1)
            pool.wait_ge(pads, 1)
            for k, src in enumerate((gate_idx, up_idx)):
                pool.dma_start(raw_gu[:, k:2 * FT:2, :],
                               src[0:FT * P, :].rearrange("(t p) d -> p t d", p=P)).then_inc(gu_in, 16)
                pool.dma_start(raw_gu[k * UP0:k * UP0 + TAIL, GT - 1, :], src[FT * P:INTER, :]).then_inc(gu_in, 16)
            pool.dma_start(raw_dn[:, :, :], down_idx.rearrange("(c p) f -> p c f", p=P)).then_inc(dn_in, 16)
            pool.dma_start(ssm_nat[:, 0, :, :], w_in.rearrange("(c p) d -> p c d", p=P)).then_inc(ssm_in, 16)
            pool.dma_start(ssm_nat[:, 2, :, :], w_out.rearrange("(c p) d -> p c d", p=P)).then_inc(ssm_in, 16)
            hpc = P // (DIM // 32)
            for c in range(CK):
                pool.dma_start(ssm_nat[:, 1, c, :],
                               w_dt[c * hpc:(c + 1) * hpc, :].unsqueeze(1).to_broadcast([hpc, DIM // 32, DIM]))\
                    .then_inc(ssm_in, 16)
                pool.dma_start(dt_bias[:, c:c + 1],
                               b_dt[c * hpc:(c + 1) * hpc].unsqueeze(1).unsqueeze(2).to_broadcast([hpc, DIM // 32, 1]))\
                    .then_inc(bias_in, 16)
            flat_i = idx_gu[:, :, :].rearrange("p t d -> p (t d)")
            flat_w = w_gu[:, :, :].rearrange("p t d -> p (t d)")
            pool.wait_ge(const_in, 16 * 11)
            pool.wait_ge(idx_ready, 2)
            n_hot = 0
            for c in range(GT * DIM // GC):
                w = flat_w[:, c * GC:(c + 1) * GC]
                for v in range(LUT):
                    dst = w if v == 0 else hot_gu[:, :]
                    nc.gpsimd.tensor_scalar(dst, flat_i[:, c * GC:(c + 1) * GC], float(v), lut[:, v:v + 1],
                                            ALU.is_equal, ALU.mult).then_inc(lut_hot, 1)
                    n_hot += 1
                    pool.wait_ge(lut_hot, n_hot)
                    if v:
                        nc.gpsimd.tensor_tensor(w, w, hot_gu[:, :], ALU.add).then_inc(lut_sum, 1)
                        pool.wait_ge(lut_sum, c * (LUT - 1) + v)

        @block.scalar
        def _(act):
            prime(act, "act")
            kvu = wkv_up.rearrange("(h two d) r -> two d h r", h=HEADS, two=2)
            act.dma_start(wkn[:, :, :], kvu[0]).then_inc(wkn_in, 16)
            act.dma_start(cos2[:, :, :], c_cos).then_inc(const_in, 16)
            act.dma_start(sin2[:, :, :], c_sin).then_inc(const_in, 16)
            act.dma_start(mask[:, :], c_mask).then_inc(const_in, 16)
            act.dma_start(lut[:, :], lut_in.unsqueeze(0).to_broadcast([P, LUT])).then_inc(const_in, 16)
            act.dma_start(qn_a[:, :], q_norm_w[0:P].unsqueeze(1)).then_inc(const_in, 16)
            for k in range(2):
                act.dma_start(qn_b[k * QB:(k + 1) * QB, :], q_norm_w[P:QR].unsqueeze(1)).then_inc(const_in, 16)
            act.dma_start(kvn[:, :], kv_norm_w.unsqueeze(0).to_broadcast([P, KR])).then_inc(const_in, 16)
            for c in range(CK):
                act.dma_start(a_neg[:, c:c + 1], log_a.rearrange("h (e a) -> (h e) a", a=1)[c * P:(c + 1) * P, :])\
                    .then_inc(const_in, 16)
            qrr = wq_rope.rearrange("(g hh r two) q -> hh two r g q", hh=2, two=2, r=ROPE // 2)
            for hh in range(2):
                for two in range(2):
                    rows = slice(64 * hh + 32 * two, 64 * hh + 32 * two + 32)
                    act.dma_start(wqr[rows, :, 0:QR], qrr[hh, two]).then_inc(wqr_in, 16)
                    act.dma_start(wqr[rows, :, QR:QR + QB], qrr[hh, two][:, :, P:QR]).then_inc(wqr_in, 16)
            for k in range(2):
                act.dma_start(wv2[:, :, k, :], kvu[1]).then_inc(wv_in, 16)

            act.wait_ge(consts, 3)
            act_ln(0)
            act_xt(0)
            act.wait_ge(const_in, 16 * 11)
            nc.scalar.activation(a_neg[:, :], a_neg[:, :], ACT.Exp).then_inc(a_exp, 1)
            act_tasks(act, A_TASKS, 0)

            with act.Fori(0, BATCH) as b:
                act_ln(b + 1)
                for t in range(TB):
                    act.wait_ge(dp_mm, b * TB + t + 1)
                    if t == 0:
                        act.wait_ge(at_mm, 1 + 3 * b)
                        act.wait_ge(tok, 1 + 14 * b)
                    nc.scalar.copy(cd[:, t, :], bank[2 + t % 2][:, 0:DOWN]).then_inc(dp_cp, 1)
                for t in range(TB):
                    act.wait_ge(dp_cp, b * TB + t + 1)
                    for k, (c0, c1) in enumerate(((0, QR), (QR, QR + KR))):
                        nc.scalar.activation(q_tok[:, 0, :, :].rearrange("p h d -> p (h d)")[:, c0:c1], cd[:, t, c0:c1], ACT.Square,
                                             scale=float(c1 - c0) ** -0.5, accum_out=ms[:, t, k:k + 1]).then_inc(sq, 1)
                        act.wait_ge(sq, b * 2 * TB + 2 * t + k + 1)
                nc.scalar.activation(rms_y[:, :, :], ms[:, :, :], ACT.Ln, bias=eps_rms[:, 0:1]).then_inc(rms_seed, 1)
                act.wait_ge(rms_seed, 2 * b + 1)
                nc.scalar.activation(rms_y[:, :, :], rms_y[:, :, :], ACT.Exp, scale=-0.5).then_inc(rms_seed, 1)
                act_xt(b + 1)
                for k, (dst, src) in enumerate(((qa_hi[:, :], bank[0][:, :]), (qb_hl[0:QB, :], bank[1][0:QB, :]),
                                                (kt_hi[:, :], bank[6][:, :]))):
                    act.wait_ge(at_mm, 1 + 3 * b + k + 1)
                    nc.scalar.copy(dst, src).then_inc(at_hi, 1)

                def exp(n, h):
                    w = (tile_of(n) + 1) * P
                    act.wait_ge(s_max, b * HEADS * TB + G * n + h + 1)
                    if h == 0 and n >= 2:
                        act.wait_ge(pt_mm, b * BLOCKS + blocks_before(n - 1))
                    nc.scalar.activation(prob[:, n % 2, h, 0:w], bank[2 + h % 2][:, 0:w], ACT.Exp,
                                         bias=bias_m[:, n % 2, h:h + 1], scale=-1.0,
                                         accum_out=den[:, n % 2, h:h + 1]).then_inc(s_exp, 1)

                def q_copy(n):
                    act.wait_ge(qa_mm, b * UNITS + n + 1)
                    if n >= 2:
                        act.wait_ge(qt_mm, b * UNITS + n - 1)
                    nc.scalar.mul(q_tok[:, n % 2, :, :].rearrange("p h d -> p (h d)"), bank[0][:, :], -SM_SCALE)\
                        .then_inc(qa_cp, 1)

                def qt_high(n):
                    act.wait_ge(qt_mm, b * UNITS + n + 1)
                    if n >= 2:
                        act.wait_ge(s_mm, b * HEADS * TB + G * (n - 1))
                    nc.scalar.copy(qt_hi[:, n % 2, :, :].rearrange("p h d -> p (h d)"), bank[1][:, :])\
                        .then_inc(qt_hi_s, 1)

                def normalise(n):
                    w = (tile_of(n) + 1) * P
                    act.wait_ge(recip_s, b * UNITS + n + 1)
                    for h in range(2):
                        nc.scalar.activation(prob[:, n % 2, h, 0:w], prob[:, n % 2, h, 0:w], ACT.Copy,
                                             scale=rden[:, n % 2, h:h + 1]).then_inc(norm_a, 1)

                def pt_high(n, j):
                    c = blocks_before(n) + j
                    act.wait_ge(pt_mm, b * BLOCKS + c + 1)
                    if c >= 2:
                        act.wait_ge(pv_mm, b * BLOCKS + c - 1)
                    nc.scalar.copy(pt_hi[:, c % 2, :, :].rearrange("p h d -> p (h d)"), bank[4 + c % 2][:, :])\
                        .then_inc(pt_hi_s, 1)

                def out_high(n):
                    act.wait_ge(pv_mm, b * BLOCKS + blocks_before(n + 1))
                    if n >= 2:
                        act.wait_ge(y_mm, b * UNITS + n - 1)
                    nc.scalar.copy(o_a[:, n % 2, :, :].rearrange("p h d -> p (h d)"), bank[6][:, :])\
                        .then_inc(o_hi_s, 1)
                    nc.scalar.copy(o_b[0:KR, n % 2, :, :].rearrange("p h d -> p (h d)"), bank[6][0:KR, :])\
                        .then_inc(o_hi_s, 1)

                for s in range(UNITS + 4):
                    for h in range(2):
                        if 0 <= s - 2 < UNITS:
                            exp(s - 2, h)
                    if s < UNITS:
                        q_copy(s)
                    if 0 <= s - 2 < UNITS:
                        exp(s - 2, 2)
                    if 0 <= s - 1 < UNITS:
                        qt_high(s - 1)
                    if 0 <= s - 2 < UNITS:
                        exp(s - 2, 3)
                    m = s - 3
                    if 0 <= m < UNITS:
                        for j in range(min(2, tile_of(m) + 1)):
                            pt_high(m, j)
                    if 0 <= s - 2 < UNITS:
                        normalise(s - 2)
                    if 0 <= m < UNITS:
                        for j in range(2, tile_of(m) + 1):
                            pt_high(m, j)
                        out_high(m)

            act.wait_ge(pads, 3)
            act_tasks(act, F_TASKS, NA)

            def ffn_act(layer):
                f = ffn[layer]
                n_gu = 2 * FT + 1
                with act.Fori(0, BATCH) as b:
                    act_ln(BATCH * layer + b + 1)

                    def gate(m):
                        act.wait_ge(f.gu_mm, b * n_gu + 2 * m + 1)
                        if m >= 2:
                            act.wait_ge(f.hf, 1 + b * (FT + 1) + m - 1)
                        if m < FT:
                            nc.scalar.activation(silu[:, m % 2, :], bank[m % 2][:, :], ACT.Silu).then_inc(f.silu, 1)
                        else:
                            nc.scalar.activation(silu[UP0:UP0 + TAIL, m % 2, :], bank[m % 2][0:TAIL, :], ACT.Silu)\
                                .then_inc(f.silu, 1)

                    def high(m):
                        act.wait_ge(f.hf, 1 + b * (FT + 1) + m + 1)
                        rows = P if m < FT else TAIL
                        nc.scalar.copy(h_hi[0:rows, m, :], h_f[0:rows, m % 2, :]).then_inc(f.hhi, 1)

                    gate(0)
                    for m in range(FT + 1):
                        if m < FT:
                            gate(m + 1)
                        high(m)
                    act_xt(BATCH * layer + b + 1)

            ffn_act(1)

            act.wait_ge(bias_in, 16 * CK)
            with act.Fori(0, BATCH) as b:
                act_ln(BATCH * 2 + b + 1)
                for m in range(CK):
                    act.wait_ge(xp_mm, CK * b + m + 1)
                    nc.scalar.copy(xp_hi[:, m, :], bank[m][:, :]).then_inc(xp_hi_s, 1)
                for m in range(CK):
                    act.wait_ge(dt_mm, CK * b + m + 1)
                    act.wait_ge(dt_sum, 1 + CK * b)
                    nc.scalar.activation(sp[:, m, :], bank[2 + m][:, :], ACT.Abs, bias=dt_bias[:, m:m + 1])\
                        .then_inc(sp_act, 1)
                act_xt(BATCH * 2 + b + 1)
                act.wait_ge(sp_act, 4 * b + 2)
                nc.scalar.activation(sp[:, :, :], sp[:, :, :], ACT.Exp, scale=-1.0).then_inc(sp_act, 1)
                act.wait_ge(sp_act, 4 * b + 3)
                nc.scalar.activation(sp[:, :, :], sp[:, :, :], ACT.Ln, bias=one[:, 0:1]).then_inc(sp_act, 1)
                act.wait_ge(scan_s, 1 + CK * b)
                for m in range(CK):
                    act.wait_ge(dt_sum, 1 + CK * b + m + 1)
                    nc.scalar.activation(decay[:, m, :], dts[:, m, :], ACT.Exp, scale=a_neg[:, m:m + 1])\
                        .then_inc(dec_s, 1)
                for m in range(CK):
                    act.wait_ge(scan_s, 1 + CK * b + m + 1)
                    act.wait_ge(so_mm, 1 + TB * b)
                    nc.scalar.copy(y_hi[:, m, :], ys[:, m, :]).then_inc(y_hi_s, 1)

            ffn_act(3)

        @block.vector
        def _(dve):
            prime(dve, "dve")
            nc.vector.memset(eps_ln[:, :], LN_EPS).then_inc(consts, 1)
            nc.vector.memset(eps_rms[:, :], RMS_EPS).then_inc(consts, 1)
            nc.vector.memset(one[:, :], 1.0).then_inc(consts, 1)
            dve.wait_ge(x_in_s[0], 16)
            dve_ln(0, 0)
            dve_xt(0)
            dve.wait_ge(gu_in, 64)
            nc.vector.tensor_copy(idx_gu[:, :, :], raw_gu[:, :, :]).then_inc(idx_ready, 1)
            dve.wait_ge(dn_in, 16)
            nc.vector.tensor_copy(idx_dn[:, :, :], raw_dn[:, :, :]).then_inc(idx_ready, 1)
            dve.wait_ge(a_exp, 1)
            nc.vector.tensor_scalar(a_neg[:, :], a_neg[:, :], -1.0, None, ALU.mult).then_inc(a_ready, 1)
            dve_tasks(dve, A_TASKS, 0)
            for b in range(1, BATCH):
                dve.wait_ge(x_in_s[b], 16)
            dve.wait_ge(idx_ready, 2)
            idx_dn_f = idx_dn[:, :, :].rearrange("p c f -> p (c f)")

            with dve.Fori(0, BATCH) as b:
                dve.wait_ge(x_add[0], 1 + b * TB)
                dve_ln(b + 1, (b + 1) % BATCH)

                dve.wait_ge(sq, (b + 1) * 2 * TB)
                nc.vector.tensor_scalar(rms_v[:, :, :], ms[:, :, :], RMS_EPS, None, ALU.add).then_inc(rms_ref, 1)
                dve.wait_ge(rms_seed, 2 * b + 2)
                nc.vector.tensor_tensor(rms_t[:, :, :], rms_y[:, :, :], rms_y[:, :, :], ALU.mult).then_inc(rms_ref, 1)
                dve.wait_ge(rms_ref, 5 * b + 2)
                nc.vector.tensor_tensor(rms_t[:, :, :], rms_t[:, :, :], rms_v[:, :, :], ALU.mult).then_inc(rms_ref, 1)
                dve.wait_ge(rms_ref, 5 * b + 3)
                nc.vector.tensor_scalar(rms_t[:, :, :], rms_t[:, :, :], -0.5, 1.5, ALU.mult, ALU.add)\
                    .then_inc(rms_ref, 1)
                dve.wait_ge(rms_ref, 5 * b + 4)
                nc.vector.tensor_tensor(rms_r[:, :, :], rms_t[:, :, :], rms_y[:, :, :], ALU.mult).then_inc(rms_ref, 1)
                dve.wait_ge(rms_ref, 5 * b + 5)
                for t in range(TB):
                    nc.vector.tensor_scalar(cd[:, t, 0:QR], cd[:, t, 0:QR], rms_r[:, t, 0:1], None, ALU.mult)\
                        .then_inc(tok, 1)
                for t in range(TB):
                    nc.vector.scalar_tensor_tensor(out=cd[:, t, QR:QR + KR], in0=cd[:, t, QR:QR + KR],
                                                   scalar=rms_r[:, t, 1:2], in1=kvn[:, :],
                                                   op0=ALU.mult, op1=ALU.mult).then_inc(tok, 1)
                kr, half = cd[:, :, QR + KR:DOWN], ROPE // 2
                nc.vector.tensor_tensor(k_rot[:, :, 0:half], kr[:, :, half:ROPE], sin2[:, :, 0:half], ALU.mult)\
                    .then_inc(tok, 1)
                nc.vector.tensor_tensor(k_rot[:, :, half:ROPE], kr[:, :, 0:half], sin2[:, :, half:ROPE], ALU.mult)\
                    .then_inc(tok, 1)
                dve.wait_ge(tok, 1 + 14 * b + 10)
                nc.vector.tensor_tensor(kr, kr, cos2[:, :, :], ALU.mult).then_inc(tok, 1)
                dve.wait_ge(tok, 1 + 14 * b + 11)
                nc.vector.tensor_tensor(kr, kr, k_rot[:, :, :], ALU.add).then_inc(tok, 1)
                kv = cd[:, :, QR:QR + KR]
                nc.vector.tensor_copy(v_hl[:, :, 0, :], kv).then_inc(tok, 1)
                dve.wait_ge(tok, 1 + 14 * b + 13)
                nc.vector.tensor_tensor(v_hl[:, :, 1, :], kv, v_hl[:, :, 0, :], ALU.subtract).then_inc(tok, 1)
                dve_xt(b + 1)
                for k, (dst, src, hi) in enumerate(((qa_lo[:, :], bank[0][:, :], qa_hi[:, :]),
                                                    (qb_hl[QB:P, :], bank[1][0:QB, :], qb_hl[0:QB, :]),
                                                    (kt_lo[:, :], bank[6][:, :], kt_hi[:, :]))):
                    dve.wait_ge(at_hi, 3 * b + k + 1)
                    nc.vector.tensor_tensor(dst, src, hi, ALU.subtract).then_inc(at_lo, 1)

                def row_max(n, h):
                    w = (tile_of(n) + 1) * P
                    dve.wait_ge(s_mm, b * HEADS * TB + G * n + h + 1)
                    if n >= 2:
                        dve.wait_ge(s_exp, 1 + b * HEADS * TB + G * (n - 2) + h + 1)
                    settle(n % 2 * G + h)
                    nc.vector.tensor_tensor_reduce(out=bank[2 + h % 2][:, 0:w], in0=bank[2 + h % 2][:, 0:w],
                                                   in1=mask[:, TB * P - w:TB * P], scale=1.0, scalar=3e38,
                                                   op0=ALU.add, op1=ALU.min,
                                                   accum_out=bias_m[:, n % 2, h:h + 1]).then_inc(s_max, 1)

                def rope_q(n):
                    i = tile_of(n)
                    q = q_tok[:, n % 2, :, ROPE:2 * ROPE]
                    cs = cos2[:, i:i + 1, :].to_broadcast([P, G, ROPE])
                    s0 = sin2[:, i:i + 1, 0:half].to_broadcast([P, G, half])
                    s1 = sin2[:, i:i + 1, half:ROPE].to_broadcast([P, G, half])
                    k = b * 4 * UNITS + 4 * n
                    dve.wait_ge(qa_cp, 1 + b * UNITS + n + 1)
                    if n:
                        dve.wait_ge(q_rope, k)
                    nc.vector.tensor_tensor(q_rot[:, :, 0:half], q[:, :, half:ROPE], s0, ALU.mult).then_inc(q_rope, 1)
                    nc.vector.tensor_tensor(q_rot[:, :, half:ROPE], q[:, :, 0:half], s1, ALU.mult).then_inc(q_rope, 1)
                    dve.wait_ge(q_rope, k + 2)
                    nc.vector.tensor_tensor(q, q, cs, ALU.mult).then_inc(q_rope, 1)
                    dve.wait_ge(q_rope, k + 3)
                    nc.vector.tensor_tensor(q, q, q_rot[:, :, :], ALU.add).then_inc(q_rope, 1)

                def qt_low(n):
                    dve.wait_ge(qt_hi_s, b * UNITS + n + 1)
                    if n >= 2:
                        dve.wait_ge(s_mm, b * HEADS * TB + G * (n - 1))
                    nc.vector.tensor_tensor(qt_lo[:, n % 2, :, :].rearrange("p h d -> p (h d)"), bank[1][:, :],
                                            qt_hi[:, n % 2, :, :].rearrange("p h d -> p (h d)"), ALU.subtract)\
                        .then_inc(qt_lo_s, 1)

                def normalise(n):
                    w = (tile_of(n) + 1) * P
                    dve.wait_ge(s_exp, 1 + b * HEADS * TB + G * n + G)
                    if n >= 2:
                        dve.wait_ge(norm_a, b * 2 * UNITS + 2 * (n - 1))
                        dve.wait_ge(norm_d, b * 2 * UNITS + 2 * (n - 1))
                    nc.vector.reciprocal(rden[:, n % 2, :], den[:, n % 2, :]).then_inc(recip_s, 1)
                    dve.wait_ge(recip_s, b * UNITS + n + 1)
                    for h in range(2, G):
                        nc.vector.tensor_scalar(prob[:, n % 2, h, 0:w], prob[:, n % 2, h, 0:w],
                                                rden[:, n % 2, h:h + 1], None, ALU.mult).then_inc(norm_d, 1)

                def pt_low(n, j):
                    c = blocks_before(n) + j
                    dve.wait_ge(pt_hi_s, b * BLOCKS + c + 1)
                    if c >= 2:
                        dve.wait_ge(pv_mm, b * BLOCKS + c - 1)
                    nc.vector.tensor_tensor(pt_lo[:, c % 2, :, :].rearrange("p h d -> p (h d)"), bank[4 + c % 2][:, :],
                                            pt_hi[:, c % 2, :, :].rearrange("p h d -> p (h d)"), ALU.subtract)\
                        .then_inc(pt_lo_s, 1)

                def out_low(n):
                    dve.wait_ge(o_hi_s, 2 * (b * UNITS + n) + 2)
                    nc.vector.tensor_tensor(o_b[KR:P, n % 2, :, :].rearrange("p h d -> p (h d)"), bank[6][0:KR, :],
                                            o_a[0:KR, n % 2, :, :].rearrange("p h d -> p (h d)"), ALU.subtract)\
                        .then_inc(o_lo_s, 1)

                def lookup(v):
                    ix = idx_dn_f[:, bass.ds(b * DC, DC)]
                    w = w_dn[:, bass.ds(b * DC, DC)]
                    if v > 1:
                        dve.wait_ge(dlut_sum, b * (LUT - 1) + v - 1)
                    nc.vector.tensor_scalar(hot_dn[:, :] if v else w, ix, float(v), lut[:, v:v + 1],
                                            ALU.is_equal, ALU.mult).then_inc(dlut_hot, 1)
                    if v:
                        dve.wait_ge(dlut_hot, b * LUT + v + 1)
                        nc.vector.tensor_tensor(w, w, hot_dn[:, :], ALU.add).then_inc(dlut_sum, 1)

                for s in range(UNITS + 5):
                    for h in range(2):
                        if 0 <= s - 2 < UNITS:
                            row_max(s - 2, h)
                    if s < UNITS:
                        rope_q(s)
                    if 0 <= s - 2 < UNITS:
                        row_max(s - 2, 2)
                    if 0 <= s - 1 < UNITS:
                        qt_low(s - 1)
                    if 0 <= s - 2 < UNITS:
                        row_max(s - 2, 3)
                    m = s - 3
                    if 0 <= m < UNITS:
                        for j in range(min(2, tile_of(m) + 1)):
                            pt_low(m, j)
                    if 0 <= s - 2 < UNITS:
                        normalise(s - 2)
                    if 0 <= m < UNITS:
                        for j in range(2, tile_of(m) + 1):
                            pt_low(m, j)
                        out_low(m)
                    if s < LUT:
                        lookup(s)
                    y = s - 4
                    if 0 <= y < UNITS and y % G == G - 1:
                        dve.wait_ge(y_mm, b * UNITS + y + 1)
                        dve_x_add(0, b, tile_of(y), bank[7])

            dve.wait_ge(y_mm, BATCH * UNITS)
            nc.vector.memset(h_hi[32:64, FT, :].bitcast(F32), 0.0).then_inc(pads, 1)
            nc.vector.memset(dn_hi[32:64, FT, :].bitcast(F32), 0.0).then_inc(pads, 1)
            dve_tasks(dve, F_TASKS, NA)

            def ffn_dve(layer):
                f = ffn[layer]
                n_gu = 2 * FT + 1
                dve.wait_ge(x_add[layer - 1], 1 + BATCH * TB)
                with dve.Fori(0, BATCH) as b:
                    dve.wait_ge(x_add[layer], 1 + b * TB)
                    dve_ln(BATCH * layer + b + 1, (b + 1) % BATCH)
                    for m in range(FT + 1):
                        k = b * (FT + 1) + m
                        dve.wait_ge(f.silu, 1 + k + 1)
                        if m < FT:
                            dve.wait_ge(f.gu_mm, b * n_gu + 2 * m + 2)
                        if m >= 2:
                            dve.wait_ge(f.hlo, k - 1)
                        if m < FT:
                            nc.vector.tensor_tensor(h_f[:, m % 2, :], bank[2 + m % 2][:, :], silu[:, m % 2, :],
                                                    ALU.mult).then_inc(f.hf, 1)
                        else:
                            nc.vector.tensor_tensor(h_f[0:TAIL, m % 2, :], bank[m % 2][UP0:UP0 + TAIL, :],
                                                    silu[UP0:UP0 + TAIL, m % 2, :], ALU.mult).then_inc(f.hf, 1)
                        dve.wait_ge(f.hhi, k + 1)
                        if m < FT:
                            nc.vector.tensor_tensor(h_lo[:, m, :], h_f[:, m % 2, :], h_hi[:, m, :],
                                                    ALU.subtract).then_inc(f.hlo, 1)
                        else:
                            nc.vector.tensor_tensor(h_hi[UP0:UP0 + TAIL, m, :], h_f[0:TAIL, m % 2, :],
                                                    h_hi[0:TAIL, m, :], ALU.subtract).then_inc(f.hlo, 1)
                    dve_xt(BATCH * layer + b + 1)
                    for t in range(TB):
                        dve.wait_ge(f.dn_mm, b * TB + t + 1)
                        dve_x_add(layer, b, t, bank[6 + t % 2])

            ffn_dve(1)

            dve.wait_ge(x_add[1], 1 + BATCH * TB)
            dve.wait_ge(a_ready, 1)
            dve.wait_ge(bias_in, 16 * CK)
            with dve.Fori(0, BATCH) as b:
                dve.wait_ge(x_add[2], 1 + b * TB)
                dve_ln(BATCH * 2 + b + 1, (b + 1) % BATCH)
                for m in range(CK):
                    dve.wait_ge(xp_hi_s, CK * b + m + 1)
                    nc.vector.tensor_tensor(xp_lo[:, m, :], bank[m][:, :], xp_hi[:, m, :], ALU.subtract)\
                        .then_inc(xp_lo_s, 1)
                for m in range(CK):
                    dve.wait_ge(sp_act, 4 * b + m + 1)
                    if m == 0:
                        dve.wait_ge(dec_s, 1 + CK * b)
                    nc.vector.tensor_scalar(dts[:, m, :], bank[2 + m][:, :], dt_bias[:, m:m + 1], 0.0,
                                            ALU.add, ALU.max).then_inc(sp_relu, 1)
                dve_xt(BATCH * 2 + b + 1)
                dve.wait_ge(sp_act, 4 * b + 4)
                dve.wait_ge(sp_relu, 1 + CK * b + 2)
                for m in range(CK):
                    nc.vector.tensor_tensor(dts[:, m, :], dts[:, m, :], sp[:, m, :], ALU.add).then_inc(dt_sum, 1)
                dve.wait_ge(y_hi_s, 1 + CK * b)
                dve.wait_ge(y_lo_s, 1 + CK * b)
                for m in range(CK):
                    dve.wait_ge(dec_s, 1 + CK * b + m + 1)
                    nc.vector.tensor_tensor_scan(ys[:, m, :], decay[:, m, :], bank[m][:, :], 0.0,
                                                 ALU.mult, ALU.add).then_inc(scan_s, 1)
                for m in range(CK):
                    dve.wait_ge(y_hi_s, 1 + CK * b + m + 1)
                    nc.vector.tensor_tensor(y_lo[:, m, :], ys[:, m, :], y_hi[:, m, :], ALU.subtract)\
                        .then_inc(y_lo_s, 1)
                for t in range(TB):
                    dve.wait_ge(so_mm, 1 + TB * b + t + 1)
                    dve_x_add(2, b, t, bank[6 + t % 2])

            ffn_dve(3)

        @block.tensor
        def _(pe):
            prime(pe, "pe")
            pe.wait_ge(const_in, 16 * 11)
            pe_xt(0)
            wait_xt(pe, 0)
            pe_tasks(pe, A_TASKS, 0)
            pe.wait_ge(prep_act, NA)
            pe.wait_ge(prep_dve, NA)

            with pe.Fori(0, BATCH) as b:
                wait_xt(pe, b)
                for t in range(TB):
                    if t == 0:
                        pe.wait_ge(s_exp, 1 + b * HEADS * TB)
                    if t >= 2:
                        pe.wait_ge(dp_cp, b * TB + t - 1)
                    tt = slice(t * P, (t + 1) * P)
                    split_mm(bank[2 + t % 2][:, 0:DOWN],
                             [(xt_hi[:, c, tt], xt_lo[:, c, tt], down_hi[:, c, :], down_lo[:, c, :])
                              for c in range(CK)], True, True).then_inc(dp_mm, 1)
                pe_xt(b + 1)
                pe.wait_ge(tok, 1 + 14 * b + 12)
                for o, c0, c1 in ((bank[0], 0, P), (bank[1], P, QR), (bank[6], QR, DOWN)):
                    for t in range(TB):
                        last = nc.tensor.transpose(o[0:c1 - c0, t * P:(t + 1) * P], cd[:, t, c0:c1], ident[:, :])
                    last.then_inc(at_mm, 1)
                pe.wait_ge(at_hi, 3 * b + 3)
                pe.wait_ge(at_lo, 3 * b + 3)
                pe.wait_ge(tok, 1 + 14 * b + 14)
                wait_xt(pe, b + 1)

                def q_up(n):
                    tt = slice(tile_of(n) * P, (tile_of(n) + 1) * P)
                    g = n % (HEADS // G)

                    def w(m, rows=P):
                        return m[0:rows, g * G:(g + 1) * G, :, :].rearrange("p h a r -> p (h a r)")
                    pe.wait_ge(qa_cp, 1 + b * UNITS + n)
                    o = bank[0][:, :]
                    nc.tensor.matmul(o, qa_hi[:, tt], w(wa_hi), start=True, stop=False)
                    nc.tensor.matmul(o, qa_hi[:, tt], w(wa_lo), start=False, stop=False)
                    nc.tensor.matmul(o, qa_lo[:, tt], w(wa_hi), start=False, stop=False)
                    nc.tensor.matmul(o, qb_hl[:, tt], w(wb_hi), start=False, stop=False)
                    nc.tensor.matmul(o, qb_hl[0:QB, tt], w(wb_lo, QB), start=False, stop=True).then_inc(qa_mm, 1)

                def q_transpose(n):
                    pe.wait_ge(q_rope, 4 * (b * UNITS + n + 1))
                    pe.wait_ge(qt_lo_s, 1 + b * UNITS + n)
                    for h in range(G):
                        last = nc.tensor.transpose(bank[1][:, h * P:(h + 1) * P], q_tok[:, n % 2, h, :], ident[:, :])
                    last.then_inc(qt_mm, 1)

                def scores(n, h):
                    w = (tile_of(n) + 1) * P
                    if h == 0:
                        pe.wait_ge(qt_hi_s, b * UNITS + n + 1)
                        pe.wait_ge(qt_lo_s, 1 + b * UNITS + n + 1)
                    if G * n + h >= 2:
                        pe.wait_ge(s_exp, 1 + b * HEADS * TB + G * n + h - 1)
                    split_mm(bank[2 + h % 2][:, 0:w],
                             [(qt_hi[:, n % 2, h, :], qt_lo[:, n % 2, h, :], kt_hi[:, 0:w], kt_lo[:, 0:w])],
                             True, True).then_inc(s_mm, 1)

                def p_transpose(n, j):
                    c = blocks_before(n) + j
                    if j == 0:
                        pe.wait_ge(norm_a, b * 2 * UNITS + 2 * n + 2)
                        pe.wait_ge(norm_d, b * 2 * UNITS + 2 * n + 2)
                    if c >= 2:
                        pe.wait_ge(pt_lo_s, b * BLOCKS + c - 1)
                    for h in range(G):
                        last = nc.tensor.transpose(bank[4 + c % 2][:, h * P:(h + 1) * P],
                                                   prob[:, n % 2, h, j * P:(j + 1) * P], ident[:, :])
                    last.then_inc(pt_mm, 1)

                def values(n, j):
                    c = blocks_before(n) + j
                    if j == 0:
                        pe.wait_ge(o_lo_s, 1 + b * UNITS + n)
                    v = v_hl[:, j, :, :].rearrange("p a r -> p (a r)")
                    pe.wait_ge(pt_hi_s, b * BLOCKS + c + 1)
                    nc.tensor.matmul(bank[6][:, :], v, pt_hi[:, c % 2, :, :].rearrange("p h d -> p (h d)"),
                                     start=j == 0, stop=False)
                    pe.wait_ge(pt_lo_s, b * BLOCKS + c + 1)
                    nc.tensor.matmul(bank[6][:, :], v, pt_lo[:, c % 2, :, :].rearrange("p h d -> p (h d)"),
                                     start=False, stop=j == tile_of(n)).then_inc(pv_mm, 1)

                def project(n):
                    g = n % (HEADS // G)
                    pe.wait_ge(o_hi_s, 2 * (b * UNITS + n) + 2)
                    pe.wait_ge(o_lo_s, 1 + b * UNITS + n + 1)
                    if g == 0:
                        pe.wait_ge(x_add[0], 1 + b * TB + tile_of(n))
                    for h in range(G):
                        nc.tensor.matmul(bank[7][:, 0:DIM], o_a[:, n % 2, h, :], wo_a[:, g * G + h, :],
                                         start=g == 0 and h == 0, stop=False)
                        last = nc.tensor.matmul(bank[7][:, 0:DIM], o_b[:, n % 2, h, :], wo_b[:, g * G + h, :],
                                                start=False, stop=g == HEADS // G - 1 and h == G - 1)
                    last.then_inc(y_mm, 1)

                for s in range(UNITS + 4 + 1):
                    for h in range(2):
                        if 0 <= s - 2 < UNITS:
                            scores(s - 2, h)
                    if s < UNITS:
                        q_up(s)
                    if 0 <= s - 2 < UNITS:
                        scores(s - 2, 2)
                    if 0 <= s - 1 < UNITS:
                        q_transpose(s - 1)
                    if 0 <= s - 2 < UNITS:
                        scores(s - 2, 3)
                    m = s - 3
                    if 0 <= m < UNITS:
                        k = tile_of(m) + 1
                        for j in range(min(2, k)):
                            p_transpose(m, j)
                        for j in range(k):
                            values(m, j)
                            if j + 2 < k:
                                p_transpose(m, j + 2)
                    if 0 <= s - 4 < UNITS:
                        project(s - 4)

            pe.wait_ge(lut_sum, (LUT - 1) * (GT * DIM // GC))
            pe.wait_ge(dlut_sum, (LUT - 1) * BATCH)
            pe.wait_ge(x_add[0], 1 + BATCH * TB)
            pe_tasks(pe, F_TASKS, NA)
            pe.wait_ge(prep_act, NA + NF)
            pe.wait_ge(prep_dve, NA + NF)

            def ffn_pe(layer):
                f = ffn[layer]
                with pe.Fori(0, BATCH) as b:
                    wait_xt(pe, BATCH * layer + b)

                    def up(o, c0, cols):
                        pairs = [(gu_hi[:, c, c0:c0 + cols], gu_lo[:, c, c0:c0 + cols], xt_hi[:, c, :], xt_lo[:, c, :])
                                 for c in range(CK)]
                        split_mm(o[0:cols, :], pairs, True, True).then_inc(f.gu_mm, 1)

                    for m in range(FT + 1):
                        k = b * (FT + 1) + m
                        pe.wait_ge(f.silu, (k if m >= 2 else b * (FT + 1) + 1))
                        pe.wait_ge(f.hf, (k if m >= 2 else b * (FT + 1) + 1))
                        if m < FT:
                            up(bank[m % 2], 2 * m * P, P)
                            up(bank[2 + m % 2], (2 * m + 1) * P, P)
                        else:
                            up(bank[m % 2], 2 * m * P, UP0 + TAIL)
                    pe_xt(BATCH * layer + b + 1)
                    for t in range(TB):
                        pe.wait_ge(x_add[layer], 1 + b * TB + (t - 1 if t >= 2 else 0))
                        o = bank[6 + t % 2][:, 0:DIM]
                        tt = slice(t * P, (t + 1) * P)
                        for m in range(FT):
                            pe.wait_ge(f.hlo, b * (FT + 1) + m + 1)
                            split_mm(o, [(h_hi[:, m, tt], h_lo[:, m, tt], dn_hi[:, m, :], dn_lo[:, m, :])],
                                     m == 0, False)
                        pe.wait_ge(f.hlo, b * (FT + 1) + FT + 1)
                        nc.tensor.matmul(o, h_hi[0:UP0 + TAIL, FT, tt], dn_hi[0:UP0 + TAIL, FT, :],
                                         start=False, stop=False)
                        nc.tensor.matmul(o, h_hi[0:TAIL, FT, tt], dn_lo[0:TAIL, FT, :],
                                         start=False, stop=True).then_inc(f.dn_mm, 1)

            ffn_pe(1)

            pe.wait_ge(x_add[1], 1 + BATCH * TB)
            with pe.Fori(0, BATCH) as b:
                wait_xt(pe, BATCH * 2 + b)
                for m in range(CK):
                    pe.wait_ge(scan_s, 1 + CK * b)
                    mm = slice(m * P, (m + 1) * P)
                    split_mm(bank[m][:, :], [(ssm_hi[:, 0, c, mm], ssm_lo[:, 0, c, mm], xt_hi[:, c, :], xt_lo[:, c, :])
                                             for c in range(CK)], True, True).then_inc(xp_mm, 1)
                pe_xt(BATCH * 2 + b + 1)
                pe.wait_ge(xp_hi_s, CK * b + 2)
                pe.wait_ge(xp_lo_s, CK * b + 2)
                for m in range(CK):
                    pe.wait_ge(sp_relu, 1 + CK * b)
                    mm = slice(m * P, (m + 1) * P)
                    split_mm(bank[2 + m][:, :], [(ssm_hi[:, 1, c, mm], ssm_lo[:, 1, c, mm], xp_hi[:, c, :], xp_lo[:, c, :])
                                                 for c in range(CK)], True, True).then_inc(dt_mm, 1)
                pe.wait_ge(y_hi_s, 1 + CK * b + 2)
                pe.wait_ge(y_lo_s, 1 + CK * b + 2)
                for t in range(TB):
                    pe.wait_ge(x_add[2], 1 + b * TB + (t - 1 if t >= 2 else 0))
                    tt = slice(t * P, (t + 1) * P)
                    split_mm(bank[6 + t % 2][:, 0:DIM],
                             [(y_hi[:, c, tt], y_lo[:, c, tt], ssm_hi[:, 2, c, :], ssm_lo[:, 2, c, :])
                              for c in range(CK)], True, True).then_inc(so_mm, 1)
            pe.wait_ge(x_add[2], 1 + BATCH * TB)
            ffn_pe(3)


_INS = ['L0_attn_a_x', 'L0_attn_a_wq_down', 'L0_attn_a_wq_up', 'L0_attn_a_wq_rope', 'L0_attn_a_q_norm_w',
        'L0_attn_a_wkv_down', 'L0_attn_a_kv_norm_w', 'L0_attn_a_wkv_up', 'L0_attn_a_wk_rope', 'L0_attn_a_wo',
        'L0_attn_b_W_in', 'L0_attn_b_W_out', 'L0_attn_b_log_A', 'L0_attn_b_W_dt', 'L0_attn_b_b_dt',
        'L0_ffn_lut', 'L0_ffn_gate_idx', 'L0_ffn_up_idx', 'L0_ffn_down_idx']


def _constants(np):
    ident = np.eye(P, dtype=np.float32)
    mask = np.zeros((P, TB * P), np.float32)
    mask[:, -P:] = np.where(np.arange(P)[None, :] > np.arange(P)[:, None], np.float32(BIG), np.float32(0))
    inv = (1.0 / np.float32(10000.0) ** (np.arange(0, ROPE, 2, dtype=np.float32) / np.float32(ROPE))).astype(np.float32)
    ang = np.outer(np.arange(SEQ, dtype=np.float32), inv).astype(np.float32)
    c, s = np.cos(ang), np.sin(ang)
    cos2 = np.concatenate([c, c], 1).reshape(TB, P, ROPE).transpose(1, 0, 2)
    sin2 = np.concatenate([-s, s], 1).reshape(TB, P, ROPE).transpose(1, 0, 2)
    return {"ident": ident, "mask": mask, "cos2": np.ascontiguousarray(cos2), "sin2": np.ascontiguousarray(sin2)}


def kernel(**inputs):
    import numpy as _np
    import concourse.bacc as _bacc
    from concourse import mybir as _mybir
    from concourse.bass_utils import run_bass_kernel_spmd as _run

    nc = _bacc.Bacc("TRN2", target_bir_lowering=False, num_devices=1)
    arrays, args = {}, []
    named = [(n, inputs[n]) for n in _INS] + list(_constants(_np).items())
    for name, value in named:
        a = _np.ascontiguousarray(value)
        arrays[f"in_{name}_dram"] = a
        args.append(nc.dram_tensor(f"in_{name}_dram", a.shape, _mybir.dt.from_np(a.dtype), kind="ExternalInput").ap())
    out = nc.dram_tensor("out_0_dram", (BATCH, SEQ, DIM), F32, kind="ExternalOutput").ap()
    build(nc, *args, out)
    r = _run(nc, [arrays], core_ids=[0])
    return r.results[0]["out_0_dram"]
```

```python
import concourse.bass as bass
from concourse import mybir
from contextlib import ExitStack

F32 = mybir.dt.float32
F32R = mybir.dt.float32r
BF16 = mybir.dt.bfloat16
I32 = mybir.dt.int32
ALU = mybir.AluOpType
ACT = mybir.ActivationFunctionType

P = 128
BATCH, SEQ, DIM = 4, 512, 256
TB = SEQ // P
CK = DIM // P
HEADS, NOPE, ROPE, DV = 16, 128, 64, 128
QR, KR = 192, 64
QB = QR - P
DOWN = QR + KR + ROPE
G = 4
UNITS = TB * (HEADS // G)
BLOCKS = (HEADS // G) * TB * (TB + 1) // 2
INTER = 688
FT = INTER // P
TAIL = INTER - FT * P
UP0 = 64
GT = 2 * FT + 1
GW = 2 * FT * P + UP0 + TAIL
LUT = 16
SM_SCALE = float(NOPE + ROPE) ** -0.5
LN_EPS, RMS_EPS = 1e-5, 1e-6
BIG = 1e30


def tile_of(n):
    return n // (HEADS // G)


def blocks_before(n):
    return sum(tile_of(m) + 1 for m in range(n))


class Arena:

    def __init__(self, nc, start, size):
        self.nc, self.at, self.end = nc, start, start + size

    def __call__(self, name, shape, dt):
        n = 2 if dt == BF16 else 4
        for s in shape[1:]:
            n *= s
        t = self.nc.alloc_sbuf_tensor_at(name, shape, dt, offset=self.at)
        self.at += (n + 31) // 32 * 32
        assert self.at <= self.end, (name, self.at, self.end)
        return t


def build(nc, x_in, wq_down, wq_up, wq_rope, q_norm_w, wkv_down, kv_norm_w, wkv_up, wk_rope, wo,
          w_in, w_out, log_a, w_dt, b_dt, lut_in, gate_idx, up_idx, down_idx,
          c_ident, c_mask, c_cos, c_sin, out):
    ctx = ExitStack()
    with ctx:
        start = (nc.sbuf_base + 63) // 64 * 64
        space = nc.sbuf_usable_end - start
        keep = Arena(nc, start, space)
        x = keep("x", [P, BATCH * TB, DIM], F32)
        idx_gu = keep("idx_gu", [P, GT, DIM], BF16)
        idx_dn = keep("idx_dn", [P, CK, INTER], BF16)
        w_gu = keep("w_gu", [P, GT, DIM], F32)
        w_dn = keep("w_dn", [P, CK * INTER], F32)
        raw_gu = nc.alloc_sbuf_tensor_at("raw_gu", [P, GT, DIM], I32, offset=keep.at - 4 * (GT * DIM + CK * INTER))
        raw_dn = nc.alloc_sbuf_tensor_at("raw_dn", [P, CK, INTER], I32, offset=keep.at - 4 * CK * INTER)
        down_hi = keep("down_hi", [P, CK, DOWN], F32R)
        down_lo = keep("down_lo", [P, CK, DOWN], F32R)
        ssm_hi = keep("ssm_hi", [P, 3, CK, DIM], F32R)
        ssm_lo = keep("ssm_lo", [P, 3, CK, DIM], F32R)
        cos2 = keep("cos2", [P, TB, ROPE], F32)
        sin2 = keep("sin2", [P, TB, ROPE], F32)
        mask = keep("mask", [P, TB * P], F32)
        ident = keep("ident", [P, P], F32)
        lut = keep("lut", [P, LUT], F32)
        qn_a = keep("qn_a", [P, 1], F32)
        qn_b = keep("qn_b", [P, 1], F32)
        kvn = keep("kvn", [P, KR], F32)
        dt_bias = keep("dt_bias", [P, CK], F32)
        a_neg = keep("a_neg", [P, CK], F32)
        one = keep("one", [P, 1], F32)
        scratch = keep("scratch", [P, 2 * G + 1], F32)
        stats = keep("stats", [P, TB, 6], F32)
        mv = keep("mv", [P, TB, 2], F32)
        ln_v = keep("ln_v", [P, TB], F32)
        ln_t = keep("ln_t", [P, TB], F32)
        ln_r = keep("ln_r", [P, TB], F32)
        ms = keep("ms", [P, TB * 2], F32)
        rms_v = keep("rms_v", [P, TB * 2], F32)
        rms_t = keep("rms_t", [P, TB * 2], F32)
        rms_r = keep("rms_r", [P, TB * 2], F32)
        bias_m = keep("bias_m", [P, 2, G], F32)
        den = keep("den", [P, 2, G], F32)
        rden = keep("rden", [P, 2, G], F32)
        xt_hi = keep("xt_hi", [P, CK, SEQ], F32R)
        xt_lo = keep("xt_lo", [P, CK, SEQ], F32R)
        xn = keep("xn", [P, TB, DIM], F32)

        r1_at, r1_size = keep.at, 65536
        r1 = Arena(nc, r1_at, r1_size)
        wa_hi = r1("wa_hi", [P, HEADS, 2, KR], F32R)
        wa_lo = r1("wa_lo", [P, HEADS, 2, KR], F32R)
        wb_hi = r1("wb_hi", [P, HEADS, 2, KR], F32R)
        wb_lo = r1("wb_lo", [QB, HEADS, 2, KR], F32R)
        ssm_at = r1.at
        wo_a = r1("wo_a", [P, HEADS, DIM], F32R)
        wo_at = r1.at
        wo_b = r1("wo_b", [P, HEADS, DIM], F32R)
        ssm_nat = nc.alloc_sbuf_tensor_at("ssm_nat", [P, 3, CK, DIM], F32, offset=ssm_at)
        wo_nat = nc.alloc_sbuf_tensor_at("wo_nat", [P, CK, HEADS * DV], F32, offset=wo_at)
        r1f = Arena(nc, r1_at, r1_size)
        gu_hi = r1f("gu_hi", [P, CK, GW], F32R)
        gu_lo = r1f("gu_lo", [P, CK, GW], F32R)
        dn_hi = r1f("dn_hi", [P, FT + 1, DIM], F32R)
        dn_lo = r1f("dn_lo", [P, FT + 1, DIM], F32R)
        h_hi = r1f("h_hi", [P, FT + 1, SEQ], F32R)
        h_lo = r1f("h_lo", [P, FT, SEQ], F32R)

        r2_at = r1_at + r1_size
        r2_size = start + space - r2_at
        r2s = Arena(nc, r2_at, r2_size)
        wqu = r2s("wqu", [P, HEADS, QR + QB], F32)
        wkn = r2s("wkn", [P, HEADS, KR], F32)
        wv2 = r2s("wv2", [P, HEADS, 2, KR], F32)
        wo_t = r2s("wo_t", [P, HEADS, DIM], F32)
        wqr = r2s("wqr", [P, HEADS // 2, QR + QB], F32)
        dn_nat = r2s("dn_nat", [P, 3, DIM], F32)
        r2 = Arena(nc, r2_at, r2_size)
        cd = r2("cd", [P, TB, DOWN], F32)
        k_rot = r2("k_rot", [P, TB, ROPE], F32)
        qa_hi = r2("qa_hi", [P, SEQ], F32R)
        qa_lo = r2("qa_lo", [P, SEQ], F32R)
        qb_hl = r2("qb_hl", [P, SEQ], F32R)
        kt_hi = r2("kt_hi", [P, SEQ], F32R)
        kt_lo = r2("kt_lo", [P, SEQ], F32R)
        v_hl = r2("v_hl", [P, TB, 2, KR], F32R)
        q_tok = r2("q_tok", [P, 2, G, P], F32)
        q_rot = r2("q_rot", [P, G, ROPE], F32)
        qt_hi = r2("qt_hi", [P, 2, G, P], F32R)
        qt_lo = r2("qt_lo", [P, 2, G, P], F32R)
        prob = r2("prob", [P, 2, G, SEQ], F32)
        pt_hi = r2("pt_hi", [P, 2, G, P], F32R)
        pt_lo = r2("pt_lo", [P, 2, G, P], F32R)
        o_a = r2("o_a", [P, 2, G, P], F32R)
        o_b = r2("o_b", [P, 2, G, P], F32R)
        r2f = Arena(nc, r2_at, r2_size)
        silu = r2f("silu", [P, 2, SEQ], F32)
        h_f = r2f("h_f", [P, 2, SEQ], F32)
        xp_hi = r2f("xp_hi", [P, CK, SEQ], F32R)
        xp_lo = r2f("xp_lo", [P, CK, SEQ], F32R)
        sp = r2f("sp", [P, CK, SEQ], F32)
        dts = r2f("dts", [P, CK, SEQ], F32)
        decay = r2f("decay", [P, CK, SEQ], F32)
        ys = r2f("ys", [P, CK, SEQ], F32)
        y_hi = r2f("y_hi", [P, CK, SEQ], F32R)
        y_lo = r2f("y_lo", [P, CK, SEQ], F32R)
        r2.at = max(r2.at, r2s.at)
        hot_dn = nc.alloc_sbuf_tensor_at("hot_dn", [P, CK * INTER], F32, offset=r2s.at)
        GC = GT * DIM // 11
        hot_gu = r2("hot_gu", [P, GC], F32)

        bank = [nc.alloc_psum_tensor(f"bank{i}", [P, 512], F32) for i in range(8)]

        def sem(name):
            return ctx.enter_context(nc.semaphore(name))

        x_in_s = [sem(f"x_in{b}") for b in range(BATCH)]
        const_in, bias_in, ident_in = sem("const_in"), sem("bias_in"), sem("ident_in")
        dnat_in, ssm_in, wqu_in, wkn_in, wv_in, wqr_in, wo_in = (
            sem(n) for n in ("dnat_in", "ssm_in", "wqu_in", "wkn_in", "wv_in", "wqr_in", "wo_in"))
        gu_in, dn_in = sem("gu_in"), sem("dn_in")
        consts = sem("consts")
        pads = sem("pads")
        a_exp, a_ready = sem("a_exp"), sem("a_ready")
        idx_ready = sem("idx_ready")
        lut_hot, lut_sum = sem("lut_hot"), sem("lut_sum")
        dlut_hot, dlut_sum = sem("dlut_hot"), sem("dlut_sum")
        prep_mm, prep_act, prep_dve = sem("prep_mm"), sem("prep_act"), sem("prep_dve")
        ln_stats, ln_aggr, ln_ref, ln_norm = (
            sem(n) for n in ("ln_stats", "ln_aggr", "ln_ref", "ln_norm"))
        xt_mm, xt_hi_s, xt_lo_s = sem("xt_mm"), sem("xt_hi_s"), sem("xt_lo_s")

        dp_mm, dp_cp, sq, rms_ref, tok = (
            sem(n) for n in ("dp_mm", "dp_cp", "sq", "rms_ref", "tok"))
        at_mm, at_hi, at_lo = sem("at_mm"), sem("at_hi"), sem("at_lo")
        qa_mm, qa_cp, q_rope = sem("qa_mm"), sem("qa_cp"), sem("q_rope")
        qt_mm, qt_hi_s, qt_lo_s = sem("qt_mm"), sem("qt_hi_s"), sem("qt_lo_s")
        s_mm, s_max, s_exp = sem("s_mm"), sem("s_max"), sem("s_exp")
        recip_s, norm_a, norm_d = sem("recip_s"), sem("norm_a"), sem("norm_d")
        pt_mm, pt_hi_s, pt_lo_s, pv_mm = sem("pt_mm"), sem("pt_hi_s"), sem("pt_lo_s"), sem("pv_mm")
        o_hi_s, o_lo_s, y_mm = sem("o_hi_s"), sem("o_lo_s"), sem("y_mm")
        x_add = [sem(f"x_add{layer}") for layer in range(4)]

        class Ffn:
            def __init__(self, name):
                self.gu_mm, self.silu, self.hf, self.hhi, self.hlo, self.dn_mm = (
                    sem(name + n) for n in ("gu_mm", "silu", "hf", "hhi", "hlo", "dn_mm"))

        ffn = {1: Ffn("f1_"), 3: Ffn("f3_")}
        xp_mm, xp_hi_s, xp_lo_s, dt_mm = sem("xp_mm"), sem("xp_hi_s"), sem("xp_lo_s"), sem("dt_mm")
        sp_act, sp_relu, dt_sum, dec_s, scan_s = (
            sem(n) for n in ("sp_act", "sp_relu", "dt_sum", "dec_s", "scan_s"))
        y_hi_s, y_lo_s, so_mm = sem("y_hi_s"), sem("y_lo_s"), sem("so_mm")
        stored = sem("stored")

        block = ctx.enter_context(nc.Block())

        def t_down(c):
            def pe(e, o):
                for r, rows in ((0, P), (1, P), (2, ROPE)):
                    last = nc.tensor.transpose(o[:, r * P:r * P + rows], dn_nat[0:rows, r, c * P:(c + 1) * P],
                                               ident[0:rows, 0:rows])
                return last

            def act(e, o):
                return nc.scalar.copy(down_hi[:, c, :], o[:, 0:DOWN])

            def dve(e, o):
                return nc.vector.tensor_tensor(down_lo[:, c, :], o[:, 0:DOWN], down_hi[:, c, :], ALU.subtract)
            return pe, act, dve

        def split_scaled(o, hi, lo, s, rows):
            def act(e, b):
                return nc.scalar.activation(hi, o(b), ACT.Copy, scale=s[:, 0:1])

            def dve(e, b):
                return nc.vector.scalar_tensor_tensor(out=lo, in0=o(b)[0:rows], scalar=s[0:rows, 0:1],
                                                      in1=hi[0:rows], op0=ALU.mult, op1=ALU.subtract)
            return act, dve

        def t_nope(part, k):
            hs = slice(8 * k, 8 * k + 8)
            hi, lo, s, rows = ((wa_hi, wa_lo, qn_a, P), (wb_hi, wb_lo, qn_b, QB))[part]

            def pe(e, o):
                for j in range(8):
                    last = nc.tensor.matmul(o[:, j * KR:(j + 1) * KR], wqu[:, 8 * k + j, part * P:(part + 1) * P],
                                            wkn[:, 8 * k + j, :], start=True, stop=True)
                return last
            return (pe, *split_scaled(lambda b: b[:, :].rearrange("p (h r) -> p h r", h=8),
                                      hi[:, hs, 0, :], lo[:, hs, 0, :], s, rows))

        def t_rope(part, k):
            hs = slice(8 * k, 8 * k + 8)
            hi, lo, s, rows = ((wa_hi, wa_lo, qn_a, P), (wb_hi, wb_lo, qn_b, QB))[part]

            def pe(e, o):
                for j in range(4):
                    last = nc.tensor.transpose(o[:, j * P:(j + 1) * P], wqr[:, 4 * k + j, part * P:(part + 1) * P],
                                               ident[:, :])
                return last
            return (pe, *split_scaled(lambda b: b[:, :].rearrange("p (h r) -> p h r", h=8),
                                      hi[:, hs, 1, :], lo[:, hs, 1, :], s, rows))

        def t_wo_t(k):
            def pe(e, o):
                for j in range(2):
                    for r in range(CK):
                        last = nc.tensor.transpose(o[:, j * DIM + r * P:j * DIM + (r + 1) * P],
                                                   wo_nat[:, r, (2 * k + j) * DV:(2 * k + j + 1) * DV], ident[:, :])
                return last

            def act(e, o):
                return nc.scalar.copy(wo_t[:, 2 * k, :], o[:, 0:DIM])

            def dve(e, o):
                return nc.vector.tensor_copy(wo_t[:, 2 * k + 1, :], o[:, DIM:2 * DIM])
            return pe, act, dve

        def t_ssm(j):
            def pe(e, o):
                for c in range(CK):
                    for r in range(CK):
                        last = nc.tensor.transpose(o[:, c * DIM + r * P:c * DIM + (r + 1) * P],
                                                   ssm_nat[:, j, r, c * P:(c + 1) * P], ident[:, :])
                return last

            def act(e, o):
                return nc.scalar.copy(ssm_hi[:, j, :, :], o[:, :].rearrange("p (c n) -> p c n", c=CK))

            def dve(e, o):
                return nc.vector.tensor_tensor(ssm_lo[:, j, :, :], o[:, :].rearrange("p (c n) -> p c n", c=CK),
                                               ssm_hi[:, j, :, :], ALU.subtract)
            return pe, act, dve

        def t_vo(k):
            def pe(e, o):
                for j in range(2):
                    last = nc.tensor.matmul(o[:, j * DIM:(j + 1) * DIM],
                                            wv2[:, 2 * k + j, :, :].rearrange("p a r -> p (a r)"),
                                            wo_t[:, 2 * k + j, :], start=True, stop=True)
                return last

            def act(e, o):
                nc.scalar.copy(wo_a[:, 2 * k:2 * k + 2, :], o[:, :].rearrange("p (h n) -> p h n", h=2))
                return nc.scalar.copy(wo_b[KR:P, 2 * k:2 * k + 2, :], o[KR:P, :].rearrange("p (h n) -> p h n", h=2))

            def dve(e, o):
                return nc.vector.tensor_tensor(wo_b[0:KR, 2 * k:2 * k + 2, :],
                                               o[0:KR, :].rearrange("p (h n) -> p h n", h=2),
                                               wo_a[0:KR, 2 * k:2 * k + 2, :], ALU.subtract)
            return pe, act, dve

        def t_gu(c, k):
            lo_t, hi_t = 4 * k, min(4 * k + 4, GT)
            c0, c1 = lo_t * P, min(hi_t * P, GW)

            def pe(e, o):
                for t in range(lo_t, hi_t):
                    n = min(P, GW - t * P)
                    last = nc.tensor.transpose(o[:, (t - lo_t) * P:(t - lo_t) * P + n], w_gu[0:n, t, c * P:(c + 1) * P],
                                               ident[0:n, 0:n])
                return last

            def act(e, o):
                return nc.scalar.copy(gu_hi[:, c, c0:c1], o[:, 0:c1 - c0])

            def dve(e, o):
                return nc.vector.tensor_tensor(gu_lo[:, c, c0:c1], o[:, 0:c1 - c0], gu_hi[:, c, c0:c1], ALU.subtract)
            return pe, act, dve

        def t_dn(k):
            tail = k == FT // 2

            def pe(e, o):
                for j in range(2):
                    f = 2 * k + j
                    n = min(P, INTER - f * P)
                    for r in range(CK):
                        last = nc.tensor.transpose(o[0:n, j * DIM + r * P:j * DIM + (r + 1) * P],
                                                   w_dn[:, r * INTER + f * P:r * INTER + f * P + n], ident[:, :])
                return last

            def act(e, o):
                if not tail:
                    return nc.scalar.copy(dn_hi[:, 2 * k:2 * k + 2, :], o[:, :].rearrange("p (f n) -> p f n", f=2))
                nc.scalar.copy(dn_hi[:, 2 * k, :], o[:, 0:DIM])
                nc.scalar.copy(dn_hi[0:TAIL, FT, :], o[0:TAIL, DIM:2 * DIM])
                return nc.scalar.copy(dn_hi[UP0:UP0 + TAIL, FT, :], o[0:TAIL, DIM:2 * DIM])

            def dve(e, o):
                if not tail:
                    return nc.vector.tensor_tensor(dn_lo[:, 2 * k:2 * k + 2, :],
                                                   o[:, :].rearrange("p (f n) -> p f n", f=2),
                                                   dn_hi[:, 2 * k:2 * k + 2, :], ALU.subtract)
                nc.vector.tensor_tensor(dn_lo[:, 2 * k, :], o[:, 0:DIM], dn_hi[:, 2 * k, :], ALU.subtract)
                return nc.vector.tensor_tensor(dn_lo[0:TAIL, FT, :], o[0:TAIL, DIM:2 * DIM],
                                               dn_hi[0:TAIL, FT, :], ALU.subtract)
            return pe, act, dve

        A_TASKS = [((dnat_in, 80), t_down(c)) for c in range(CK)]
        A_TASKS += [((wqu_in, 32), t_nope(p, k)) for p in range(2) for k in range(2)]
        A_TASKS += [((wqr_in, 128), t_rope(p, k)) for p in range(2) for k in range(2)]
        WO_T0 = len(A_TASKS)
        A_TASKS += [((wo_in, 16), t_wo_t(k)) for k in range(HEADS // 2)]
        A_TASKS += [((ssm_in, 64), t_ssm(j)) for j in range(3)]
        VO0 = len(A_TASKS)
        A_TASKS += [((wv_in, 32), t_vo(k)) for k in range(HEADS // 2)]
        F_TASKS = [(None, t_gu(c, k)) for c in range(CK) for k in range(3)] + [(None, t_dn(k)) for k in range(3)]
        NA, NF = len(A_TASKS), len(F_TASKS)

        def pe_tasks(e, tasks, k0):
            for k, (load, (pe, _, _)) in enumerate(tasks, k0):
                if load:
                    e.wait_ge(*load)
                if load and load[0] is wqu_in:
                    e.wait_ge(wkn_in, 16)
                if k == VO0:
                    e.wait_ge(prep_act, VO0)
                    e.wait_ge(prep_dve, VO0)
                if k - 8 >= 0:
                    e.wait_ge(prep_dve, k - 7)
                pe(e, bank[k % 8]).then_inc(prep_mm, 1)

        def act_tasks(e, tasks, k0):
            for k, (_, (_, act, _)) in enumerate(tasks, k0):
                e.wait_ge(prep_mm, k + 1)
                act(e, bank[k % 8]).then_inc(prep_act, 1)

        def dve_tasks(e, tasks, k0, between=None):
            for k, (_, (_, _, dve)) in enumerate(tasks, k0):
                e.wait_ge(prep_act, k + 1)
                dve(e, bank[k % 8]).then_inc(prep_dve, 1)
                if between and k < LUT:
                    between(k)

        def settle(k):
            nc.vector.memset(scratch[:, k:k + 1], 0.0)

        RSQRT = 11

        def dve_rsqrt(sem_, c0, v, r, t):
            e = nc.vector
            e.wait_ge(sem_, c0)
            e.tensor_scalar(t.bitcast(I32), v.bitcast(I32), 1, None, ALU.logical_shift_right).then_inc(sem_, 1)
            e.wait_ge(sem_, c0 + 1)
            e.tensor_scalar(r.bitcast(I32), t.bitcast(I32), -1.0, float(0x5F3759DF), ALU.mult, ALU.add)\
                .then_inc(sem_, 1)
            for k in range(3):
                e.wait_ge(sem_, c0 + 3 * k + 2)
                e.tensor_tensor(t, r, r, ALU.mult).then_inc(sem_, 1)
                e.wait_ge(sem_, c0 + 3 * k + 3)
                e.scalar_tensor_tensor(out=t, in0=t, scalar=-0.5, in1=v, op0=ALU.mult, op1=ALU.mult).then_inc(sem_, 1)
                e.wait_ge(sem_, c0 + 3 * k + 4)
                e.scalar_tensor_tensor(out=r, in0=t, scalar=1.5, in1=r, op0=ALU.add, op1=ALU.mult).then_inc(sem_, 1)
            e.wait_ge(sem_, c0 + RSQRT)

        def dve_ln(p, xb):
            e = nc.vector
            for t in range(TB):
                e.bn_stats(stats[:, t, :], x[:, bass.ds(xb * TB + t, 1), :].rearrange("p a d -> p (a d)"))\
                    .then_inc(ln_stats, 1)
            e.wait_ge(ln_stats, p * TB + TB)
            e.wait_ge(ln_norm, p * TB)
            settle(2 * G)
            for t in range(TB):
                e.bn_aggr(mv[:, t, :], stats[:, t, :]).then_inc(ln_aggr, 1)
            e.wait_ge(ln_aggr, p * TB + TB)
            e.tensor_scalar(ln_v[:, :], mv[:, :, 1], LN_EPS, None, ALU.add).then_inc(ln_ref, 1)
            dve_rsqrt(ln_ref, (RSQRT + 1) * p + 1, ln_v[:, :], ln_r[:, :], ln_t[:, :])
            e.wait_ge(xt_mm, 2 * p)
            for t in range(TB):
                e.tensor_scalar(xn[:, t, :], x[:, bass.ds(xb * TB + t, 1), :].rearrange("p a d -> p (a d)"),
                                mv[:, t, 0:1], ln_r[:, t:t + 1],
                                ALU.subtract, ALU.mult).then_inc(ln_norm, 1)

        def pe_xt(p):
            e = nc.tensor
            e.wait_ge(ln_norm, p * TB + TB)
            e.wait_ge(xt_lo_s, 2 * p)
            for c in range(CK):
                for t in range(TB):
                    last = nc.tensor.transpose(bank[4 + c][:, t * P:(t + 1) * P], xn[:, t, c * P:(c + 1) * P],
                                               ident[:, :])
                last.then_inc(xt_mm, 1)

        def act_xt(p):
            for c in range(CK):
                nc.scalar.wait_ge(xt_mm, 2 * p + c + 1)
                nc.scalar.copy(xt_hi[:, c, :], bank[4 + c][:, :]).then_inc(xt_hi_s, 1)

        def dve_xt(p):
            for c in range(CK):
                nc.vector.wait_ge(xt_hi_s, 2 * p + c + 1)
                nc.vector.tensor_tensor(xt_lo[:, c, :], bank[4 + c][:, :], xt_hi[:, c, :], ALU.subtract)\
                    .then_inc(xt_lo_s, 1)

        def wait_xt(e, p):
            e.wait_ge(xt_hi_s, 2 * p + 2)
            e.wait_ge(xt_lo_s, 2 * p + 2)

        def split_mm(o, pairs, start, stop):
            n = len(pairs)
            for k, (l_hi, l_lo, r_hi, r_lo) in enumerate(pairs):
                nc.tensor.matmul(o, l_hi, r_hi, start=start and k == 0, stop=False)
                nc.tensor.matmul(o, l_hi, r_lo, start=False, stop=False)
                last = nc.tensor.matmul(o, l_lo, r_hi, start=False, stop=stop and k == n - 1)
            return last

        def dve_x_add(layer, b, t, o):
            xr = x[:, bass.ds(b * TB + t, 1), :].rearrange("p a d -> p (a d)")
            nc.vector.tensor_tensor(xr, o[:, 0:DIM], xr, ALU.add).then_inc(x_add[layer], 1)

        primed = {
            "act": [qa_cp, s_exp, dec_s, y_hi_s, ffn[1].silu, ffn[3].silu],
            "dve": [tok, qt_lo_s, o_lo_s, dt_sum, scan_s, y_lo_s, sp_relu, ffn[1].hf, ffn[3].hf, *x_add],
            "pe": [at_mm, so_mm],
        }

        def prime(e, name):
            for s in primed[name]:
                e.sem_inc(s, 1)

        @block.sync
        def _(sp_):
            xr = x_in.rearrange("b (t p) d -> b p t d", p=P)
            outr = out.rearrange("b (t p) d -> b p t d", p=P)
            sp_.dma_start(ident[:, :], c_ident).then_inc(ident_in, 16)
            sp_.dma_start(x[:, 0:TB, :], xr[0]).then_inc(x_in_s[0], 16)
            sp_.dma_start(dn_nat[:, 0, :], wq_down[0:P, :]).then_inc(dnat_in, 16)
            sp_.dma_start(dn_nat[0:QB, 1, :], wq_down[P:QR, :]).then_inc(dnat_in, 16)
            sp_.dma_start(dn_nat[QB:QB + KR, 1, :], wkv_down[:, :]).then_inc(dnat_in, 16)
            wkr = wk_rope.rearrange("(r two) d -> two r d", two=2)
            for two in range(2):
                sp_.dma_start(dn_nat[32 * two:32 * two + 32, 2, :], wkr[two]).then_inc(dnat_in, 16)
            qu = wq_up.rearrange("(h d) q -> d h q", h=HEADS)
            sp_.dma_start(wqu[:, :, 0:QR], qu).then_inc(wqu_in, 16)
            sp_.dma_start(wqu[:, :, QR:QR + QB], qu[:, :, P:QR]).then_inc(wqu_in, 16)
            sp_.dma_start(wo_nat[:, :, :], wo.rearrange("(c p) d -> p c d", p=P)).then_inc(wo_in, 16)
            for b in range(1, BATCH):
                sp_.dma_start(x[:, b * TB:(b + 1) * TB, :], xr[b]).then_inc(x_in_s[b], 16)
            with sp_.Fori(0, BATCH) as b:
                for t in range(TB):
                    sp_.wait_ge(x_add[3], 1 + b * TB + t + 1)
                    sp_.dma_start(outr[bass.ds(b, 1), :, t, :].rearrange("a p d -> (a p) d"),
                                  x[:, bass.ds(b * TB + t, 1), :].rearrange("p a d -> p (a d)")).then_inc(stored, 16)
            sp_.wait_ge(stored, 16 * BATCH * TB)

        @block.gpsimd
        def _(pool):
            pool.dma_start(raw_dn[:, :, :], down_idx.rearrange("(c p) f -> p c f", p=P)).then_inc(dn_in, 16)
            nc.gpsimd.memset(raw_gu[:, GT - 1, :].bitcast(F32), 0.0).then_inc(pads, 1)
            pool.wait_ge(pads, 1)
            for k, src in enumerate((gate_idx, up_idx)):
                pool.dma_start(raw_gu[:, k:2 * FT:2, :],
                               src[0:FT * P, :].rearrange("(t p) d -> p t d", p=P)).then_inc(gu_in, 16)
                pool.dma_start(raw_gu[k * UP0:k * UP0 + TAIL, GT - 1, :], src[FT * P:INTER, :]).then_inc(gu_in, 16)
            pool.dma_start(ssm_nat[:, 0, :, :], w_in.rearrange("(c p) d -> p c d", p=P)).then_inc(ssm_in, 16)
            pool.dma_start(ssm_nat[:, 2, :, :], w_out.rearrange("(c p) d -> p c d", p=P)).then_inc(ssm_in, 16)
            hpc = P // (DIM // 32)
            for c in range(CK):
                pool.dma_start(ssm_nat[:, 1, c, :],
                               w_dt[c * hpc:(c + 1) * hpc, :].unsqueeze(1).to_broadcast([hpc, DIM // 32, DIM]))\
                    .then_inc(ssm_in, 16)
                pool.dma_start(dt_bias[:, c:c + 1],
                               b_dt[c * hpc:(c + 1) * hpc].unsqueeze(1).unsqueeze(2).to_broadcast([hpc, DIM // 32, 1]))\
                    .then_inc(bias_in, 16)
            flat_i = idx_gu[:, :, :].rearrange("p t d -> p (t d)")
            flat_w = w_gu[:, :, :].rearrange("p t d -> p (t d)")
            pool.wait_ge(const_in, 16 * 10)
            pool.wait_ge(idx_ready, 2)
            n_hot = 0
            for c in range(GT * DIM // GC):
                w = flat_w[:, c * GC:(c + 1) * GC]
                for v in range(LUT):
                    dst = w if v == 0 else hot_gu[:, :]
                    nc.gpsimd.tensor_scalar(dst, flat_i[:, c * GC:(c + 1) * GC], float(v), lut[:, v:v + 1],
                                            ALU.is_equal, ALU.mult).then_inc(lut_hot, 1)
                    n_hot += 1
                    pool.wait_ge(lut_hot, n_hot)
                    if v:
                        nc.gpsimd.tensor_tensor(w, w, hot_gu[:, :], ALU.add).then_inc(lut_sum, 1)
                        pool.wait_ge(lut_sum, c * (LUT - 1) + v)

        @block.scalar
        def _(act):
            prime(act, "act")
            kvu = wkv_up.rearrange("(h two d) r -> two d h r", h=HEADS, two=2)
            act.dma_start(cos2[:, :, :], c_cos).then_inc(const_in, 16)
            act.dma_start(sin2[:, :, :], c_sin).then_inc(const_in, 16)
            act.dma_start(mask[:, :], c_mask).then_inc(const_in, 16)
            act.dma_start(lut[:, :], lut_in.unsqueeze(0).to_broadcast([P, LUT])).then_inc(const_in, 16)
            act.dma_start(qn_a[:, :], q_norm_w[0:P].unsqueeze(1)).then_inc(const_in, 16)
            for k in range(2):
                act.dma_start(qn_b[k * QB:(k + 1) * QB, :], q_norm_w[P:QR].unsqueeze(1)).then_inc(const_in, 16)
            act.dma_start(kvn[:, :], kv_norm_w.unsqueeze(0).to_broadcast([P, KR])).then_inc(const_in, 16)
            for c in range(CK):
                act.dma_start(a_neg[:, c:c + 1], log_a.rearrange("h (e a) -> (h e) a", a=1)[c * P:(c + 1) * P, :])\
                    .then_inc(const_in, 16)
            act.dma_start(wkn[:, :, :], kvu[0]).then_inc(wkn_in, 16)
            qrr = wq_rope.rearrange("(g hh r two) q -> hh two r g q", hh=2, two=2, r=ROPE // 2)
            for hh in range(2):
                for two in range(2):
                    rows = slice(64 * hh + 32 * two, 64 * hh + 32 * two + 32)
                    act.dma_start(wqr[rows, :, 0:QR], qrr[hh, two]).then_inc(wqr_in, 16)
                    act.dma_start(wqr[rows, :, QR:QR + QB], qrr[hh, two][:, :, P:QR]).then_inc(wqr_in, 16)
            for k in range(2):
                act.dma_start(wv2[:, :, k, :], kvu[1]).then_inc(wv_in, 16)

            act.wait_ge(consts, 1)
            act_xt(0)
            act.wait_ge(const_in, 16 * 10)
            nc.scalar.activation(a_neg[:, :], a_neg[:, :], ACT.Exp).then_inc(a_exp, 1)
            act_tasks(act, A_TASKS, 0)

            with act.Fori(0, BATCH) as b:
                for t in range(TB):
                    act.wait_ge(dp_mm, b * TB + t + 1)
                    if t == 0:
                        act.wait_ge(at_mm, 1 + 3 * b)
                        act.wait_ge(tok, 1 + 14 * b)
                    nc.scalar.copy(cd[:, t, :], bank[2 + t % 2][:, 0:DOWN]).then_inc(dp_cp, 1)
                for t in range(TB):
                    act.wait_ge(dp_cp, b * TB + t + 1)
                    for k, (c0, c1) in enumerate(((0, QR), (QR, QR + KR))):
                        nc.scalar.activation(q_tok[:, 0, :, :].rearrange("p h d -> p (h d)")[:, c0:c1], cd[:, t, c0:c1], ACT.Square,
                                             scale=float(c1 - c0) ** -0.5, accum_out=ms[:, 2 * t + k:2 * t + k + 1]).then_inc(sq, 1)
                        act.wait_ge(sq, b * 2 * TB + 2 * t + k + 1)
                act_xt(b + 1)
                for k, (dst, src) in enumerate(((qa_hi[:, :], bank[0][:, :]), (qb_hl[0:QB, :], bank[1][0:QB, :]),
                                                (kt_hi[:, :], bank[6][:, :]))):
                    act.wait_ge(at_mm, 1 + 3 * b + k + 1)
                    nc.scalar.copy(dst, src).then_inc(at_hi, 1)

                def exp(n, h):
                    w = (tile_of(n) + 1) * P
                    act.wait_ge(s_max, b * HEADS * TB + G * n + h + 1)
                    if h == 0 and n >= 2:
                        act.wait_ge(pt_mm, b * BLOCKS + blocks_before(n - 1))
                    nc.scalar.activation(prob[:, n % 2, h, 0:w], bank[2 + h % 2][:, 0:w], ACT.Exp,
                                         bias=bias_m[:, n % 2, h:h + 1], scale=-1.0,
                                         accum_out=den[:, n % 2, h:h + 1]).then_inc(s_exp, 1)

                def q_copy(n):
                    act.wait_ge(qa_mm, b * UNITS + n + 1)
                    if n >= 2:
                        act.wait_ge(qt_mm, b * UNITS + n - 1)
                    nc.scalar.mul(q_tok[:, n % 2, :, :].rearrange("p h d -> p (h d)"), bank[0][:, :], -SM_SCALE)\
                        .then_inc(qa_cp, 1)

                def qt_high(n):
                    act.wait_ge(qt_mm, b * UNITS + n + 1)
                    if n >= 2:
                        act.wait_ge(s_mm, b * HEADS * TB + G * (n - 1))
                    nc.scalar.copy(qt_hi[:, n % 2, :, :].rearrange("p h d -> p (h d)"), bank[1][:, :])\
                        .then_inc(qt_hi_s, 1)

                def normalise(n):
                    w = (tile_of(n) + 1) * P
                    act.wait_ge(recip_s, 2 * (b * UNITS + n) + 1)
                    for h in range(2):
                        nc.scalar.activation(prob[:, n % 2, h, 0:w], prob[:, n % 2, h, 0:w], ACT.Copy,
                                             scale=rden[:, n % 2, h:h + 1]).then_inc(norm_a, 1)

                def pt_high(n, j):
                    c = blocks_before(n) + j
                    act.wait_ge(pt_mm, b * BLOCKS + c + 1)
                    if c >= 2:
                        act.wait_ge(pv_mm, b * BLOCKS + c - 1)
                    nc.scalar.copy(pt_hi[:, c % 2, :, :].rearrange("p h d -> p (h d)"), bank[4 + c % 2][:, :])\
                        .then_inc(pt_hi_s, 1)

                def out_high(n):
                    act.wait_ge(pv_mm, b * BLOCKS + blocks_before(n + 1))
                    if n >= 2:
                        act.wait_ge(y_mm, b * UNITS + n - 1)
                    nc.scalar.copy(o_a[:, n % 2, :, :].rearrange("p h d -> p (h d)"), bank[6][:, :])\
                        .then_inc(o_hi_s, 1)
                    nc.scalar.copy(o_b[0:KR, n % 2, :, :].rearrange("p h d -> p (h d)"), bank[6][0:KR, :])\
                        .then_inc(o_hi_s, 1)

                for s in range(UNITS + 4):
                    n, m, y = s - 2, s - 3, s - 4

                    def high(k):
                        if 0 <= m < UNITS and k <= tile_of(m):
                            pt_high(m, k)

                    for k in range(G):
                        if 0 <= n < UNITS:
                            exp(n, k)
                        if k == 0 and 0 <= y:
                            out_high(y)
                        if k == 1 and 0 <= s - 1 < UNITS:
                            qt_high(s - 1)
                        if k == 1 and s < UNITS:
                            q_copy(s)
                        if k:
                            high(k - 1)
                        if k == 2 and 0 <= n < UNITS:
                            normalise(n)
                    high(G - 1)

            act.wait_ge(pads, 3)
            act_tasks(act, F_TASKS, NA)

            def ffn_act(layer):
                f = ffn[layer]
                n_gu = 2 * FT + 1
                with act.Fori(0, BATCH) as b:

                    def gate(m):
                        act.wait_ge(f.gu_mm, b * n_gu + 2 * m + 1)
                        if m >= 2:
                            act.wait_ge(f.hf, 1 + b * (FT + 1) + m - 1)
                        if m < FT:
                            nc.scalar.activation(silu[:, m % 2, :], bank[m % 2][:, :], ACT.Silu).then_inc(f.silu, 1)
                        else:
                            nc.scalar.activation(silu[UP0:UP0 + TAIL, m % 2, :], bank[m % 2][0:TAIL, :], ACT.Silu)\
                                .then_inc(f.silu, 1)

                    def high(m):
                        act.wait_ge(f.hf, 1 + b * (FT + 1) + m + 1)
                        rows = P if m < FT else TAIL
                        nc.scalar.copy(h_hi[0:rows, m, :], h_f[0:rows, m % 2, :]).then_inc(f.hhi, 1)

                    gate(0)
                    for m in range(FT + 1):
                        if m < FT:
                            gate(m + 1)
                        high(m)
                    act_xt(BATCH * layer + b + 1)

            ffn_act(1)

            act.wait_ge(bias_in, 16 * CK)
            with act.Fori(0, BATCH) as b:
                for m in range(CK):
                    act.wait_ge(xp_mm, CK * b + m + 1)
                    nc.scalar.copy(xp_hi[:, m, :], bank[m][:, :]).then_inc(xp_hi_s, 1)
                for m in range(CK):
                    act.wait_ge(dt_mm, CK * b + m + 1)
                    act.wait_ge(dt_sum, 1 + CK * b)
                    nc.scalar.activation(sp[:, m, :], bank[2 + m][:, :], ACT.Abs, bias=dt_bias[:, m:m + 1])\
                        .then_inc(sp_act, 1)
                act_xt(BATCH * 2 + b + 1)
                act.wait_ge(sp_act, 4 * b + 2)
                nc.scalar.activation(sp[:, :, :], sp[:, :, :], ACT.Exp, scale=-1.0).then_inc(sp_act, 1)
                act.wait_ge(sp_act, 4 * b + 3)
                nc.scalar.activation(sp[:, :, :], sp[:, :, :], ACT.Ln, bias=one[:, 0:1]).then_inc(sp_act, 1)
                act.wait_ge(scan_s, 1 + CK * b)
                for m in range(CK):
                    act.wait_ge(dt_sum, 1 + CK * b + m + 1)
                    nc.scalar.activation(decay[:, m, :], dts[:, m, :], ACT.Exp, scale=a_neg[:, m:m + 1])\
                        .then_inc(dec_s, 1)
                for m in range(CK):
                    act.wait_ge(scan_s, 1 + CK * b + m + 1)
                    act.wait_ge(so_mm, 1 + TB * b)
                    nc.scalar.copy(y_hi[:, m, :], ys[:, m, :]).then_inc(y_hi_s, 1)

            ffn_act(3)

        @block.vector
        def _(dve):
            prime(dve, "dve")
            nc.vector.memset(one[:, :], 1.0).then_inc(consts, 1)
            dve.wait_ge(x_in_s[0], 16)
            dve_ln(0, 0)
            dve_xt(0)
            dve.wait_ge(gu_in, 64)
            nc.vector.tensor_copy(idx_gu[:, :, :], raw_gu[:, :, :]).then_inc(idx_ready, 1)
            dve.wait_ge(dn_in, 16)
            nc.vector.tensor_copy(idx_dn[:, :, :], raw_dn[:, :, :]).then_inc(idx_ready, 1)
            dve.wait_ge(a_exp, 1)
            nc.vector.tensor_scalar(a_neg[:, :], a_neg[:, :], -1.0, None, ALU.mult).then_inc(a_ready, 1)
            idx_dn_f = idx_dn[:, :, :].rearrange("p c f -> p (c f)")

            def lookup(v):
                if v == 1:
                    dve.wait_ge(dlut_hot, 1)
                if v > 1:
                    dve.wait_ge(dlut_sum, v - 1)
                nc.vector.tensor_scalar(hot_dn[:, :] if v else w_dn[:, :], idx_dn_f, float(v), lut[:, v:v + 1],
                                        ALU.is_equal, ALU.mult).then_inc(dlut_hot, 1)
                if v:
                    dve.wait_ge(dlut_hot, v + 1)
                    nc.vector.tensor_tensor(w_dn[:, :], w_dn[:, :], hot_dn[:, :], ALU.add).then_inc(dlut_sum, 1)

            dve.wait_ge(idx_ready, 2)
            dve_tasks(dve, A_TASKS, 0, lookup)
            for b in range(1, BATCH):
                dve.wait_ge(x_in_s[b], 16)

            with dve.Fori(0, BATCH) as b:
                dve.wait_ge(x_add[0], 1 + b * TB)
                dve_ln(b + 1, (b + 1) % BATCH)

                dve.wait_ge(sq, (b + 1) * 2 * TB)
                nc.vector.tensor_scalar(rms_v[:, :], ms[:, :], RMS_EPS, None, ALU.add).then_inc(rms_ref, 1)
                dve_rsqrt(rms_ref, (RSQRT + 1) * b + 1, rms_v[:, :], rms_r[:, :], rms_t[:, :])
                for t in range(TB):
                    nc.vector.tensor_scalar(cd[:, t, 0:QR], cd[:, t, 0:QR], rms_r[:, 2 * t:2 * t + 1], None, ALU.mult)\
                        .then_inc(tok, 1)
                for t in range(TB):
                    nc.vector.scalar_tensor_tensor(out=cd[:, t, QR:QR + KR], in0=cd[:, t, QR:QR + KR],
                                                   scalar=rms_r[:, 2 * t + 1:2 * t + 2], in1=kvn[:, :],
                                                   op0=ALU.mult, op1=ALU.mult).then_inc(tok, 1)
                kr, half = cd[:, :, QR + KR:DOWN], ROPE // 2
                nc.vector.tensor_tensor(k_rot[:, :, 0:half], kr[:, :, half:ROPE], sin2[:, :, 0:half], ALU.mult)\
                    .then_inc(tok, 1)
                nc.vector.tensor_tensor(k_rot[:, :, half:ROPE], kr[:, :, 0:half], sin2[:, :, half:ROPE], ALU.mult)\
                    .then_inc(tok, 1)
                dve.wait_ge(tok, 1 + 14 * b + 10)
                nc.vector.tensor_tensor(kr, kr, cos2[:, :, :], ALU.mult).then_inc(tok, 1)
                dve.wait_ge(tok, 1 + 14 * b + 11)
                nc.vector.tensor_tensor(kr, kr, k_rot[:, :, :], ALU.add).then_inc(tok, 1)
                kv = cd[:, :, QR:QR + KR]
                nc.vector.tensor_copy(v_hl[:, :, 0, :], kv).then_inc(tok, 1)
                dve.wait_ge(tok, 1 + 14 * b + 13)
                nc.vector.tensor_tensor(v_hl[:, :, 1, :], kv, v_hl[:, :, 0, :], ALU.subtract).then_inc(tok, 1)
                dve_xt(b + 1)
                for k, (dst, src, hi) in enumerate(((qa_lo[:, :], bank[0][:, :], qa_hi[:, :]),
                                                    (qb_hl[QB:P, :], bank[1][0:QB, :], qb_hl[0:QB, :]),
                                                    (kt_lo[:, :], bank[6][:, :], kt_hi[:, :]))):
                    dve.wait_ge(at_hi, 3 * b + k + 1)
                    nc.vector.tensor_tensor(dst, src, hi, ALU.subtract).then_inc(at_lo, 1)

                def row_max(n, h):
                    w = (tile_of(n) + 1) * P
                    dve.wait_ge(s_mm, b * HEADS * TB + G * n + h + 1)
                    if n >= 2:
                        dve.wait_ge(s_exp, 1 + b * HEADS * TB + G * (n - 2) + h + 1)
                    settle(n % 2 * G + h)
                    nc.vector.tensor_tensor_reduce(out=bank[2 + h % 2][:, 0:w], in0=bank[2 + h % 2][:, 0:w],
                                                   in1=mask[:, TB * P - w:TB * P], scale=1.0, scalar=3e38,
                                                   op0=ALU.add, op1=ALU.min,
                                                   accum_out=bias_m[:, n % 2, h:h + 1]).then_inc(s_max, 1)

                def rope_q(n):
                    i = tile_of(n)
                    q = q_tok[:, n % 2, :, ROPE:2 * ROPE]
                    cs = cos2[:, i:i + 1, :].to_broadcast([P, G, ROPE])
                    s0 = sin2[:, i:i + 1, 0:half].to_broadcast([P, G, half])
                    s1 = sin2[:, i:i + 1, half:ROPE].to_broadcast([P, G, half])
                    k = b * 4 * UNITS + 4 * n
                    dve.wait_ge(qa_cp, 1 + b * UNITS + n + 1)
                    if n:
                        dve.wait_ge(q_rope, k)
                    nc.vector.tensor_tensor(q_rot[:, :, 0:half], q[:, :, half:ROPE], s0, ALU.mult).then_inc(q_rope, 1)
                    nc.vector.tensor_tensor(q_rot[:, :, half:ROPE], q[:, :, 0:half], s1, ALU.mult).then_inc(q_rope, 1)
                    dve.wait_ge(q_rope, k + 2)
                    nc.vector.tensor_tensor(q, q, cs, ALU.mult).then_inc(q_rope, 1)
                    dve.wait_ge(q_rope, k + 3)
                    nc.vector.tensor_tensor(q, q, q_rot[:, :, :], ALU.add).then_inc(q_rope, 1)

                def qt_low(n):
                    dve.wait_ge(qt_hi_s, b * UNITS + n + 1)
                    if n >= 2:
                        dve.wait_ge(s_mm, b * HEADS * TB + G * (n - 1))
                    nc.vector.tensor_tensor(qt_lo[:, n % 2, :, :].rearrange("p h d -> p (h d)"), bank[1][:, :],
                                            qt_hi[:, n % 2, :, :].rearrange("p h d -> p (h d)"), ALU.subtract)\
                        .then_inc(qt_lo_s, 1)

                def recip(n, k):
                    dve.wait_ge(s_exp, 1 + b * HEADS * TB + G * n + 2 * k + 2)
                    if n >= 2:
                        dve.wait_ge((norm_a, norm_d)[k], b * 2 * UNITS + 2 * (n - 1))
                    nc.vector.reciprocal(rden[:, n % 2, 2 * k:2 * k + 2], den[:, n % 2, 2 * k:2 * k + 2])\
                        .then_inc(recip_s, 1)

                def normalise(n):
                    w = (tile_of(n) + 1) * P
                    dve.wait_ge(recip_s, 2 * (b * UNITS + n) + 2)
                    for h in range(2, G):
                        nc.vector.tensor_scalar(prob[:, n % 2, h, 0:w], prob[:, n % 2, h, 0:w],
                                                rden[:, n % 2, h:h + 1], None, ALU.mult).then_inc(norm_d, 1)

                def pt_low(n, j):
                    c = blocks_before(n) + j
                    dve.wait_ge(pt_hi_s, b * BLOCKS + c + 1)
                    if c >= 2:
                        dve.wait_ge(pv_mm, b * BLOCKS + c - 1)
                    nc.vector.tensor_tensor(pt_lo[:, c % 2, :, :].rearrange("p h d -> p (h d)"), bank[4 + c % 2][:, :],
                                            pt_hi[:, c % 2, :, :].rearrange("p h d -> p (h d)"), ALU.subtract)\
                        .then_inc(pt_lo_s, 1)

                def out_low(n):
                    dve.wait_ge(o_hi_s, 2 * (b * UNITS + n) + 2)
                    nc.vector.tensor_tensor(o_b[KR:P, n % 2, :, :].rearrange("p h d -> p (h d)"), bank[6][0:KR, :],
                                            o_a[0:KR, n % 2, :, :].rearrange("p h d -> p (h d)"), ALU.subtract)\
                        .then_inc(o_lo_s, 1)

                for s in range(UNITS + 5):
                    n, m, y = s - 2, s - 3, s - 5

                    def low(k):
                        if 0 <= m < UNITS and k <= tile_of(m):
                            pt_low(m, k)

                    for k in range(G):
                        if 0 <= n < UNITS:
                            row_max(n, k)
                        if k == 1 and 0 <= s - 4 < UNITS:
                            out_low(s - 4)
                        if k == 1 and 0 <= y and y % G == G - 1:
                            dve.wait_ge(y_mm, b * UNITS + y + 1)
                            dve_x_add(0, b, tile_of(y), bank[7])
                        if k == 1 and 0 <= s - 1 < UNITS:
                            qt_low(s - 1)
                        if k == 1 and 0 <= n < UNITS:
                            recip(n, 0)
                        if k in (1, 2):
                            low(k - 1)
                    if s < UNITS:
                        rope_q(s)
                    low(G - 2)
                    if 0 <= n < UNITS:
                        recip(n, 1)
                        normalise(n)
                    low(G - 1)

            dve.wait_ge(y_mm, BATCH * UNITS)
            nc.vector.memset(h_hi[32:64, FT, :].bitcast(F32), 0.0).then_inc(pads, 1)
            nc.vector.memset(dn_hi[32:64, FT, :].bitcast(F32), 0.0).then_inc(pads, 1)
            dve_tasks(dve, F_TASKS, NA)

            def ffn_dve(layer):
                f = ffn[layer]
                n_gu = 2 * FT + 1
                dve.wait_ge(x_add[layer - 1], 1 + BATCH * TB)
                with dve.Fori(0, BATCH) as b:
                    dve.wait_ge(x_add[layer], 1 + b * TB)
                    dve_ln(BATCH * layer + b + 1, (b + 1) % BATCH)
                    for m in range(FT + 1):
                        k = b * (FT + 1) + m
                        dve.wait_ge(f.silu, 1 + k + 1)
                        if m < FT:
                            dve.wait_ge(f.gu_mm, b * n_gu + 2 * m + 2)
                        if m >= 2:
                            dve.wait_ge(f.hlo, k - 1)
                        if m < FT:
                            nc.vector.tensor_tensor(h_f[:, m % 2, :], bank[2 + m % 2][:, :], silu[:, m % 2, :],
                                                    ALU.mult).then_inc(f.hf, 1)
                        else:
                            nc.vector.tensor_tensor(h_f[0:TAIL, m % 2, :], bank[m % 2][UP0:UP0 + TAIL, :],
                                                    silu[UP0:UP0 + TAIL, m % 2, :], ALU.mult).then_inc(f.hf, 1)
                        dve.wait_ge(f.hhi, k + 1)
                        if m < FT:
                            nc.vector.tensor_tensor(h_lo[:, m, :], h_f[:, m % 2, :], h_hi[:, m, :],
                                                    ALU.subtract).then_inc(f.hlo, 1)
                        else:
                            nc.vector.tensor_tensor(h_hi[UP0:UP0 + TAIL, m, :], h_f[0:TAIL, m % 2, :],
                                                    h_hi[0:TAIL, m, :], ALU.subtract).then_inc(f.hlo, 1)
                    dve_xt(BATCH * layer + b + 1)
                    for t in range(TB):
                        dve.wait_ge(f.dn_mm, b * TB + t + 1)
                        dve_x_add(layer, b, t, bank[6 + t % 2])

            ffn_dve(1)

            dve.wait_ge(x_add[1], 1 + BATCH * TB)
            dve.wait_ge(a_ready, 1)
            dve.wait_ge(bias_in, 16 * CK)
            with dve.Fori(0, BATCH) as b:
                dve.wait_ge(x_add[2], 1 + b * TB)
                dve_ln(BATCH * 2 + b + 1, (b + 1) % BATCH)
                for m in range(CK):
                    dve.wait_ge(xp_hi_s, CK * b + m + 1)
                    nc.vector.tensor_tensor(xp_lo[:, m, :], bank[m][:, :], xp_hi[:, m, :], ALU.subtract)\
                        .then_inc(xp_lo_s, 1)
                for m in range(CK):
                    dve.wait_ge(sp_act, 4 * b + m + 1)
                    if m == 0:
                        dve.wait_ge(dec_s, 1 + CK * b)
                    nc.vector.tensor_scalar(dts[:, m, :], bank[2 + m][:, :], dt_bias[:, m:m + 1], 0.0,
                                            ALU.add, ALU.max).then_inc(sp_relu, 1)
                dve_xt(BATCH * 2 + b + 1)
                dve.wait_ge(sp_act, 4 * b + 4)
                dve.wait_ge(sp_relu, 1 + CK * b + 2)
                for m in range(CK):
                    nc.vector.tensor_tensor(dts[:, m, :], dts[:, m, :], sp[:, m, :], ALU.add).then_inc(dt_sum, 1)
                dve.wait_ge(y_hi_s, 1 + CK * b)
                dve.wait_ge(y_lo_s, 1 + CK * b)
                for m in range(CK):
                    dve.wait_ge(dec_s, 1 + CK * b + m + 1)
                    nc.vector.tensor_tensor_scan(ys[:, m, :], decay[:, m, :], bank[m][:, :], 0.0,
                                                 ALU.mult, ALU.add).then_inc(scan_s, 1)
                for m in range(CK):
                    dve.wait_ge(y_hi_s, 1 + CK * b + m + 1)
                    nc.vector.tensor_tensor(y_lo[:, m, :], ys[:, m, :], y_hi[:, m, :], ALU.subtract)\
                        .then_inc(y_lo_s, 1)
                for t in range(TB):
                    dve.wait_ge(so_mm, 1 + TB * b + t + 1)
                    dve_x_add(2, b, t, bank[6 + t % 2])

            ffn_dve(3)

        @block.tensor
        def _(pe):
            prime(pe, "pe")
            pe.wait_ge(ident_in, 16)
            pe_xt(0)
            wait_xt(pe, 0)
            pe_tasks(pe, A_TASKS, 0)
            pe.wait_ge(prep_act, NA)
            pe.wait_ge(prep_dve, NA)

            with pe.Fori(0, BATCH) as b:
                wait_xt(pe, b)
                for t in range(TB):
                    if t == 0:
                        pe.wait_ge(s_exp, 1 + b * HEADS * TB)
                    if t >= 2:
                        pe.wait_ge(dp_cp, b * TB + t - 1)
                    tt = slice(t * P, (t + 1) * P)
                    split_mm(bank[2 + t % 2][:, 0:DOWN],
                             [(xt_hi[:, c, tt], xt_lo[:, c, tt], down_hi[:, c, :], down_lo[:, c, :])
                              for c in range(CK)], True, True).then_inc(dp_mm, 1)
                pe_xt(b + 1)
                pe.wait_ge(tok, 1 + 14 * b + 12)
                for o, c0, c1 in ((bank[0], 0, P), (bank[1], P, QR), (bank[6], QR, DOWN)):
                    for t in range(TB):
                        last = nc.tensor.transpose(o[0:c1 - c0, t * P:(t + 1) * P], cd[:, t, c0:c1], ident[:, :])
                    last.then_inc(at_mm, 1)
                pe.wait_ge(at_hi, 3 * b + 3)
                pe.wait_ge(at_lo, 3 * b + 3)
                pe.wait_ge(tok, 1 + 14 * b + 14)
                wait_xt(pe, b + 1)

                def q_up(n):
                    tt = slice(tile_of(n) * P, (tile_of(n) + 1) * P)
                    g = n % (HEADS // G)

                    def w(m, rows=P):
                        return m[0:rows, g * G:(g + 1) * G, :, :].rearrange("p h a r -> p (h a r)")
                    pe.wait_ge(qa_cp, 1 + b * UNITS + n)
                    o = bank[0][:, :]
                    nc.tensor.matmul(o, qa_hi[:, tt], w(wa_hi), start=True, stop=False)
                    nc.tensor.matmul(o, qa_hi[:, tt], w(wa_lo), start=False, stop=False)
                    nc.tensor.matmul(o, qa_lo[:, tt], w(wa_hi), start=False, stop=False)
                    nc.tensor.matmul(o, qb_hl[:, tt], w(wb_hi), start=False, stop=False)
                    nc.tensor.matmul(o, qb_hl[0:QB, tt], w(wb_lo, QB), start=False, stop=True).then_inc(qa_mm, 1)

                def q_transpose(n):
                    pe.wait_ge(q_rope, 4 * (b * UNITS + n + 1))
                    pe.wait_ge(qt_lo_s, 1 + b * UNITS + n)
                    for h in range(G):
                        last = nc.tensor.transpose(bank[1][:, h * P:(h + 1) * P], q_tok[:, n % 2, h, :], ident[:, :])
                    last.then_inc(qt_mm, 1)

                def scores(n, h):
                    w = (tile_of(n) + 1) * P
                    if h == 0:
                        pe.wait_ge(qt_hi_s, b * UNITS + n + 1)
                        pe.wait_ge(qt_lo_s, 1 + b * UNITS + n + 1)
                    if G * n + h >= 2:
                        pe.wait_ge(s_exp, 1 + b * HEADS * TB + G * n + h - 1)
                    split_mm(bank[2 + h % 2][:, 0:w],
                             [(qt_hi[:, n % 2, h, :], qt_lo[:, n % 2, h, :], kt_hi[:, 0:w], kt_lo[:, 0:w])],
                             True, True).then_inc(s_mm, 1)

                def p_transpose(n, j):
                    c = blocks_before(n) + j
                    if j == 0:
                        pe.wait_ge(norm_a, b * 2 * UNITS + 2 * n + 2)
                        pe.wait_ge(norm_d, b * 2 * UNITS + 2 * n + 2)
                    if c >= 2:
                        pe.wait_ge(pt_lo_s, b * BLOCKS + c - 1)
                    for h in range(G):
                        last = nc.tensor.transpose(bank[4 + c % 2][:, h * P:(h + 1) * P],
                                                   prob[:, n % 2, h, j * P:(j + 1) * P], ident[:, :])
                    last.then_inc(pt_mm, 1)

                def values(n, j):
                    c = blocks_before(n) + j
                    if j == 0:
                        pe.wait_ge(o_lo_s, 1 + b * UNITS + n)
                    v = v_hl[:, j, :, :].rearrange("p a r -> p (a r)")
                    pe.wait_ge(pt_hi_s, b * BLOCKS + c + 1)
                    nc.tensor.matmul(bank[6][:, :], v, pt_hi[:, c % 2, :, :].rearrange("p h d -> p (h d)"),
                                     start=j == 0, stop=False)
                    pe.wait_ge(pt_lo_s, b * BLOCKS + c + 1)
                    nc.tensor.matmul(bank[6][:, :], v, pt_lo[:, c % 2, :, :].rearrange("p h d -> p (h d)"),
                                     start=False, stop=j == tile_of(n)).then_inc(pv_mm, 1)

                def project(n):
                    g = n % (HEADS // G)
                    pe.wait_ge(o_hi_s, 2 * (b * UNITS + n) + 2)
                    pe.wait_ge(o_lo_s, 1 + b * UNITS + n + 1)
                    if g == 0:
                        pe.wait_ge(x_add[0], 1 + b * TB + tile_of(n))
                    for h in range(G):
                        nc.tensor.matmul(bank[7][:, 0:DIM], o_a[:, n % 2, h, :], wo_a[:, g * G + h, :],
                                         start=g == 0 and h == 0, stop=False)
                        last = nc.tensor.matmul(bank[7][:, 0:DIM], o_b[:, n % 2, h, :], wo_b[:, g * G + h, :],
                                                start=False, stop=g == HEADS // G - 1 and h == G - 1)
                    last.then_inc(y_mm, 1)

                for s in range(UNITS + 4):
                    n, m, y = s - 2, s - 3, s - 4
                    if 0 <= n < UNITS:
                        scores(n, 0)
                        scores(n, 1)
                    if 0 <= s - 1 < UNITS:
                        q_transpose(s - 1)
                    if s < UNITS:
                        q_up(s)
                    blocks = tile_of(m) + 1 if 0 <= m < UNITS else 0
                    for j in range(min(2, blocks)):
                        p_transpose(m, j)
                    if 0 <= n < UNITS:
                        scores(n, 2)
                    for j in range(TB - 1):
                        if j < blocks:
                            values(m, j)
                        if j + 2 < blocks:
                            p_transpose(m, j + 2)
                        if j == 0 and 0 <= n < UNITS:
                            scores(n, 3)
                    if 0 <= y:
                        project(y)
                    if blocks == TB:
                        values(m, TB - 1)

            pe.wait_ge(lut_sum, (LUT - 1) * (GT * DIM // GC))
            pe.wait_ge(dlut_sum, LUT - 1)
            pe.wait_ge(x_add[0], 1 + BATCH * TB)
            pe_tasks(pe, F_TASKS, NA)
            pe.wait_ge(prep_act, NA + NF)
            pe.wait_ge(prep_dve, NA + NF)

            def ffn_pe(layer):
                f = ffn[layer]
                with pe.Fori(0, BATCH) as b:
                    wait_xt(pe, BATCH * layer + b)

                    def up(o, c0, cols):
                        pairs = [(gu_hi[:, c, c0:c0 + cols], gu_lo[:, c, c0:c0 + cols], xt_hi[:, c, :], xt_lo[:, c, :])
                                 for c in range(CK)]
                        split_mm(o[0:cols, :], pairs, True, True).then_inc(f.gu_mm, 1)

                    for m in range(FT + 1):
                        k = b * (FT + 1) + m
                        pe.wait_ge(f.silu, (k if m >= 2 else b * (FT + 1) + 1))
                        pe.wait_ge(f.hf, (k if m >= 2 else b * (FT + 1) + 1))
                        if m < FT:
                            up(bank[m % 2], 2 * m * P, P)
                            up(bank[2 + m % 2], (2 * m + 1) * P, P)
                        else:
                            up(bank[m % 2], 2 * m * P, UP0 + TAIL)
                    pe_xt(BATCH * layer + b + 1)
                    for t in range(TB):
                        pe.wait_ge(x_add[layer], 1 + b * TB + (t - 1 if t >= 2 else 0))
                        o = bank[6 + t % 2][:, 0:DIM]
                        tt = slice(t * P, (t + 1) * P)
                        for m in range(FT):
                            pe.wait_ge(f.hlo, b * (FT + 1) + m + 1)
                            split_mm(o, [(h_hi[:, m, tt], h_lo[:, m, tt], dn_hi[:, m, :], dn_lo[:, m, :])],
                                     m == 0, False)
                        pe.wait_ge(f.hlo, b * (FT + 1) + FT + 1)
                        nc.tensor.matmul(o, h_hi[0:UP0 + TAIL, FT, tt], dn_hi[0:UP0 + TAIL, FT, :],
                                         start=False, stop=False)
                        nc.tensor.matmul(o, h_hi[0:TAIL, FT, tt], dn_lo[0:TAIL, FT, :],
                                         start=False, stop=True).then_inc(f.dn_mm, 1)

            ffn_pe(1)

            pe.wait_ge(x_add[1], 1 + BATCH * TB)
            with pe.Fori(0, BATCH) as b:
                wait_xt(pe, BATCH * 2 + b)
                for m in range(CK):
                    pe.wait_ge(scan_s, 1 + CK * b)
                    mm = slice(m * P, (m + 1) * P)
                    split_mm(bank[m][:, :], [(ssm_hi[:, 0, c, mm], ssm_lo[:, 0, c, mm], xt_hi[:, c, :], xt_lo[:, c, :])
                                             for c in range(CK)], True, True).then_inc(xp_mm, 1)
                pe_xt(BATCH * 2 + b + 1)
                pe.wait_ge(xp_hi_s, CK * b + 2)
                pe.wait_ge(xp_lo_s, CK * b + 2)
                for m in range(CK):
                    pe.wait_ge(sp_relu, 1 + CK * b)
                    mm = slice(m * P, (m + 1) * P)
                    split_mm(bank[2 + m][:, :], [(ssm_hi[:, 1, c, mm], ssm_lo[:, 1, c, mm], xp_hi[:, c, :], xp_lo[:, c, :])
                                                 for c in range(CK)], True, True).then_inc(dt_mm, 1)
                pe.wait_ge(y_hi_s, 1 + CK * b + 2)
                pe.wait_ge(y_lo_s, 1 + CK * b + 2)
                for t in range(TB):
                    pe.wait_ge(x_add[2], 1 + b * TB + (t - 1 if t >= 2 else 0))
                    tt = slice(t * P, (t + 1) * P)
                    split_mm(bank[6 + t % 2][:, 0:DIM],
                             [(y_hi[:, c, tt], y_lo[:, c, tt], ssm_hi[:, 2, c, :], ssm_lo[:, 2, c, :])
                              for c in range(CK)], True, True).then_inc(so_mm, 1)
            pe.wait_ge(x_add[2], 1 + BATCH * TB)
            ffn_pe(3)


_INS = ['L0_attn_a_x', 'L0_attn_a_wq_down', 'L0_attn_a_wq_up', 'L0_attn_a_wq_rope', 'L0_attn_a_q_norm_w',
        'L0_attn_a_wkv_down', 'L0_attn_a_kv_norm_w', 'L0_attn_a_wkv_up', 'L0_attn_a_wk_rope', 'L0_attn_a_wo',
        'L0_attn_b_W_in', 'L0_attn_b_W_out', 'L0_attn_b_log_A', 'L0_attn_b_W_dt', 'L0_attn_b_b_dt',
        'L0_ffn_lut', 'L0_ffn_gate_idx', 'L0_ffn_up_idx', 'L0_ffn_down_idx']


def _constants(np):
    ident = np.eye(P, dtype=np.float32)
    mask = np.zeros((P, TB * P), np.float32)
    mask[:, -P:] = np.where(np.arange(P)[None, :] > np.arange(P)[:, None], np.float32(BIG), np.float32(0))
    inv = (1.0 / np.float32(10000.0) ** (np.arange(0, ROPE, 2, dtype=np.float32) / np.float32(ROPE))).astype(np.float32)
    ang = np.outer(np.arange(SEQ, dtype=np.float32), inv).astype(np.float32)
    c, s = np.cos(ang), np.sin(ang)
    cos2 = np.concatenate([c, c], 1).reshape(TB, P, ROPE).transpose(1, 0, 2)
    sin2 = np.concatenate([-s, s], 1).reshape(TB, P, ROPE).transpose(1, 0, 2)
    return {"ident": ident, "mask": mask, "cos2": np.ascontiguousarray(cos2), "sin2": np.ascontiguousarray(sin2)}


def kernel(**inputs):
    import numpy as _np
    import concourse.bacc as _bacc
    from concourse import mybir as _mybir
    from concourse.bass_utils import run_bass_kernel_spmd as _run

    nc = _bacc.Bacc("TRN2", target_bir_lowering=False, num_devices=1)
    arrays, args = {}, []
    named = [(n, inputs[n]) for n in _INS] + list(_constants(_np).items())
    for name, value in named:
        a = _np.ascontiguousarray(value)
        arrays[f"in_{name}_dram"] = a
        args.append(nc.dram_tensor(f"in_{name}_dram", a.shape, _mybir.dt.from_np(a.dtype), kind="ExternalInput").ap())
    out = nc.dram_tensor("out_0_dram", (BATCH, SEQ, DIM), F32, kind="ExternalOutput").ap()
    build(nc, *args, out)
    r = _run(nc, [arrays], core_ids=[0])
    return r.results[0]["out_0_dram"]
```

```python
import concourse.bass as bass
from concourse import mybir
from contextlib import ExitStack

F32 = mybir.dt.float32
F32R = mybir.dt.float32r
BF16 = mybir.dt.bfloat16
I32 = mybir.dt.int32
ALU = mybir.AluOpType
ACT = mybir.ActivationFunctionType

P = 128
BATCH, SEQ, DIM = 4, 512, 256
TB = SEQ // P
CK = DIM // P
HEADS, NOPE, ROPE, DV = 16, 128, 64, 128
QR, KR = 192, 64
QB = QR - P
DOWN = QR + KR + ROPE
G = 4
UNITS = TB * (HEADS // G)
BLOCKS = (HEADS // G) * TB * (TB + 1) // 2
INTER = 688
FT = INTER // P
TAIL = INTER - FT * P
UP0 = 64
GT = 2 * FT + 1
GW = 2 * FT * P + UP0 + TAIL
LUT = 16
SM_SCALE = float(NOPE + ROPE) ** -0.5
LN_EPS, RMS_EPS = 1e-5, 1e-6
BIG = 1e30
DEPTH = 6
GAPS = 13
LEAD = 8


def tile_of(n):
    return n // (HEADS // G)


def blocks_before(n):
    if n < 0:
        return blocks_before(UNITS + n) - blocks_before(UNITS)
    return sum(tile_of(m) + 1 for m in range(n))


def step_of(b, nb, step, n, *k):
    if 0 <= n < UNITS:
        step(b, n, *k)
    elif n >= UNITS and nb is not None:
        step(nb, n - UNITS, *k)


def free_after(e, sem, count):
    if not (isinstance(count, int) and count <= 0):
        e.wait_ge(sem, count)


class Arena:

    def __init__(self, nc, start, size):
        self.nc, self.at, self.end = nc, start, start + size

    def __call__(self, name, shape, dt):
        n = 2 if dt == BF16 else 4
        for s in shape[1:]:
            n *= s
        t = self.nc.alloc_sbuf_tensor_at(name, shape, dt, offset=self.at)
        self.at += (n + 31) // 32 * 32
        assert self.at <= self.end, (name, self.at, self.end)
        return t


def build(nc, x_in, wq_down, wq_up, wq_rope, q_norm_w, wkv_down, kv_norm_w, wkv_up, wk_rope, wo,
          w_in, w_out, log_a, w_dt, b_dt, lut_in, gate_idx, up_idx, down_idx,
          c_ident, c_mask, c_cos, c_sin, out):
    ctx = ExitStack()
    with ctx:
        start = (nc.sbuf_base + 63) // 64 * 64
        space = nc.sbuf_usable_end - start
        keep = Arena(nc, start, space)
        x = keep("x", [P, BATCH * TB, DIM], F32)
        idx_gu = keep("idx_gu", [P, GT, DIM], BF16)
        idx_dn = keep("idx_dn", [P, CK, INTER], BF16)
        w_gu = keep("w_gu", [P, GT, DIM], F32)
        w_dn = keep("w_dn", [P, CK * INTER], F32)
        raw_gu = nc.alloc_sbuf_tensor_at("raw_gu", [P, GT, DIM], I32, offset=keep.at - 4 * (GT * DIM + CK * INTER))
        raw_dn = nc.alloc_sbuf_tensor_at("raw_dn", [P, CK, INTER], I32, offset=keep.at - 4 * CK * INTER)
        down_hi = keep("down_hi", [P, CK, DOWN], F32R)
        down_lo = keep("down_lo", [P, CK, DOWN], F32R)
        ssm_hi = keep("ssm_hi", [P, 3, CK, DIM], F32R)
        ssm_lo = keep("ssm_lo", [P, 3, CK, DIM], F32R)
        cos2 = keep("cos2", [P, TB, ROPE], F32)
        sin2 = keep("sin2", [P, TB, ROPE], F32)
        mask = keep("mask", [P, TB * P], F32)
        ident = keep("ident", [P, P], F32)
        lut = keep("lut", [P, LUT], F32)
        qn_a = keep("qn_a", [P, 1], F32)
        qn_b = keep("qn_b", [P, 1], F32)
        kvn = keep("kvn", [P, KR], F32)
        dt_bias = keep("dt_bias", [P, CK], F32)
        a_neg = keep("a_neg", [P, CK], F32)
        one = keep("one", [P, 1], F32)
        scratch = keep("scratch", [P, 2 * G + 1], F32)
        stats = keep("stats", [P, TB, 6], F32)
        mv = keep("mv", [P, TB, 2], F32)
        ln_v = keep("ln_v", [P, TB], F32)
        ln_t = keep("ln_t", [P, TB], F32)
        ln_r = keep("ln_r", [P, TB], F32)
        ms = keep("ms", [P, TB * 2], F32)
        rms_v = keep("rms_v", [P, TB * 2], F32)
        rms_t = keep("rms_t", [P, TB * 2], F32)
        rms_r = keep("rms_r", [P, TB * 2], F32)
        bias_m = keep("bias_m", [P, 2, G], F32)
        den = keep("den", [P, 2, G], F32)
        rden = keep("rden", [P, 2, G], F32)
        xt_hi = keep("xt_hi", [P, CK, SEQ], F32R)
        xt_lo = keep("xt_lo", [P, CK, SEQ], F32R)
        xn = keep("xn", [P, TB, DIM], F32)

        r1_at, r1_size = keep.at, 65536
        r1 = Arena(nc, r1_at, r1_size)
        wa_hi = r1("wa_hi", [P, HEADS, 2, KR], F32R)
        wa_lo = r1("wa_lo", [P, HEADS, 2, KR], F32R)
        wb_hi = r1("wb_hi", [P, HEADS, 2, KR], F32R)
        wb_lo = r1("wb_lo", [QB, HEADS, 2, KR], F32R)
        ssm_at = r1.at
        wo_a = r1("wo_a", [P, HEADS, DIM], F32R)
        wo_at = r1.at
        wo_b = r1("wo_b", [P, HEADS, DIM], F32R)
        ssm_nat = nc.alloc_sbuf_tensor_at("ssm_nat", [P, 3, CK, DIM], F32, offset=ssm_at)
        wo_nat = nc.alloc_sbuf_tensor_at("wo_nat", [P, CK, HEADS * DV], F32, offset=wo_at)
        r1f = Arena(nc, r1_at, r1_size)
        gu_hi = r1f("gu_hi", [P, CK, GW], F32R)
        gu_lo = r1f("gu_lo", [P, CK, GW], F32R)
        dn_hi = r1f("dn_hi", [P, FT + 1, DIM], F32R)
        dn_lo = r1f("dn_lo", [P, FT + 1, DIM], F32R)
        h_hi = r1f("h_hi", [P, FT + 1, SEQ], F32R)
        h_lo = r1f("h_lo", [P, FT, SEQ], F32R)

        r2_at = r1_at + r1_size
        r2_size = start + space - r2_at
        r2s = Arena(nc, r2_at, r2_size)
        wqu = r2s("wqu", [P, HEADS, QR + QB], F32)
        wkn = r2s("wkn", [P, HEADS, KR], F32)
        wv2 = r2s("wv2", [P, HEADS, 2, KR], F32)
        wo_t = r2s("wo_t", [P, HEADS, DIM], F32)
        wqr = r2s("wqr", [P, HEADS // 2, QR + QB], F32)
        dn_nat = r2s("dn_nat", [P, 3, DIM], F32)
        r2 = Arena(nc, r2_at, r2_size)
        cd = r2("cd", [P, TB, DOWN], F32)
        k_rot = r2("k_rot", [P, TB, ROPE], F32)
        qa_hi = r2("qa_hi", [P, SEQ], F32R)
        qa_lo = r2("qa_lo", [P, SEQ], F32R)
        qb_hl = r2("qb_hl", [P, SEQ], F32R)
        kt_hi = r2("kt_hi", [P, SEQ], F32R)
        kt_lo = r2("kt_lo", [P, SEQ], F32R)
        v_hl = r2("v_hl", [P, TB, 2, KR], F32R)
        q_tok = r2("q_tok", [P, 2, G, P], F32)
        q_rot = r2("q_rot", [P, G, ROPE], F32)
        qt_hi = r2("qt_hi", [P, 2, G, P], F32R)
        qt_lo = r2("qt_lo", [P, 2, G, P], F32R)
        prob = r2("prob", [P, 2, G, SEQ], F32)
        pt_hi = r2("pt_hi", [P, 2, G, P], F32R)
        pt_lo = r2("pt_lo", [P, 2, G, P], F32R)
        o_a = r2("o_a", [P, 2, G, P], F32R)
        o_b = r2("o_b", [P, 2, G, P], F32R)
        r2f = Arena(nc, r2_at, r2_size)
        silu = r2f("silu", [P, 2, SEQ], F32)
        h_f = r2f("h_f", [P, 2, SEQ], F32)
        xp_hi = r2f("xp_hi", [P, CK, SEQ], F32R)
        xp_lo = r2f("xp_lo", [P, CK, SEQ], F32R)
        sp = r2f("sp", [P, CK, SEQ], F32)
        dts = r2f("dts", [P, CK, SEQ], F32)
        decay = r2f("decay", [P, CK, SEQ], F32)
        ys = r2f("ys", [P, CK, SEQ], F32)
        y_hi = r2f("y_hi", [P, CK, SEQ], F32R)
        y_lo = r2f("y_lo", [P, CK, SEQ], F32R)
        r2.at = max(r2.at, r2s.at)
        GC = GT * DIM // 11
        hot = r2("hot", [P, GC], F32)
        DN_POOL = CK * INTER // GC * GC - GC
        hot_dn = r2("hot_dn", [P, CK * INTER - DN_POOL], F32)

        bank = [nc.alloc_psum_tensor(f"bank{i}", [P, 512], F32) for i in range(8)]

        def sem(name):
            return ctx.enter_context(nc.semaphore(name))

        x_in_s = [sem(f"x_in{b}") for b in range(BATCH)]
        const_in, bias_in, ident_in, tables_in = sem("const_in"), sem("bias_in"), sem("ident_in"), sem("tables_in")
        dnat_in, ssm_in, wqu_in, wkn_in, wv_in, wqr_in, wo_in = (
            sem(n) for n in ("dnat_in", "ssm_in", "wqu_in", "wkn_in", "wv_in", "wqr_in", "wo_in"))
        gu_in, dn_in = sem("gu_in"), sem("dn_in")
        consts = sem("consts")
        pads = sem("pads")
        a_exp, a_ready = sem("a_exp"), sem("a_ready")
        idx_ready = sem("idx_ready")
        lut_hot, lut_sum = sem("lut_hot"), sem("lut_sum")
        dlut_hot, dlut_sum = sem("dlut_hot"), sem("dlut_sum")
        prep_mm, prep_act, prep_dve = sem("prep_mm"), sem("prep_act"), sem("prep_dve")
        ln_stats, ln_aggr, ln_ref, ln_norm = (
            sem(n) for n in ("ln_stats", "ln_aggr", "ln_ref", "ln_norm"))
        xt_mm, xt_hi_s, xt_lo_s = sem("xt_mm"), sem("xt_hi_s"), sem("xt_lo_s")

        dp_mm, dp_cp, sq, rms_ref, tok = (
            sem(n) for n in ("dp_mm", "dp_cp", "sq", "rms_ref", "tok"))
        at_mm, at_hi, at_lo = sem("at_mm"), sem("at_hi"), sem("at_lo")
        qa_mm, qa_cp, q_rope = sem("qa_mm"), sem("qa_cp"), sem("q_rope")
        qt_mm, qt_hi_s, qt_lo_s = sem("qt_mm"), sem("qt_hi_s"), sem("qt_lo_s")
        s_mm, s_max, s_exp = sem("s_mm"), sem("s_max"), sem("s_exp")
        recip_s, norm_a, norm_d = sem("recip_s"), sem("norm_a"), sem("norm_d")
        pt_mm, pt_hi_s, pt_lo_s, pv_mm = sem("pt_mm"), sem("pt_hi_s"), sem("pt_lo_s"), sem("pv_mm")
        o_hi_s, o_lo_s, y_mm = sem("o_hi_s"), sem("o_lo_s"), sem("y_mm")
        x_add = [sem(f"x_add{layer}") for layer in range(4)]

        class Ffn:
            def __init__(self, name):
                self.gu_mm, self.silu, self.hf, self.hhi, self.hlo, self.dn_mm = (
                    sem(name + n) for n in ("gu_mm", "silu", "hf", "hhi", "hlo", "dn_mm"))

        ffn = {1: Ffn("f1_"), 3: Ffn("f3_")}
        xp_mm, xp_hi_s, xp_lo_s, dt_mm = sem("xp_mm"), sem("xp_hi_s"), sem("xp_lo_s"), sem("dt_mm")
        sp_act, sp_relu, dt_sum, dec_s, scan_s = (
            sem(n) for n in ("sp_act", "sp_relu", "dt_sum", "dec_s", "scan_s"))
        y_hi_s, y_lo_s, so_mm = sem("y_hi_s"), sem("y_lo_s"), sem("so_mm")
        stored = sem("stored")

        block = ctx.enter_context(nc.Block())

        def t_down(c):
            def pe(e, o):
                for r, rows in ((0, P), (1, P), (2, ROPE)):
                    last = nc.tensor.transpose(o[:, r * P:r * P + rows], dn_nat[0:rows, r, c * P:(c + 1) * P],
                                               ident[0:rows, 0:rows])
                return last

            def act(e, o):
                return nc.scalar.copy(down_hi[:, c, :], o[:, 0:DOWN])

            def dve(e, o):
                return nc.vector.tensor_tensor(down_lo[:, c, :], o[:, 0:DOWN], down_hi[:, c, :], ALU.subtract)
            return pe, act, dve

        def split_scaled(o, hi, lo, s, rows):
            def act(e, b):
                return nc.scalar.activation(hi, o(b), ACT.Copy, scale=s[:, 0:1])

            def dve(e, b):
                return nc.vector.scalar_tensor_tensor(out=lo, in0=o(b)[0:rows], scalar=s[0:rows, 0:1],
                                                      in1=hi[0:rows], op0=ALU.mult, op1=ALU.subtract)
            return act, dve

        def t_nope(part, k):
            hs = slice(8 * k, 8 * k + 8)
            hi, lo, s, rows = ((wa_hi, wa_lo, qn_a, P), (wb_hi, wb_lo, qn_b, QB))[part]

            def pe(e, o):
                for j in range(8):
                    last = nc.tensor.matmul(o[:, j * KR:(j + 1) * KR], wqu[:, 8 * k + j, part * P:(part + 1) * P],
                                            wkn[:, 8 * k + j, :], start=True, stop=True)
                return last
            return (pe, *split_scaled(lambda b: b[:, :].rearrange("p (h r) -> p h r", h=8),
                                      hi[:, hs, 0, :], lo[:, hs, 0, :], s, rows))

        def t_rope(part, k):
            hs = slice(8 * k, 8 * k + 8)
            hi, lo, s, rows = ((wa_hi, wa_lo, qn_a, P), (wb_hi, wb_lo, qn_b, QB))[part]

            def pe(e, o):
                for j in range(4):
                    last = nc.tensor.transpose(o[:, j * P:(j + 1) * P], wqr[:, 4 * k + j, part * P:(part + 1) * P],
                                               ident[:, :])
                return last
            return (pe, *split_scaled(lambda b: b[:, :].rearrange("p (h r) -> p h r", h=8),
                                      hi[:, hs, 1, :], lo[:, hs, 1, :], s, rows))

        def t_wo_t(k):
            def pe(e, o):
                for j in range(2):
                    for r in range(CK):
                        last = nc.tensor.transpose(o[:, j * DIM + r * P:j * DIM + (r + 1) * P],
                                                   wo_nat[:, r, (2 * k + j) * DV:(2 * k + j + 1) * DV], ident[:, :])
                return last

            def act(e, o):
                return nc.scalar.copy(wo_t[:, 2 * k, :], o[:, 0:DIM])

            def dve(e, o):
                return nc.vector.tensor_copy(wo_t[:, 2 * k + 1, :], o[:, DIM:2 * DIM])
            return pe, act, dve

        def t_ssm(j):
            def pe(e, o):
                for c in range(CK):
                    for r in range(CK):
                        last = nc.tensor.transpose(o[:, c * DIM + r * P:c * DIM + (r + 1) * P],
                                                   ssm_nat[:, j, r, c * P:(c + 1) * P], ident[:, :])
                return last

            def act(e, o):
                return nc.scalar.copy(ssm_hi[:, j, :, :], o[:, :].rearrange("p (c n) -> p c n", c=CK))

            def dve(e, o):
                return nc.vector.tensor_tensor(ssm_lo[:, j, :, :], o[:, :].rearrange("p (c n) -> p c n", c=CK),
                                               ssm_hi[:, j, :, :], ALU.subtract)
            return pe, act, dve

        def t_vo(k):
            def pe(e, o):
                for j in range(2):
                    last = nc.tensor.matmul(o[:, j * DIM:(j + 1) * DIM],
                                            wv2[:, 2 * k + j, :, :].rearrange("p a r -> p (a r)"),
                                            wo_t[:, 2 * k + j, :], start=True, stop=True)
                return last

            def act(e, o):
                nc.scalar.copy(wo_a[:, 2 * k:2 * k + 2, :], o[:, :].rearrange("p (h n) -> p h n", h=2))
                return nc.scalar.copy(wo_b[KR:P, 2 * k:2 * k + 2, :], o[KR:P, :].rearrange("p (h n) -> p h n", h=2))

            def dve(e, o):
                return nc.vector.tensor_tensor(wo_b[0:KR, 2 * k:2 * k + 2, :],
                                               o[0:KR, :].rearrange("p (h n) -> p h n", h=2),
                                               wo_a[0:KR, 2 * k:2 * k + 2, :], ALU.subtract)
            return pe, act, dve

        def t_gu(c, k):
            lo_t, hi_t = 4 * k, min(4 * k + 4, GT)
            c0, c1 = lo_t * P, min(hi_t * P, GW)

            def pe(e, o):
                for t in range(lo_t, hi_t):
                    n = min(P, GW - t * P)
                    last = nc.tensor.transpose(o[:, (t - lo_t) * P:(t - lo_t) * P + n], w_gu[0:n, t, c * P:(c + 1) * P],
                                               ident[0:n, 0:n])
                return last

            def act(e, o):
                return nc.scalar.copy(gu_hi[:, c, c0:c1], o[:, 0:c1 - c0])

            def dve(e, o):
                return nc.vector.tensor_tensor(gu_lo[:, c, c0:c1], o[:, 0:c1 - c0], gu_hi[:, c, c0:c1], ALU.subtract)
            return pe, act, dve

        def t_dn(k):
            tail = k == FT // 2

            def pe(e, o):
                for j in range(2):
                    f = 2 * k + j
                    n = min(P, INTER - f * P)
                    for r in range(CK):
                        last = nc.tensor.transpose(o[0:n, j * DIM + r * P:j * DIM + (r + 1) * P],
                                                   w_dn[:, r * INTER + f * P:r * INTER + f * P + n], ident[:, :])
                return last

            def act(e, o):
                if not tail:
                    return nc.scalar.copy(dn_hi[:, 2 * k:2 * k + 2, :], o[:, :].rearrange("p (f n) -> p f n", f=2))
                nc.scalar.copy(dn_hi[:, 2 * k, :], o[:, 0:DIM])
                nc.scalar.copy(dn_hi[0:TAIL, FT, :], o[0:TAIL, DIM:2 * DIM])
                return nc.scalar.copy(dn_hi[UP0:UP0 + TAIL, FT, :], o[0:TAIL, DIM:2 * DIM])

            def dve(e, o):
                if not tail:
                    return nc.vector.tensor_tensor(dn_lo[:, 2 * k:2 * k + 2, :],
                                                   o[:, :].rearrange("p (f n) -> p f n", f=2),
                                                   dn_hi[:, 2 * k:2 * k + 2, :], ALU.subtract)
                nc.vector.tensor_tensor(dn_lo[:, 2 * k, :], o[:, 0:DIM], dn_hi[:, 2 * k, :], ALU.subtract)
                return nc.vector.tensor_tensor(dn_lo[0:TAIL, FT, :], o[0:TAIL, DIM:2 * DIM],
                                               dn_hi[0:TAIL, FT, :], ALU.subtract)
            return pe, act, dve

        A_TASKS = [((dnat_in, 80), t_down(c)) for c in range(CK)]
        A_TASKS += [((wqu_in, 32), t_nope(p, k)) for p in range(2) for k in range(2)]
        A_TASKS += [((wqr_in, 128), t_rope(p, k)) for p in range(2) for k in range(2)]
        WO_T0 = len(A_TASKS)
        A_TASKS += [((wo_in, 16), t_wo_t(k)) for k in range(HEADS // 2)]
        A_TASKS += [((ssm_in, 64), t_ssm(j)) for j in range(3)]
        VO0 = len(A_TASKS)
        A_TASKS += [((wv_in, 32), t_vo(k)) for k in range(HEADS // 2)]
        gu_sums = (LUT - 1) * (GT * DIM // GC)
        dn_sums = (LUT - 1) * (DN_POOL // GC)
        F_TASKS = [((lut_sum, gu_sums), t_gu(c, k)) for c in range(CK) for k in range(3)]
        F_TASKS += [((lut_sum, gu_sums + dn_sums), t_dn(k)) for k in range(3)]
        NA, NF = len(A_TASKS), len(F_TASKS)

        def pe_tasks(e, tasks, k0):
            for k, (load, (pe, _, _)) in enumerate(tasks, k0):
                if load:
                    e.wait_ge(*load)
                if load and load[0] is wqu_in:
                    e.wait_ge(wkn_in, 16)
                if k == VO0:
                    e.wait_ge(prep_act, VO0)
                    e.wait_ge(prep_dve, VO0)
                if k - 8 >= 0:
                    e.wait_ge(prep_dve, k - 7)
                pe(e, bank[k % 8]).then_inc(prep_mm, 1)

        def act_tasks(e, tasks, k0):
            for k, (_, (_, act, _)) in enumerate(tasks, k0):
                e.wait_ge(prep_mm, k + 1)
                act(e, bank[k % 8]).then_inc(prep_act, 1)

        def dve_tasks(e, tasks, k0, between=None):
            for k, (_, (_, _, dve)) in enumerate(tasks, k0):
                e.wait_ge(prep_act, k + 1)
                dve(e, bank[k % 8]).then_inc(prep_dve, 1)
                if between and k < LUT // 2:
                    between(LUT // 2 + k)

        def settle(k):
            nc.vector.memset(scratch[:, k:k + 1], 0.0)

        RSQRT = 11

        def rsqrt_step(k, sem_, c0, v, r, t):
            e = nc.vector
            e.wait_ge(sem_, c0 + k)
            if k == 0:
                last = e.tensor_scalar(t.bitcast(I32), v.bitcast(I32), 1, None, ALU.logical_shift_right)
            elif k == 1:
                last = e.tensor_scalar(r.bitcast(I32), t.bitcast(I32), -1.0, float(0x5F3759DF), ALU.mult, ALU.add)
            elif k % 3 == 2:
                last = e.tensor_tensor(t, r, r, ALU.mult)
            elif k % 3 == 0:
                last = e.scalar_tensor_tensor(out=t, in0=t, scalar=-0.5, in1=v, op0=ALU.mult, op1=ALU.mult)
            else:
                last = e.scalar_tensor_tensor(out=r, in0=t, scalar=1.5, in1=r, op0=ALU.add, op1=ALU.mult)
            last.then_inc(sem_, 1)

        LN_STEPS = TB + 1 + RSQRT + TB

        def ln_step(k, p, xb):
            e = nc.vector

            def rows(t):
                return x[:, bass.ds(xb * TB + t, 1), :].rearrange("p a d -> p (a d)")
            c0 = (RSQRT + 1) * p + 1
            if k < TB:
                e.bn_stats(stats[:, k, :], rows(k)).then_inc(ln_stats, 1)
            elif k == TB:
                e.wait_ge(ln_stats, p * TB + TB)
                e.wait_ge(ln_norm, p * TB)
                settle(2 * G)
                for t in range(TB):
                    e.bn_aggr(mv[:, t, :], stats[:, t, :]).then_inc(ln_aggr, 1)
                e.wait_ge(ln_aggr, p * TB + TB)
                e.tensor_scalar(ln_v[:, :], mv[:, :, 1], LN_EPS, None, ALU.add).then_inc(ln_ref, 1)
            elif k <= TB + RSQRT:
                rsqrt_step(k - TB - 1, ln_ref, c0, ln_v[:, :], ln_r[:, :], ln_t[:, :])
            elif k < LN_STEPS:
                t = k - TB - 1 - RSQRT
                e.wait_ge(ln_ref, c0 + RSQRT)
                e.wait_ge(xt_mm, 2 * p)
                e.tensor_scalar(xn[:, t, :], rows(t), mv[:, t, 0:1], ln_r[:, t:t + 1],
                                ALU.subtract, ALU.mult).then_inc(ln_norm, 1)

        def dve_ln(p, xb):
            for k in range(LN_STEPS):
                ln_step(k, p, xb)

        def pe_xt(p):
            e = nc.tensor
            e.wait_ge(ln_norm, p * TB + TB)
            e.wait_ge(xt_lo_s, 2 * p)
            for c in range(CK):
                for t in range(TB):
                    last = nc.tensor.transpose(bank[4 + c][:, t * P:(t + 1) * P], xn[:, t, c * P:(c + 1) * P],
                                               ident[:, :])
                last.then_inc(xt_mm, 1)

        def act_xt(p):
            for c in range(CK):
                nc.scalar.wait_ge(xt_mm, 2 * p + c + 1)
                nc.scalar.copy(xt_hi[:, c, :], bank[4 + c][:, :]).then_inc(xt_hi_s, 1)

        def dve_xt(p):
            for c in range(CK):
                nc.vector.wait_ge(xt_hi_s, 2 * p + c + 1)
                nc.vector.tensor_tensor(xt_lo[:, c, :], bank[4 + c][:, :], xt_hi[:, c, :], ALU.subtract)\
                    .then_inc(xt_lo_s, 1)

        def wait_xt(e, p):
            e.wait_ge(xt_hi_s, 2 * p + 2)
            e.wait_ge(xt_lo_s, 2 * p + 2)

        def split_mm(o, pairs, start, stop):
            n = len(pairs)
            for k, (l_hi, l_lo, r_hi, r_lo) in enumerate(pairs):
                nc.tensor.matmul(o, l_hi, r_hi, start=start and k == 0, stop=False)
                nc.tensor.matmul(o, l_hi, r_lo, start=False, stop=False)
                last = nc.tensor.matmul(o, l_lo, r_hi, start=False, stop=stop and k == n - 1)
            return last

        def dve_x_add(layer, b, t, o):
            xr = x[:, bass.ds(b * TB + t, 1), :].rearrange("p a d -> p (a d)")
            nc.vector.tensor_tensor(xr, o[:, 0:DIM], xr, ALU.add).then_inc(x_add[layer], 1)

        def xp_bank(b, m):
            return bank[6 * (b % 2) + m]

        feature_major = ((qa_hi[:, :], bank[0][:, :], qa_lo[:, :], qa_hi[:, :]),
                         (qb_hl[0:QB, :], bank[1][0:QB, :], qb_hl[QB:P, :], qb_hl[0:QB, :]),
                         (kt_hi[:, :], bank[2][:, :], kt_lo[:, :], kt_hi[:, :]))

        primed = {
            "act": [qa_cp, s_exp, dec_s, y_hi_s, ffn[1].silu, ffn[3].silu],
            "dve": [tok, qt_lo_s, o_lo_s, dt_sum, scan_s, y_lo_s, sp_relu, ffn[1].hf, ffn[3].hf, *x_add],
            "pe": [at_mm, so_mm],
        }

        def prime(e, name):
            for s in primed[name]:
                e.sem_inc(s, 1)

        @block.sync
        def _(sp_):
            xr = x_in.rearrange("b (t p) d -> b p t d", p=P)
            outr = out.rearrange("b (t p) d -> b p t d", p=P)
            sp_.dma_start(ident[:, :], c_ident).then_inc(ident_in, 16)
            sp_.dma_start(x[:, 0:TB, :], xr[0]).then_inc(x_in_s[0], 16)
            sp_.dma_start(dn_nat[:, 0, :], wq_down[0:P, :]).then_inc(dnat_in, 16)
            sp_.dma_start(dn_nat[0:QB, 1, :], wq_down[P:QR, :]).then_inc(dnat_in, 16)
            sp_.dma_start(dn_nat[QB:QB + KR, 1, :], wkv_down[:, :]).then_inc(dnat_in, 16)
            wkr = wk_rope.rearrange("(r two) d -> two r d", two=2)
            for two in range(2):
                sp_.dma_start(dn_nat[32 * two:32 * two + 32, 2, :], wkr[two]).then_inc(dnat_in, 16)
            qu = wq_up.rearrange("(h d) q -> d h q", h=HEADS)
            sp_.dma_start(wqu[:, :, 0:QR], qu).then_inc(wqu_in, 16)
            sp_.dma_start(wqu[:, :, QR:QR + QB], qu[:, :, P:QR]).then_inc(wqu_in, 16)
            sp_.dma_start(wo_nat[:, :, :], wo.rearrange("(c p) d -> p c d", p=P)).then_inc(wo_in, 16)
            for b in range(1, BATCH):
                sp_.dma_start(x[:, b * TB:(b + 1) * TB, :], xr[b]).then_inc(x_in_s[b], 16)
            with sp_.Fori(0, BATCH) as b:
                for t in range(TB):
                    sp_.wait_ge(x_add[3], 1 + b * TB + t + 1)
                    sp_.dma_start(outr[bass.ds(b, 1), :, t, :].rearrange("a p d -> (a p) d"),
                                  x[:, bass.ds(b * TB + t, 1), :].rearrange("p a d -> p (a d)")).then_inc(stored, 16)
            sp_.wait_ge(stored, 16 * BATCH * TB)

        @block.gpsimd
        def _(pool):
            pool.dma_start(raw_dn[:, :, :], down_idx.rearrange("(c p) f -> p c f", p=P)).then_inc(dn_in, 16)
            nc.gpsimd.memset(raw_gu[:, GT - 1, :].bitcast(F32), 0.0).then_inc(pads, 1)
            pool.wait_ge(pads, 1)
            for k, src in enumerate((gate_idx, up_idx)):
                pool.dma_start(raw_gu[:, k:2 * FT:2, :],
                               src[0:FT * P, :].rearrange("(t p) d -> p t d", p=P)).then_inc(gu_in, 16)
                pool.dma_start(raw_gu[k * UP0:k * UP0 + TAIL, GT - 1, :], src[FT * P:INTER, :]).then_inc(gu_in, 16)
            pool.dma_start(ssm_nat[:, 0, :, :], w_in.rearrange("(c p) d -> p c d", p=P)).then_inc(ssm_in, 16)
            pool.dma_start(ssm_nat[:, 2, :, :], w_out.rearrange("(c p) d -> p c d", p=P)).then_inc(ssm_in, 16)
            hpc = P // (DIM // 32)
            for c in range(CK):
                pool.dma_start(ssm_nat[:, 1, c, :],
                               w_dt[c * hpc:(c + 1) * hpc, :].unsqueeze(1).to_broadcast([hpc, DIM // 32, DIM]))\
                    .then_inc(ssm_in, 16)
                pool.dma_start(dt_bias[:, c:c + 1],
                               b_dt[c * hpc:(c + 1) * hpc].unsqueeze(1).unsqueeze(2).to_broadcast([hpc, DIM // 32, 1]))\
                    .then_inc(bias_in, 16)
            pool.wait_ge(const_in, 16 * 7)
            pool.wait_ge(idx_ready, 2)
            n_hot = n_sum = 0
            for idx, w_flat in ((idx_gu[:, :, :].rearrange("p t d -> p (t d)"), w_gu[:, :, :].rearrange("p t d -> p (t d)")),
                                (idx_dn[:, :, :].rearrange("p c f -> p (c f)")[:, 0:DN_POOL], w_dn[:, 0:DN_POOL])):
                cols = idx.shape[1]
                for c in range(0, cols, GC):
                    n = min(GC, cols - c)
                    w = w_flat[:, c:c + n]
                    for v in range(LUT):
                        dst = hot[:, 0:n] if v else w
                        nc.gpsimd.tensor_scalar(dst, idx[:, c:c + n], float(v), lut[:, v:v + 1],
                                                ALU.is_equal, ALU.mult).then_inc(lut_hot, 1)
                        n_hot += 1
                        pool.wait_ge(lut_hot, n_hot)
                        if v:
                            nc.gpsimd.tensor_tensor(w, w, hot[:, 0:n], ALU.add).then_inc(lut_sum, 1)
                            n_sum += 1
                            pool.wait_ge(lut_sum, n_sum)

        @block.scalar
        def _(act):
            prime(act, "act")
            kvu = wkv_up.rearrange("(h two d) r -> two d h r", h=HEADS, two=2)
            act.dma_start(wkn[:, :, :], kvu[0]).then_inc(wkn_in, 16)
            act.dma_start(qn_a[:, :], q_norm_w[0:P].unsqueeze(1)).then_inc(const_in, 16)
            for k in range(2):
                act.dma_start(qn_b[k * QB:(k + 1) * QB, :], q_norm_w[P:QR].unsqueeze(1)).then_inc(const_in, 16)
            act.dma_start(lut[:, :], lut_in.unsqueeze(0).to_broadcast([P, LUT])).then_inc(const_in, 16)
            act.dma_start(kvn[:, :], kv_norm_w.unsqueeze(0).to_broadcast([P, KR])).then_inc(const_in, 16)
            for c in range(CK):
                act.dma_start(a_neg[:, c:c + 1], log_a.rearrange("h (e a) -> (h e) a", a=1)[c * P:(c + 1) * P, :])\
                    .then_inc(const_in, 16)
            qrr = wq_rope.rearrange("(g hh r two) q -> hh two r g q", hh=2, two=2, r=ROPE // 2)
            for hh in range(2):
                for two in range(2):
                    rows = slice(64 * hh + 32 * two, 64 * hh + 32 * two + 32)
                    act.dma_start(wqr[rows, :, 0:QR], qrr[hh, two]).then_inc(wqr_in, 16)
                    act.dma_start(wqr[rows, :, QR:QR + QB], qrr[hh, two][:, :, P:QR]).then_inc(wqr_in, 16)
            for k in range(2):
                act.dma_start(wv2[:, :, k, :], kvu[1]).then_inc(wv_in, 16)
            act.dma_start(cos2[:, :, :], c_cos).then_inc(tables_in, 16)
            act.dma_start(sin2[:, :, :], c_sin).then_inc(tables_in, 16)
            act.dma_start(mask[:, :], c_mask).then_inc(tables_in, 16)

            act.wait_ge(consts, 1)
            act_xt(0)
            act.wait_ge(const_in, 16 * 7)
            nc.scalar.activation(a_neg[:, :], a_neg[:, :], ACT.Exp).then_inc(a_exp, 1)
            act_tasks(act, A_TASKS, 0)

            def down_copy(b, t):
                act.wait_ge(dp_mm, b * TB + t + 1)
                if t == 0:
                    act.wait_ge(at_mm, 1 + 3 * b)
                    act.wait_ge(tok, 1 + 14 * b)
                nc.scalar.copy(cd[:, t, :], bank[2 + t % 2][:, 0:DOWN]).then_inc(dp_cp, 1)
                act.wait_ge(dp_cp, b * TB + t + 1)
                for k, (c0, c1) in enumerate(((0, QR), (QR, QR + KR))):
                    nc.scalar.activation(bank[2 + t % 2][:, c0:c1], cd[:, t, c0:c1], ACT.Square,
                                         scale=float(c1 - c0) ** -0.5, accum_out=ms[:, 2 * t + k:2 * t + k + 1])\
                        .then_inc(sq, 1)

            def feature_high(b, k):
                dst, src, _, _ = feature_major[k]
                act.wait_ge(at_mm, 1 + 3 * b + k + 1)
                nc.scalar.copy(dst, src).then_inc(at_hi, 1)

            def exp(b, n, h):
                w = (tile_of(n) + 1) * P
                act.wait_ge(s_max, b * HEADS * TB + G * n + h + 1)
                if h == 0:
                    free_after(act, pt_mm, b * BLOCKS + blocks_before(n - 1))
                nc.scalar.activation(prob[:, n % 2, h, 0:w], bank[2 + h % 2][:, 0:w], ACT.Exp,
                                     bias=bias_m[:, n % 2, h:h + 1], scale=-1.0,
                                     accum_out=den[:, n % 2, h:h + 1]).then_inc(s_exp, 1)

            def q_copy(b, n):
                act.wait_ge(qa_mm, b * UNITS + n + 1)
                free_after(act, qt_mm, b * UNITS + n - 1)
                nc.scalar.mul(q_tok[:, n % 2, :, :].rearrange("p h d -> p (h d)"), bank[0][:, :], -SM_SCALE)\
                    .then_inc(qa_cp, 1)

            def qt_high(b, n):
                act.wait_ge(qt_mm, b * UNITS + n + 1)
                free_after(act, s_mm, b * HEADS * TB + G * (n - 1))
                nc.scalar.copy(qt_hi[:, n % 2, :, :].rearrange("p h d -> p (h d)"), bank[1][:, :])\
                    .then_inc(qt_hi_s, 1)

            def normalise(b, n, h):
                w = (tile_of(n) + 1) * P
                act.wait_ge(recip_s, 2 * (b * UNITS + n) + 1)
                nc.scalar.activation(prob[:, n % 2, h, 0:w], prob[:, n % 2, h, 0:w], ACT.Copy,
                                     scale=rden[:, n % 2, h:h + 1]).then_inc(norm_a, 1)

            def pt_high(b, n, j):
                if j > tile_of(n):
                    return
                c = blocks_before(n) + j
                act.wait_ge(pt_mm, b * BLOCKS + c + 1)
                free_after(act, pv_mm, b * BLOCKS + c - 1)
                nc.scalar.copy(pt_hi[:, c % 2, :, :].rearrange("p h d -> p (h d)"), bank[4 + c % 2][:, :])\
                    .then_inc(pt_hi_s, 1)

            def out_high(b, n):
                act.wait_ge(pv_mm, b * BLOCKS + blocks_before(n + 1))
                free_after(act, y_mm, b * UNITS + n - 1)
                nc.scalar.copy(o_a[:, n % 2, :, :].rearrange("p h d -> p (h d)"), bank[6][:, :])\
                    .then_inc(o_hi_s, 1)
                nc.scalar.copy(o_b[0:KR, n % 2, :, :].rearrange("p h d -> p (h d)"), bank[6][0:KR, :])\
                    .then_inc(o_hi_s, 1)

            def act_slot(s, b, nb):
                def do(step, n, *k):
                    step_of(b, nb, step, n, *k)

                do(normalise, s - 4, 1)
                do(exp, s - 3, 0)
                do(pt_high, s - 5, 3)
                do(qt_high, s - 2)
                do(exp, s - 3, 1)
                do(pt_high, s - 4, 0)
                do(out_high, s - 5)
                do(exp, s - 3, 2)
                do(pt_high, s - 4, 1)
                do(exp, s - 3, 3)
                if nb is not None and s in (8, 9):
                    down_copy(nb, 2 * (s - 8))
                    down_copy(nb, 2 * (s - 8) + 1)
                if nb is not None and s == 18:
                    feature_high(nb, 2)
                do(q_copy, s)
                if nb is not None and s == 10:
                    act_xt(nb + 1)
                if nb is not None and s == 15:
                    feature_high(nb, 0)
                    feature_high(nb, 1)
                do(normalise, s - 3, 0)
                do(pt_high, s - 4, 2)

            for t in range(TB):
                down_copy(0, t)
            act_xt(1)
            for k in range(3):
                feature_high(0, k)
            for s in range(LEAD):
                act_slot(s, 0, None)
            with act.Fori(0, BATCH - 1) as b:
                for s in range(LEAD, UNITS + LEAD):
                    act_slot(s, b, b + 1)
            for s in range(LEAD, UNITS + DEPTH):
                act_slot(s, BATCH - 1, None)

            act.wait_ge(pads, 3)
            act_tasks(act, F_TASKS, NA)

            def ffn_act(layer):
                f = ffn[layer]
                n_gu = 2 * FT + 1
                with act.Fori(0, BATCH) as b:

                    def gate(m):
                        act.wait_ge(f.gu_mm, b * n_gu + 2 * m + 1)
                        if m >= 2:
                            act.wait_ge(f.hf, 1 + b * (FT + 1) + m - 1)
                        if m < FT:
                            nc.scalar.activation(silu[:, m % 2, :], bank[m % 2][:, :], ACT.Silu).then_inc(f.silu, 1)
                        else:
                            nc.scalar.activation(silu[UP0:UP0 + TAIL, m % 2, :], bank[m % 2][0:TAIL, :], ACT.Silu)\
                                .then_inc(f.silu, 1)

                    def high(m):
                        act.wait_ge(f.hf, 1 + b * (FT + 1) + m + 1)
                        rows = P if m < FT else TAIL
                        nc.scalar.copy(h_hi[0:rows, m, :], h_f[0:rows, m % 2, :]).then_inc(f.hhi, 1)

                    gate(0)
                    for m in range(FT + 1):
                        if m < FT:
                            gate(m + 1)
                        high(m)
                    act_xt(BATCH * layer + b + 1)

            ffn_act(1)

            act.wait_ge(bias_in, 16 * CK)

            def decays(b):
                act.wait_ge(scan_s, 1 + CK * b)
                for m in range(CK):
                    act.wait_ge(dt_sum, 1 + CK * b + m + 1)
                    nc.scalar.activation(decay[:, m, :], dts[:, m, :], ACT.Exp, scale=a_neg[:, m:m + 1])\
                        .then_inc(dec_s, 1)

            def xp_high(b):
                for m in range(CK):
                    act.wait_ge(xp_mm, CK * b + m + 1)
                    nc.scalar.copy(xp_hi[:, m, :], xp_bank(b, m)[:, :]).then_inc(xp_hi_s, 1)

            def dt_abs(b):
                for m in range(CK):
                    act.wait_ge(dt_mm, CK * b + m + 1)
                    act.wait_ge(dt_sum, 1 + CK * b)
                    nc.scalar.activation(sp[:, m, :], bank[2 + m][:, :], ACT.Abs, bias=dt_bias[:, m:m + 1])\
                        .then_inc(sp_act, 1)

            def dt_log(b):
                act.wait_ge(sp_act, 4 * b + 2)
                nc.scalar.activation(sp[:, :, :], sp[:, :, :], ACT.Exp, scale=-1.0).then_inc(sp_act, 1)
                act.wait_ge(sp_act, 4 * b + 3)
                nc.scalar.activation(sp[:, :, :], sp[:, :, :], ACT.Ln, bias=one[:, 0:1]).then_inc(sp_act, 1)

            def y_high(b):
                for m in range(CK):
                    act.wait_ge(scan_s, 1 + CK * b + m + 1)
                    act.wait_ge(so_mm, 1 + TB * b)
                    nc.scalar.copy(y_hi[:, m, :], ys[:, m, :]).then_inc(y_hi_s, 1)

            for b in range(BATCH + 1):
                if b:
                    decays(b - 1)
                if b < BATCH:
                    xp_high(b)
                    dt_abs(b)
                if b:
                    y_high(b - 1)
                if b < BATCH:
                    act_xt(BATCH * 2 + b + 1)
                    dt_log(b)

            ffn_act(3)

        @block.vector
        def _(dve):
            prime(dve, "dve")
            nc.vector.memset(one[:, :], 1.0).then_inc(consts, 1)
            dve.wait_ge(x_in_s[0], 16)
            dve_ln(0, 0)
            dve_xt(0)
            dve.wait_ge(gu_in, 64)
            nc.vector.tensor_copy(idx_gu[:, :, :], raw_gu[:, :, :]).then_inc(idx_ready, 1)
            dve.wait_ge(dn_in, 16)
            nc.vector.tensor_copy(idx_dn[:, :, :], raw_dn[:, :, :]).then_inc(idx_ready, 1)
            dve.wait_ge(a_exp, 1)
            nc.vector.tensor_scalar(a_neg[:, :], a_neg[:, :], -1.0, None, ALU.mult).then_inc(a_ready, 1)
            idx_rest = idx_dn[:, :, :].rearrange("p c f -> p (c f)")[:, DN_POOL:CK * INTER]
            w_rest = w_dn[:, DN_POOL:CK * INTER]

            def lookup(v):
                if v == 0:
                    dve.wait_ge(idx_ready, 2)
                if v > 1:
                    dve.wait_ge(dlut_sum, v - 1)
                nc.vector.tensor_scalar(hot_dn[:, :] if v else w_rest, idx_rest, float(v), lut[:, v:v + 1],
                                        ALU.is_equal, ALU.mult).then_inc(dlut_hot, 1)
                if v:
                    dve.wait_ge(dlut_hot, v + 1)
                    nc.vector.tensor_tensor(w_rest, w_rest, hot_dn[:, :], ALU.add).then_inc(dlut_sum, 1)

            for v in range(LUT // 2):
                lookup(v)
            dve_tasks(dve, A_TASKS, 0, lookup)
            dve.wait_ge(tables_in, 16 * 3)
            for b in range(1, BATCH):
                dve.wait_ge(x_in_s[b], 16)

            half = ROPE // 2

            TOKEN_STEPS = 1 + RSQRT + 2 * TB + 4

            def token_step(k, b):
                kr = cd[:, :, QR + KR:DOWN]
                c0 = (RSQRT + 1) * b + 1
                n = k - 1 - RSQRT
                if k == 0:
                    dve.wait_ge(sq, (b + 1) * 2 * TB)
                    nc.vector.tensor_scalar(rms_v[:, :], ms[:, :], RMS_EPS, None, ALU.add).then_inc(rms_ref, 1)
                elif n < 0:
                    rsqrt_step(k - 1, rms_ref, c0, rms_v[:, :], rms_r[:, :], rms_t[:, :])
                elif n < TB:
                    dve.wait_ge(rms_ref, c0 + RSQRT)
                    nc.vector.tensor_scalar(cd[:, n, 0:QR], cd[:, n, 0:QR], rms_r[:, 2 * n:2 * n + 1], None, ALU.mult)\
                        .then_inc(tok, 1)
                elif n < 2 * TB:
                    t = n - TB
                    nc.vector.scalar_tensor_tensor(out=cd[:, t, QR:QR + KR], in0=cd[:, t, QR:QR + KR],
                                                   scalar=rms_r[:, 2 * t + 1:2 * t + 2], in1=kvn[:, :],
                                                   op0=ALU.mult, op1=ALU.mult).then_inc(tok, 1)
                elif n < 2 * TB + 2:
                    a = slice(0, half) if n == 2 * TB else slice(half, ROPE)
                    o = slice(half, ROPE) if n == 2 * TB else slice(0, half)
                    nc.vector.tensor_tensor(k_rot[:, :, a], kr[:, :, o], sin2[:, :, a], ALU.mult).then_inc(tok, 1)
                elif n == 2 * TB + 2:
                    dve.wait_ge(tok, 1 + 14 * b + 10)
                    nc.vector.tensor_tensor(kr, kr, cos2[:, :, :], ALU.mult).then_inc(tok, 1)
                elif n == 2 * TB + 3:
                    dve.wait_ge(tok, 1 + 14 * b + 11)
                    nc.vector.tensor_tensor(kr, kr, k_rot[:, :, :], ALU.add).then_inc(tok, 1)

            def split_values(b):
                kv = cd[:, :, QR:QR + KR]
                nc.vector.tensor_copy(v_hl[:, :, 0, :], kv).then_inc(tok, 1)
                dve.wait_ge(tok, 1 + 14 * b + 13)
                nc.vector.tensor_tensor(v_hl[:, :, 1, :], kv, v_hl[:, :, 0, :], ALU.subtract).then_inc(tok, 1)

            def feature_low(b, k):
                dst_hi, src, dst, hi = feature_major[k]
                dve.wait_ge(at_hi, 3 * b + k + 1)
                nc.vector.tensor_tensor(dst, src, hi, ALU.subtract).then_inc(at_lo, 1)

            def row_max(b, n, h):
                w = (tile_of(n) + 1) * P
                dve.wait_ge(s_mm, b * HEADS * TB + G * n + h + 1)
                free_after(dve, s_exp, 1 + b * HEADS * TB + G * (n - 2) + h + 1)
                settle(n % 2 * G + h)
                nc.vector.tensor_tensor_reduce(out=bank[2 + h % 2][:, 0:w], in0=bank[2 + h % 2][:, 0:w],
                                               in1=mask[:, TB * P - w:TB * P], scale=1.0, scalar=3e38,
                                               op0=ALU.add, op1=ALU.min,
                                               accum_out=bias_m[:, n % 2, h:h + 1]).then_inc(s_max, 1)

            def rope_q(b, n):
                i = tile_of(n)
                q = q_tok[:, n % 2, :, ROPE:2 * ROPE]
                cs = cos2[:, i:i + 1, :].to_broadcast([P, G, ROPE])
                s0 = sin2[:, i:i + 1, 0:half].to_broadcast([P, G, half])
                s1 = sin2[:, i:i + 1, half:ROPE].to_broadcast([P, G, half])
                k = b * 4 * UNITS + 4 * n
                dve.wait_ge(qa_cp, 1 + b * UNITS + n + 1)
                free_after(dve, q_rope, k)
                nc.vector.tensor_tensor(q_rot[:, :, 0:half], q[:, :, half:ROPE], s0, ALU.mult).then_inc(q_rope, 1)
                nc.vector.tensor_tensor(q_rot[:, :, half:ROPE], q[:, :, 0:half], s1, ALU.mult).then_inc(q_rope, 1)
                dve.wait_ge(q_rope, k + 2)
                nc.vector.tensor_tensor(q, q, cs, ALU.mult).then_inc(q_rope, 1)
                dve.wait_ge(q_rope, k + 3)
                nc.vector.tensor_tensor(q, q, q_rot[:, :, :], ALU.add).then_inc(q_rope, 1)

            def qt_low(b, n):
                dve.wait_ge(qt_hi_s, b * UNITS + n + 1)
                free_after(dve, s_mm, b * HEADS * TB + G * (n - 1))
                nc.vector.tensor_tensor(qt_lo[:, n % 2, :, :].rearrange("p h d -> p (h d)"), bank[1][:, :],
                                        qt_hi[:, n % 2, :, :].rearrange("p h d -> p (h d)"), ALU.subtract)\
                    .then_inc(qt_lo_s, 1)

            def recip(b, n, k):
                dve.wait_ge(s_exp, 1 + b * HEADS * TB + G * n + 2 * k + 2)
                free_after(dve, (norm_a, norm_d)[k], b * 2 * UNITS + 2 * (n - 1))
                nc.vector.reciprocal(rden[:, n % 2, 2 * k:2 * k + 2], den[:, n % 2, 2 * k:2 * k + 2])\
                    .then_inc(recip_s, 1)

            def normalise(b, n, h):
                w = (tile_of(n) + 1) * P
                dve.wait_ge(recip_s, 2 * (b * UNITS + n) + 2)
                nc.vector.tensor_scalar(prob[:, n % 2, h, 0:w], prob[:, n % 2, h, 0:w],
                                        rden[:, n % 2, h:h + 1], None, ALU.mult).then_inc(norm_d, 1)

            def pt_low(b, n, j):
                if j > tile_of(n):
                    return
                c = blocks_before(n) + j
                dve.wait_ge(pt_hi_s, b * BLOCKS + c + 1)
                free_after(dve, pv_mm, b * BLOCKS + c - 1)
                nc.vector.tensor_tensor(pt_lo[:, c % 2, :, :].rearrange("p h d -> p (h d)"), bank[4 + c % 2][:, :],
                                        pt_hi[:, c % 2, :, :].rearrange("p h d -> p (h d)"), ALU.subtract)\
                    .then_inc(pt_lo_s, 1)

            def out_low(b, n):
                dve.wait_ge(o_hi_s, 2 * (b * UNITS + n) + 2)
                nc.vector.tensor_tensor(o_b[KR:P, n % 2, :, :].rearrange("p h d -> p (h d)"), bank[6][0:KR, :],
                                        o_a[0:KR, n % 2, :, :].rearrange("p h d -> p (h d)"), ALU.subtract)\
                    .then_inc(o_lo_s, 1)

            def add_output(b, n):
                if n % (HEADS // G) == HEADS // G - 1:
                    dve.wait_ge(y_mm, b * UNITS + n + 1)
                    dve_x_add(0, b, tile_of(n), bank[7])

            def dve_slot(s, b, nb):
                def do(step, n, *k):
                    step_of(b, nb, step, n, *k)

                def between(k):
                    if nb is None:
                        return
                    if s in (8, 9):
                        if s == 8 and k == 0:
                            dve.wait_ge(x_add[0], 1 + b * TB)
                        ln_step(GAPS * (s - 8) + k, nb + 1, (nb + 1) % BATCH)
                    if s in (10, 11):
                        token_step(GAPS * (s - 10) + k, nb)

                do(recip, s - 3, 0)
                between(0)
                do(pt_low, s - 4, 1)
                between(1)
                do(add_output, s - 6)
                between(2)
                do(recip, s - 3, 1)
                between(3)
                if nb is not None and s == 18:
                    feature_low(nb, 2)
                do(row_max, s - 2, 0)
                between(4)
                do(normalise, s - 3, 2)
                between(5)
                do(normalise, s - 3, 3)
                between(6)
                if nb is not None and s == 15:
                    feature_low(nb, 0)
                    feature_low(nb, 1)
                do(pt_low, s - 4, 2)
                between(7)
                do(row_max, s - 2, 1)
                between(8)
                if nb is not None and s == 10:
                    dve_xt(nb + 1)
                do(pt_low, s - 4, 3)
                between(9)
                do(rope_q, s)
                between(10)
                do(qt_low, s - 1)
                between(11)
                do(row_max, s - 2, 2)
                between(12)
                do(pt_low, s - 3, 0)
                do(row_max, s - 2, 3)
                do(out_low, s - 4)
                if nb is not None and s == 19:
                    split_values(nb)

            dve_ln(1, 1)
            for k in range(TOKEN_STEPS):
                token_step(k, 0)
            split_values(0)
            dve_xt(1)
            for k in range(3):
                feature_low(0, k)
            for s in range(LEAD):
                dve_slot(s, 0, None)
            with dve.Fori(0, BATCH - 1) as b:
                for s in range(LEAD, UNITS + LEAD):
                    dve_slot(s, b, b + 1)
            for s in range(LEAD, UNITS + DEPTH):
                dve_slot(s, BATCH - 1, None)

            dve.wait_ge(y_mm, BATCH * UNITS)
            nc.vector.memset(h_hi[32:64, FT, :].bitcast(F32), 0.0).then_inc(pads, 1)
            nc.vector.memset(dn_hi[32:64, FT, :].bitcast(F32), 0.0).then_inc(pads, 1)
            dve_tasks(dve, F_TASKS, NA)

            def ffn_dve(layer):
                f = ffn[layer]
                n_gu = 2 * FT + 1
                dve.wait_ge(x_add[layer - 1], 1 + BATCH * TB)
                with dve.Fori(0, BATCH) as b:
                    dve.wait_ge(x_add[layer], 1 + b * TB)

                    def norm(place):
                        for k in range(3 * place, 3 * place + 3):
                            ln_step(k, BATCH * layer + b + 1, (b + 1) % BATCH)

                    for m in range(FT + 1):
                        k = b * (FT + 1) + m
                        dve.wait_ge(f.silu, 1 + k + 1)
                        if m < FT:
                            dve.wait_ge(f.gu_mm, b * n_gu + 2 * m + 2)
                        if m >= 2:
                            dve.wait_ge(f.hlo, k - 1)
                        if m < FT:
                            nc.vector.tensor_tensor(h_f[:, m % 2, :], bank[2 + m % 2][:, :], silu[:, m % 2, :],
                                                    ALU.mult).then_inc(f.hf, 1)
                        else:
                            nc.vector.tensor_tensor(h_f[0:TAIL, m % 2, :], bank[m % 2][UP0:UP0 + TAIL, :],
                                                    silu[UP0:UP0 + TAIL, m % 2, :], ALU.mult).then_inc(f.hf, 1)
                        norm(2 * m)
                        dve.wait_ge(f.hhi, k + 1)
                        if m < FT:
                            nc.vector.tensor_tensor(h_lo[:, m, :], h_f[:, m % 2, :], h_hi[:, m, :],
                                                    ALU.subtract).then_inc(f.hlo, 1)
                        else:
                            nc.vector.tensor_tensor(h_hi[UP0:UP0 + TAIL, m, :], h_f[0:TAIL, m % 2, :],
                                                    h_hi[0:TAIL, m, :], ALU.subtract).then_inc(f.hlo, 1)
                        norm(2 * m + 1)
                    dve_xt(BATCH * layer + b + 1)
                    for t in range(TB):
                        dve.wait_ge(f.dn_mm, b * TB + t + 1)
                        dve_x_add(layer, b, t, bank[6 + t % 2])

            ffn_dve(1)

            dve.wait_ge(x_add[1], 1 + BATCH * TB)
            dve.wait_ge(a_ready, 1)
            dve.wait_ge(bias_in, 16 * CK)

            def softplus_sum(b):
                dve.wait_ge(sp_act, 4 * b + 4)
                dve.wait_ge(sp_relu, 1 + CK * b + 2)
                for m in range(CK):
                    nc.vector.tensor_tensor(dts[:, m, :], dts[:, m, :], sp[:, m, :], ALU.add).then_inc(dt_sum, 1)

            def xp_low(b):
                for m in range(CK):
                    dve.wait_ge(xp_hi_s, CK * b + m + 1)
                    nc.vector.tensor_tensor(xp_lo[:, m, :], xp_bank(b, m)[:, :], xp_hi[:, m, :], ALU.subtract)\
                        .then_inc(xp_lo_s, 1)

            def scan(b):
                dve.wait_ge(y_hi_s, 1 + CK * b)
                dve.wait_ge(y_lo_s, 1 + CK * b)
                for m in range(CK):
                    dve.wait_ge(dec_s, 1 + CK * b + m + 1)
                    nc.vector.tensor_tensor_scan(ys[:, m, :], decay[:, m, :], xp_bank(b, m)[:, :], 0.0,
                                                 ALU.mult, ALU.add).then_inc(scan_s, 1)

            def dt_relu(b):
                for m in range(CK):
                    dve.wait_ge(sp_act, 4 * b + m + 1)
                    if m == 0:
                        dve.wait_ge(dec_s, 1 + CK * b)
                    nc.vector.tensor_scalar(dts[:, m, :], bank[2 + m][:, :], dt_bias[:, m:m + 1], 0.0,
                                            ALU.add, ALU.max).then_inc(sp_relu, 1)

            def y_low(b):
                for m in range(CK):
                    dve.wait_ge(y_hi_s, 1 + CK * b + m + 1)
                    nc.vector.tensor_tensor(y_lo[:, m, :], ys[:, m, :], y_hi[:, m, :], ALU.subtract)\
                        .then_inc(y_lo_s, 1)

            def norm(b, k0, k1):
                if b < BATCH:
                    if b >= 2 and k0 == 0:
                        dve.wait_ge(x_add[2], 1 + (b - 1) * TB)
                    for k in range(k0, k1):
                        ln_step(k, BATCH * 2 + b + 1, (b + 1) % BATCH)

            for b in range(BATCH + 1):
                if b:
                    softplus_sum(b - 1)
                norm(b, 0, TB + 1)
                if b < BATCH:
                    xp_low(b)
                norm(b, TB + 1, TB + 6)
                if b:
                    scan(b - 1)
                norm(b, TB + 6, LN_STEPS)
                if b < BATCH:
                    dt_relu(b)
                if b:
                    y_low(b - 1)
                if b < BATCH:
                    dve_xt(BATCH * 2 + b + 1)
                if b:
                    for t in range(TB):
                        dve.wait_ge(so_mm, 1 + TB * (b - 1) + t + 1)
                        dve_x_add(2, b - 1, t, xp_bank(b - 1, t % 2))

            ffn_dve(3)

        @block.tensor
        def _(pe):
            prime(pe, "pe")
            pe.wait_ge(ident_in, 16)
            pe_xt(0)
            wait_xt(pe, 0)
            pe_tasks(pe, A_TASKS, 0)
            pe.wait_ge(prep_act, NA)
            pe.wait_ge(prep_dve, NA)

            def down(b, t):
                tt = slice(t * P, (t + 1) * P)
                split_mm(bank[2 + t % 2][:, 0:DOWN],
                         [(xt_hi[:, c, tt], xt_lo[:, c, tt], down_hi[:, c, :], down_lo[:, c, :])
                          for c in range(CK)], True, True).then_inc(dp_mm, 1)

            def to_features(b, k):
                _, o, _, _ = feature_major[k]
                c0, c1 = ((0, P), (P, QR), (QR, DOWN))[k]
                for t in range(TB):
                    last = nc.tensor.transpose(o[:, t * P:(t + 1) * P], cd[:, t, c0:c1], ident[:, :])
                last.then_inc(at_mm, 1)

            def q_up(b, n):
                tt = slice(tile_of(n) * P, (tile_of(n) + 1) * P)
                g = n % (HEADS // G)

                def w(m, rows=P):
                    return m[0:rows, g * G:(g + 1) * G, :, :].rearrange("p h a r -> p (h a r)")
                pe.wait_ge(qa_cp, 1 + b * UNITS + n)
                if n == 0:
                    pe.wait_ge(at_hi, 3 * b + 2)
                    pe.wait_ge(at_lo, 3 * b + 2)
                o = bank[0][:, :]
                nc.tensor.matmul(o, qa_hi[:, tt], w(wa_hi), start=True, stop=False)
                nc.tensor.matmul(o, qa_hi[:, tt], w(wa_lo), start=False, stop=False)
                nc.tensor.matmul(o, qa_lo[:, tt], w(wa_hi), start=False, stop=False)
                nc.tensor.matmul(o, qb_hl[:, tt], w(wb_hi), start=False, stop=False)
                nc.tensor.matmul(o, qb_hl[0:QB, tt], w(wb_lo, QB), start=False, stop=True).then_inc(qa_mm, 1)

            def q_transpose(b, n):
                pe.wait_ge(q_rope, 4 * (b * UNITS + n + 1))
                pe.wait_ge(qt_lo_s, 1 + b * UNITS + n)
                for h in range(G):
                    last = nc.tensor.transpose(bank[1][:, h * P:(h + 1) * P], q_tok[:, n % 2, h, :], ident[:, :])
                last.then_inc(qt_mm, 1)

            def scores(b, n, h):
                w = (tile_of(n) + 1) * P
                if h == 0:
                    pe.wait_ge(qt_hi_s, b * UNITS + n + 1)
                    pe.wait_ge(qt_lo_s, 1 + b * UNITS + n + 1)
                if h == 0 and n == 0:
                    pe.wait_ge(at_hi, 3 * b + 3)
                    pe.wait_ge(at_lo, 3 * b + 3)
                free_after(pe, s_exp, 1 + b * HEADS * TB + G * n + h - 1)
                split_mm(bank[2 + h % 2][:, 0:w],
                         [(qt_hi[:, n % 2, h, :], qt_lo[:, n % 2, h, :], kt_hi[:, 0:w], kt_lo[:, 0:w])],
                         True, True).then_inc(s_mm, 1)

            def p_transpose(b, n, j):
                if j > tile_of(n):
                    return
                c = blocks_before(n) + j
                if j == 0:
                    pe.wait_ge(norm_a, b * 2 * UNITS + 2 * n + 2)
                    pe.wait_ge(norm_d, b * 2 * UNITS + 2 * n + 2)
                free_after(pe, pt_lo_s, b * BLOCKS + c - 1)
                for h in range(G):
                    last = nc.tensor.transpose(bank[4 + c % 2][:, h * P:(h + 1) * P],
                                               prob[:, n % 2, h, j * P:(j + 1) * P], ident[:, :])
                last.then_inc(pt_mm, 1)

            def values(b, n, j):
                if j > tile_of(n):
                    return
                c = blocks_before(n) + j
                if j == 0:
                    pe.wait_ge(o_lo_s, 1 + b * UNITS + n)
                if j == 0 and n == 0:
                    pe.wait_ge(tok, 1 + 14 * b + 14)
                v = v_hl[:, j, :, :].rearrange("p a r -> p (a r)")
                pe.wait_ge(pt_hi_s, b * BLOCKS + c + 1)
                nc.tensor.matmul(bank[6][:, :], v, pt_hi[:, c % 2, :, :].rearrange("p h d -> p (h d)"),
                                 start=j == 0, stop=False)
                pe.wait_ge(pt_lo_s, b * BLOCKS + c + 1)
                nc.tensor.matmul(bank[6][:, :], v, pt_lo[:, c % 2, :, :].rearrange("p h d -> p (h d)"),
                                 start=False, stop=j == tile_of(n)).then_inc(pv_mm, 1)

            def project(b, n):
                g = n % (HEADS // G)
                pe.wait_ge(o_hi_s, 2 * (b * UNITS + n) + 2)
                pe.wait_ge(o_lo_s, 1 + b * UNITS + n + 1)
                if g == 0:
                    pe.wait_ge(x_add[0], 1 + b * TB + tile_of(n))
                for h in range(G):
                    nc.tensor.matmul(bank[7][:, 0:DIM], o_a[:, n % 2, h, :], wo_a[:, g * G + h, :],
                                     start=g == 0 and h == 0, stop=False)
                    last = nc.tensor.matmul(bank[7][:, 0:DIM], o_b[:, n % 2, h, :], wo_b[:, g * G + h, :],
                                            start=False, stop=g == HEADS // G - 1 and h == G - 1)
                last.then_inc(y_mm, 1)

            def pe_slot(s, b, nb):
                def do(step, n, *k):
                    step_of(b, nb, step, n, *k)

                do(values, s - 5, 0)
                do(p_transpose, s - 5, 3)
                if nb is not None and s in (9, 10):
                    pe.wait_ge(sq, 2 * nb * TB + 4 * (s - 8))
                do(scores, s - 3, 1)
                do(values, s - 5, 1)
                if nb is not None and s == 16:
                    pe.wait_ge(at_lo, 3 * nb + 2)
                do(q_transpose, s - 2)
                if nb is not None and s == 11:
                    pe.wait_ge(xt_lo_s, 2 * nb + 4)
                do(p_transpose, s - 4, 0)
                do(values, s - 5, 2)
                do(scores, s - 3, 2)
                do(values, s - 5, 3)
                do(q_up, s)
                do(scores, s - 3, 3)
                do(p_transpose, s - 4, 1)
                do(project, s - 6)
                do(p_transpose, s - 4, 2)
                if nb is not None and s in (8, 9):
                    wait_xt(pe, nb)
                    for k in range(2):
                        pe.wait_ge(s_exp, 1 + b * HEADS * TB + G * (s - 2) + k - 1)
                        down(nb, 2 * (s - 8) + k)
                    pe.wait_ge(sq, 2 * nb * TB + 4 * (s - 8) + 2)
                if nb is not None and s == 18:
                    pe.wait_ge(s_exp, 1 + b * HEADS * TB + G * UNITS - 1)
                    to_features(nb, 2)
                do(scores, s - 2, 0)
                if nb is not None and s == 10:
                    pe.wait_ge(pt_lo_s, b * BLOCKS + blocks_before(s - 3))
                    pe_xt(nb + 1)
                if nb is not None and s == 15:
                    pe.wait_ge(tok, 1 + 14 * nb + 12)
                    pe.wait_ge(qt_lo_s, 1 + b * UNITS + UNITS - 2)
                    pe.wait_ge(qa_cp, 1 + b * UNITS + UNITS)
                    to_features(nb, 0)
                    to_features(nb, 1)

            wait_xt(pe, 0)
            for t in range(TB):
                if t >= 2:
                    pe.wait_ge(sq, 2 * (t - 1))
                down(0, t)
            pe_xt(1)
            pe.wait_ge(sq, 2 * TB)
            pe.wait_ge(tok, 1 + 12)
            for k in range(3):
                to_features(0, k)
            wait_xt(pe, 1)
            for s in range(LEAD):
                pe_slot(s, 0, None)
            with pe.Fori(0, BATCH - 1) as b:
                for s in range(LEAD, UNITS + LEAD):
                    pe_slot(s, b, b + 1)
            for s in range(LEAD, UNITS + DEPTH):
                pe_slot(s, BATCH - 1, None)

            pe.wait_ge(x_add[0], 1 + BATCH * TB)
            pe.wait_ge(dlut_sum, LUT - 1)
            pe_tasks(pe, F_TASKS, NA)
            pe.wait_ge(prep_act, NA + NF)
            pe.wait_ge(prep_dve, NA + NF)

            def ffn_pe(layer):
                f = ffn[layer]
                with pe.Fori(0, BATCH) as b:
                    wait_xt(pe, BATCH * layer + b)

                    def up(o, c0, cols):
                        pairs = [(gu_hi[:, c, c0:c0 + cols], gu_lo[:, c, c0:c0 + cols], xt_hi[:, c, :], xt_lo[:, c, :])
                                 for c in range(CK)]
                        split_mm(o[0:cols, :], pairs, True, True).then_inc(f.gu_mm, 1)

                    for m in range(FT + 1):
                        k = b * (FT + 1) + m
                        pe.wait_ge(f.silu, (k if m >= 2 else b * (FT + 1) + 1))
                        pe.wait_ge(f.hf, (k if m >= 2 else b * (FT + 1) + 1))
                        if m < FT:
                            up(bank[m % 2], 2 * m * P, P)
                            up(bank[2 + m % 2], (2 * m + 1) * P, P)
                        else:
                            up(bank[m % 2], 2 * m * P, UP0 + TAIL)
                    pe_xt(BATCH * layer + b + 1)
                    for pair in range(0, TB, 2):
                        for t in (pair, pair + 1):
                            pe.wait_ge(x_add[layer], 1 + b * TB + (t - 1 if t >= 2 else 0))
                            tt = slice(t * P, (t + 1) * P)
                            for m in range(FT):
                                pe.wait_ge(f.hlo, b * (FT + 1) + m + 1)
                                split_mm(bank[6 + t % 2][:, 0:DIM],
                                         [(h_hi[:, m, tt], h_lo[:, m, tt], dn_hi[:, m, :], dn_lo[:, m, :])],
                                         m == 0, False)
                        pe.wait_ge(f.hlo, b * (FT + 1) + FT + 1)
                        for t in (pair, pair + 1):
                            tt = slice(t * P, (t + 1) * P)
                            o = bank[6 + t % 2][:, 0:DIM]
                            nc.tensor.matmul(o, h_hi[0:UP0 + TAIL, FT, tt], dn_hi[0:UP0 + TAIL, FT, :],
                                             start=False, stop=False)
                            nc.tensor.matmul(o, h_hi[0:TAIL, FT, tt], dn_lo[0:TAIL, FT, :],
                                             start=False, stop=True).then_inc(f.dn_mm, 1)

            ffn_pe(1)

            pe.wait_ge(x_add[1], 1 + BATCH * TB)

            def input_projection(b):
                wait_xt(pe, BATCH * 2 + b)
                if b >= 2:
                    pe.wait_ge(x_add[2], 1 + (b - 1) * TB)
                for m in range(CK):
                    mm = slice(m * P, (m + 1) * P)
                    split_mm(xp_bank(b, m)[:, :],
                             [(ssm_hi[:, 0, c, mm], ssm_lo[:, 0, c, mm], xt_hi[:, c, :], xt_lo[:, c, :])
                              for c in range(CK)], True, True).then_inc(xp_mm, 1)

            def dt_projection(b):
                pe.wait_ge(xp_hi_s, CK * b + 2)
                pe.wait_ge(xp_lo_s, CK * b + 2)
                pe.wait_ge(sp_relu, 1 + CK * b)
                for m in range(CK):
                    mm = slice(m * P, (m + 1) * P)
                    split_mm(bank[2 + m][:, :],
                             [(ssm_hi[:, 1, c, mm], ssm_lo[:, 1, c, mm], xp_hi[:, c, :], xp_lo[:, c, :])
                              for c in range(CK)], True, True).then_inc(dt_mm, 1)

            def output_projection(b):
                pe.wait_ge(y_hi_s, 1 + CK * b + 2)
                pe.wait_ge(y_lo_s, 1 + CK * b + 2)
                for t in range(TB):
                    if t >= 2:
                        pe.wait_ge(x_add[2], 1 + b * TB + t - 1)
                    tt = slice(t * P, (t + 1) * P)
                    split_mm(xp_bank(b, t % 2)[:, 0:DIM],
                             [(y_hi[:, c, tt], y_lo[:, c, tt], ssm_hi[:, 2, c, :], ssm_lo[:, 2, c, :])
                              for c in range(CK)], True, True).then_inc(so_mm, 1)

            for b in range(BATCH + 1):
                if b < BATCH:
                    input_projection(b)
                    dt_projection(b)
                    pe_xt(BATCH * 2 + b + 1)
                if b:
                    output_projection(b - 1)
            pe.wait_ge(x_add[2], 1 + BATCH * TB)
            ffn_pe(3)


_INS = ['L0_attn_a_x', 'L0_attn_a_wq_down', 'L0_attn_a_wq_up', 'L0_attn_a_wq_rope', 'L0_attn_a_q_norm_w',
        'L0_attn_a_wkv_down', 'L0_attn_a_kv_norm_w', 'L0_attn_a_wkv_up', 'L0_attn_a_wk_rope', 'L0_attn_a_wo',
        'L0_attn_b_W_in', 'L0_attn_b_W_out', 'L0_attn_b_log_A', 'L0_attn_b_W_dt', 'L0_attn_b_b_dt',
        'L0_ffn_lut', 'L0_ffn_gate_idx', 'L0_ffn_up_idx', 'L0_ffn_down_idx']


def _constants(np):
    ident = np.eye(P, dtype=np.float32)
    mask = np.zeros((P, TB * P), np.float32)
    mask[:, -P:] = np.where(np.arange(P)[None, :] > np.arange(P)[:, None], np.float32(BIG), np.float32(0))
    inv = (1.0 / np.float32(10000.0) ** (np.arange(0, ROPE, 2, dtype=np.float32) / np.float32(ROPE))).astype(np.float32)
    ang = np.outer(np.arange(SEQ, dtype=np.float32), inv).astype(np.float32)
    c, s = np.cos(ang), np.sin(ang)
    cos2 = np.concatenate([c, c], 1).reshape(TB, P, ROPE).transpose(1, 0, 2)
    sin2 = np.concatenate([-s, s], 1).reshape(TB, P, ROPE).transpose(1, 0, 2)
    return {"ident": ident, "mask": mask, "cos2": np.ascontiguousarray(cos2), "sin2": np.ascontiguousarray(sin2)}


def kernel(**inputs):
    import numpy as _np
    import concourse.bacc as _bacc
    from concourse import mybir as _mybir
    from concourse.bass_utils import run_bass_kernel_spmd as _run

    nc = _bacc.Bacc("TRN2", target_bir_lowering=False, num_devices=1)
    arrays, args = {}, []
    named = [(n, inputs[n]) for n in _INS] + list(_constants(_np).items())
    for name, value in named:
        a = _np.ascontiguousarray(value)
        arrays[f"in_{name}_dram"] = a
        args.append(nc.dram_tensor(f"in_{name}_dram", a.shape, _mybir.dt.from_np(a.dtype), kind="ExternalInput").ap())
    out = nc.dram_tensor("out_0_dram", (BATCH, SEQ, DIM), F32, kind="ExternalOutput").ap()
    build(nc, *args, out)
    r = _run(nc, [arrays], core_ids=[0])
    return r.results[0]["out_0_dram"]
```
